# Optimizing a Trainium2 kernel written in Bass

```python
import numpy as np
import jax
import jax.numpy as jnp

def _softmax(x, axis=-1):
    return jax.nn.softmax(x, axis=axis)

def _gelu(x):
    return jax.nn.gelu(x, approximate=True)

def _silu(x):
    return jax.nn.silu(x)

def _sigmoid(x):
    return jax.nn.sigmoid(x)

def _layernorm(x, axis=-1, eps=1e-05):
    m = jnp.mean(x, axis=axis, keepdims=True)
    v = jnp.var(x, axis=axis, keepdims=True)
    return (x - m) / jnp.sqrt(v + eps)

def _scatter_add(tgt, idx, src, axis=0):
    return tgt.at[idx].add(src)

def _segment_sum(src, seg, n):
    return jax.ops.segment_sum(src, seg, n)
kernel_name = 'mk_seq_preln_d2_jaxref_r8_cd52fe'

def setup_inputs(seed: int=0):
    np.random.seed(seed)
    _w = jnp.asarray

    def _L0_attn_setup():
        import jax, jax.numpy as jnp
        import numpy as np
        H_K, H_V, DK, DV = (8, 16, 128, 128)
        HIDDEN = 256
        KDIM, VDIM = (H_K * DK, H_V * DV)
        CONV_DIM = 2 * KDIM + VDIM
        KS = 4
        EPS = 1e-06

        def _split_qkvz_ba(qkvz, ba):
            B, S, _ = qkvz.shape
            vpk = H_V // H_K
            qkvz = qkvz.reshape(B, S, H_K, 2 * DK + 2 * vpk * DV)
            q = qkvz[..., :DK]
            k = qkvz[..., DK:2 * DK]
            v = qkvz[..., 2 * DK:2 * DK + vpk * DV].reshape(B, S, H_V, DV)
            z = qkvz[..., 2 * DK + vpk * DV:].reshape(B, S, H_V, DV)
            ba = ba.reshape(B, S, H_K, 2 * vpk)
            b = ba[..., :vpk].reshape(B, S, H_V)
            a = ba[..., vpk:].reshape(B, S, H_V)
            return (q, k, v, z, b, a)

        def _causal_conv_silu(x, w):
            xt = jnp.swapaxes(x, 1, 2)
            xt = jnp.pad(xt, ((0, 0), (0, 0), (KS - 1, 0)))
            y = jax.lax.conv_general_dilated(xt, w[:, None, :], (1,), 'VALID', dimension_numbers=('NCH', 'OIH', 'NCH'), feature_group_count=w.shape[0])
            return jax.nn.silu(jnp.swapaxes(y, 1, 2))

        def _l2norm(x):
            return x * jax.lax.rsqrt(jnp.sum(x * x, axis=-1, keepdims=True) + 1e-06)

        def _gated_delta_rule(q, k, v, g, beta):
            B, S, H, _ = q.shape
            scale = DK ** (-0.5)
            q = _l2norm(q) * scale
            k = _l2norm(k)
            qs = jnp.moveaxis(q, 1, 0)
            ks = jnp.moveaxis(k, 1, 0)
            vs = jnp.moveaxis(v, 1, 0)
            gs = jnp.moveaxis(g, 1, 0)
            bs = jnp.moveaxis(beta, 1, 0)
            S0 = jnp.zeros((B, H, DK, DV), q.dtype)

            def step(St, xs):
                qt, kt, vt, gt, bt = xs
                St = St * jnp.exp(gt)[..., None, None]
                pred = jnp.einsum('bhk,bhkv->bhv', kt, St)
                delta = (vt - pred) * bt[..., None]
                St = St + jnp.einsum('bhk,bhv->bhkv', kt, delta)
                o = jnp.einsum('bhk,bhkv->bhv', qt, St)
                return (St, o)
            _, o = jax.lax.scan(step, S0, (qs, ks, vs, gs, bs))
            return jnp.moveaxis(o, 0, 1)

        def _gated_rmsnorm(x, z, w):
            var = jnp.mean(x * x, axis=-1, keepdims=True)
            return x * jax.lax.rsqrt(var + EPS) * w * jax.nn.silu(z)

        def _forward(hidden_states, W_qkvz, W_ba, conv_w, dt_bias, A_log, norm_weight, W_out):
            B, S, _ = hidden_states.shape
            qkvz = hidden_states @ W_qkvz
            ba = hidden_states @ W_ba
            q, k, v, z, b, a = _split_qkvz_ba(qkvz, ba)
            mixed = jnp.concatenate([q.reshape(B, S, KDIM), k.reshape(B, S, KDIM), v.reshape(B, S, VDIM)], axis=-1)
            mixed = _causal_conv_silu(mixed, conv_w)
            q = mixed[..., :KDIM].reshape(B, S, H_K, DK)
            k = mixed[..., KDIM:2 * KDIM].reshape(B, S, H_K, DK)
            v = mixed[..., 2 * KDIM:].reshape(B, S, H_V, DV)
            beta = jax.nn.sigmoid(b)
            g = -jnp.exp(A_log) * jax.nn.softplus(a + dt_bias)
            rep = H_V // H_K
            q = jnp.repeat(q, rep, axis=2)
            k = jnp.repeat(k, rep, axis=2)
            o = _gated_delta_rule(q, k, v, g, beta)
            o = _gated_rmsnorm(o, z, norm_weight)
            return o.reshape(B, S, VDIM) @ W_out
        key = jax.random.key(seed)
        ks = jax.random.split(key, 8)
        B, S = (1, 128)
        return {'hidden_states': jax.random.normal(ks[0], (B, S, HIDDEN), jnp.float32), 'W_qkvz': jax.random.uniform(ks[1], (HIDDEN, 2 * KDIM + 2 * VDIM), jnp.float32, -0.25, 0.25) * 0.1, 'W_ba': jax.random.uniform(ks[2], (HIDDEN, 2 * H_V), jnp.float32, -0.25, 0.25), 'conv_w': jax.random.normal(ks[3], (CONV_DIM, KS), jnp.float32) * 0.1, 'dt_bias': jnp.ones((H_V,), jnp.float32), 'A_log': jnp.log(jax.random.uniform(ks[4], (H_V,), jnp.float32, 0.0001, 16.0)), 'norm_weight': jnp.ones((DV,), jnp.float32), 'W_out': jax.random.uniform(ks[5], (VDIM, HIDDEN), jnp.float32, -0.06, 0.06)}
    _L0_attn_in = _L0_attn_setup()

    def _L0_ffn_setup():
        import jax, jax.numpy as jnp
        import numpy as np
        E, H, I = (8, 256, 512)
        TOP_K = 1
        B, S = (1, 256)
        key = jax.random.key(seed)
        ks = jax.random.split(key, 7)
        std = 0.02
        return {'hidden_states': jax.random.normal(ks[0], (B, S, H), dtype=jnp.float32), 'router_w': jax.random.normal(ks[1], (E, H), dtype=jnp.float32) * std, 'gate_up_proj': jax.random.normal(ks[2], (E, H, 2 * I), dtype=jnp.float32) * std, 'down_proj': jax.random.normal(ks[3], (E, I, H), dtype=jnp.float32) * std, 'shared_gate_w': jax.random.normal(ks[4], (H, I), dtype=jnp.float32) * std, 'shared_up_w': jax.random.normal(ks[5], (H, I), dtype=jnp.float32) * std, 'shared_down_w': jax.random.normal(ks[6], (I, H), dtype=jnp.float32) * std}
    _L0_ffn_in = _L0_ffn_setup()

    def _L1_attn_setup():
        import jax, jax.numpy as jnp
        import numpy as np
        B, T, C = (2, 256, 256)
        H, KVH = (16, 4)
        HD = C // H
        REP = H // KVH

        def _alibi_slopes(n_head):
            start = 2.0 ** (-2.0 ** (-(np.log2(n_head) - 3.0)))
            return jnp.asarray([start ** (i + 1) for i in range(n_head)], jnp.float32)
        key = jax.random.key(seed)
        ks = jax.random.split(key, 4)
        sc = 0.02
        return {'x': jax.random.normal(ks[0], (B, T, C), jnp.float32), 'Wq': jax.random.normal(ks[1], (C, C), jnp.float32) * sc, 'Wkv': jax.random.normal(ks[2], (C, HD * KVH * 2), jnp.float32) * sc, 'Wo': jax.random.normal(ks[3], (C, C), jnp.float32) * sc, 'bo': jnp.zeros((C,), jnp.float32)}
    _L1_attn_in = _L1_attn_setup()

    def _L1_ffn_setup():
        import jax, jax.numpy as jnp
        import numpy as np
        B_, S, D = (2, 256, 256)
        F_ = 1024
        R = 16
        H = 16
        HD = D // H
        MOD_SCALE = 0.1
        EPS = 1e-06

        def _rmsnorm(x, w):
            v = jnp.mean(x * x, axis=-1, keepdims=True)
            return x * jax.lax.rsqrt(v + EPS) * w

        def _attention(x, Wq, Wk, Wv, Wo):
            b, s, d = x.shape
            q = (x @ Wq.T).reshape(b, s, H, HD)
            k = (x @ Wk.T).reshape(b, s, H, HD)
            v = (x @ Wv.T).reshape(b, s, H, HD)
            scores = jnp.einsum('bqhd,bkhd->bhqk', q, k) / np.sqrt(HD).astype(np.float32)
            causal = jnp.tril(jnp.ones((s, s), bool))
            scores = jnp.where(causal, scores, jnp.finfo(scores.dtype).min)
            probs = jax.nn.softmax(scores, axis=-1)
            out = jnp.einsum('bhqk,bkhd->bqhd', probs, v).reshape(b, s, d)
            return out @ Wo.T
        key = jax.random.key(seed)
        ks = jax.random.split(key, 12)
        sd = 0.02
        return {'hidden_states': jax.random.normal(ks[0], (B_, S, D), jnp.float32), 'ln1_w': jnp.ones((D,), jnp.float32), 'ln2_w': jnp.ones((D,), jnp.float32), 'Wq': jax.random.normal(ks[1], (D, D), jnp.float32) * sd, 'Wk': jax.random.normal(ks[2], (D, D), jnp.float32) * sd, 'Wv': jax.random.normal(ks[3], (D, D), jnp.float32) * sd, 'Wo': jax.random.normal(ks[4], (D, D), jnp.float32) * sd, 'A': jax.random.normal(ks[5], (D, R), jnp.float32) * (0.01 / np.sqrt(D)), 'B': jax.random.normal(ks[6], (R, F_), jnp.float32) * (0.01 / np.sqrt(R)), 'W_in_base': jax.random.normal(ks[7], (F_, D), jnp.float32) * sd, 'W_up_base': jax.random.normal(ks[8], (F_, D), jnp.float32) * sd, 'W_down': jax.random.normal(ks[9], (D, F_), jnp.float32) * sd}
    _L1_ffn_in = _L1_ffn_setup()
    _d = {'L0_attn_hidden_states': _L0_attn_in['hidden_states'], 'L0_attn_W_qkvz': _L0_attn_in['W_qkvz'], 'L0_attn_W_ba': _L0_attn_in['W_ba'], 'L0_attn_conv_w': _L0_attn_in['conv_w'], 'L0_attn_dt_bias': _L0_attn_in['dt_bias'], 'L0_attn_A_log': _L0_attn_in['A_log'], 'L0_attn_norm_weight': _L0_attn_in['norm_weight'], 'L0_attn_W_out': _L0_attn_in['W_out'], 'L0_ffn_router_w': _L0_ffn_in['router_w'], 'L0_ffn_gate_up_proj': _L0_ffn_in['gate_up_proj'], 'L0_ffn_down_proj': _L0_ffn_in['down_proj'], 'L0_ffn_shared_gate_w': _L0_ffn_in['shared_gate_w'], 'L0_ffn_shared_up_w': _L0_ffn_in['shared_up_w'], 'L0_ffn_shared_down_w': _L0_ffn_in['shared_down_w'], 'L1_attn_Wq': _L1_attn_in['Wq'], 'L1_attn_Wkv': _L1_attn_in['Wkv'], 'L1_attn_Wo': _L1_attn_in['Wo'], 'L1_attn_bo': _L1_attn_in['bo'], 'L1_ffn_ln1_w': _L1_ffn_in['ln1_w'], 'L1_ffn_ln2_w': _L1_ffn_in['ln2_w'], 'L1_ffn_Wq': _L1_ffn_in['Wq'], 'L1_ffn_Wk': _L1_ffn_in['Wk'], 'L1_ffn_Wv': _L1_ffn_in['Wv'], 'L1_ffn_Wo': _L1_ffn_in['Wo'], 'L1_ffn_A': _L1_ffn_in['A'], 'L1_ffn_B': _L1_ffn_in['B'], 'L1_ffn_W_in_base': _L1_ffn_in['W_in_base'], 'L1_ffn_W_up_base': _L1_ffn_in['W_up_base'], 'L1_ffn_W_down': _L1_ffn_in['W_down']}
    _x0 = _d['L0_attn_hidden_states']
    _d['L0_attn_hidden_states'] = jax.random.normal(jax.random.fold_in(jax.random.key(seed), 1), (4, 256, 256), dtype=_x0.dtype)
    del _x0
    return _d

def reference(L0_attn_hidden_states, L0_attn_W_qkvz, L0_attn_W_ba, L0_attn_conv_w, L0_attn_dt_bias, L0_attn_A_log, L0_attn_norm_weight, L0_attn_W_out, L0_ffn_router_w, L0_ffn_gate_up_proj, L0_ffn_down_proj, L0_ffn_shared_gate_w, L0_ffn_shared_up_w, L0_ffn_shared_down_w, L1_attn_Wq, L1_attn_Wkv, L1_attn_Wo, L1_attn_bo, L1_ffn_ln1_w, L1_ffn_ln2_w, L1_ffn_Wq, L1_ffn_Wk, L1_ffn_Wv, L1_ffn_Wo, L1_ffn_A, L1_ffn_B, L1_ffn_W_in_base, L1_ffn_W_up_base, L1_ffn_W_down):

    def _L0_attn_ref(hidden_states, W_qkvz, W_ba, conv_w, dt_bias, A_log, norm_weight, W_out):
        import jax, jax.numpy as jnp
        import numpy as np
        H_K, H_V, DK, DV = (8, 16, 128, 128)
        HIDDEN = 256
        KDIM, VDIM = (H_K * DK, H_V * DV)
        CONV_DIM = 2 * KDIM + VDIM
        KS = 4
        EPS = 1e-06

        def _split_qkvz_ba(qkvz, ba):
            B, S, _ = qkvz.shape
            vpk = H_V // H_K
            qkvz = qkvz.reshape(B, S, H_K, 2 * DK + 2 * vpk * DV)
            q = qkvz[..., :DK]
            k = qkvz[..., DK:2 * DK]
            v = qkvz[..., 2 * DK:2 * DK + vpk * DV].reshape(B, S, H_V, DV)
            z = qkvz[..., 2 * DK + vpk * DV:].reshape(B, S, H_V, DV)
            ba = ba.reshape(B, S, H_K, 2 * vpk)
            b = ba[..., :vpk].reshape(B, S, H_V)
            a = ba[..., vpk:].reshape(B, S, H_V)
            return (q, k, v, z, b, a)

        def _causal_conv_silu(x, w):
            xt = jnp.swapaxes(x, 1, 2)
            xt = jnp.pad(xt, ((0, 0), (0, 0), (KS - 1, 0)))
            y = jax.lax.conv_general_dilated(xt, w[:, None, :], (1,), 'VALID', dimension_numbers=('NCH', 'OIH', 'NCH'), feature_group_count=w.shape[0])
            return jax.nn.silu(jnp.swapaxes(y, 1, 2))

        def _l2norm(x):
            return x * jax.lax.rsqrt(jnp.sum(x * x, axis=-1, keepdims=True) + 1e-06)

        def _gated_delta_rule(q, k, v, g, beta):
            B, S, H, _ = q.shape
            scale = DK ** (-0.5)
            q = _l2norm(q) * scale
            k = _l2norm(k)
            qs = jnp.moveaxis(q, 1, 0)
            ks = jnp.moveaxis(k, 1, 0)
            vs = jnp.moveaxis(v, 1, 0)
            gs = jnp.moveaxis(g, 1, 0)
            bs = jnp.moveaxis(beta, 1, 0)
            S0 = jnp.zeros((B, H, DK, DV), q.dtype)

            def step(St, xs):
                qt, kt, vt, gt, bt = xs
                St = St * jnp.exp(gt)[..., None, None]
                pred = jnp.einsum('bhk,bhkv->bhv', kt, St)
                delta = (vt - pred) * bt[..., None]
                St = St + jnp.einsum('bhk,bhv->bhkv', kt, delta)
                o = jnp.einsum('bhk,bhkv->bhv', qt, St)
                return (St, o)
            _, o = jax.lax.scan(step, S0, (qs, ks, vs, gs, bs))
            return jnp.moveaxis(o, 0, 1)

        def _gated_rmsnorm(x, z, w):
            var = jnp.mean(x * x, axis=-1, keepdims=True)
            return x * jax.lax.rsqrt(var + EPS) * w * jax.nn.silu(z)

        def _forward(hidden_states, W_qkvz, W_ba, conv_w, dt_bias, A_log, norm_weight, W_out):
            B, S, _ = hidden_states.shape
            qkvz = hidden_states @ W_qkvz
            ba = hidden_states @ W_ba
            q, k, v, z, b, a = _split_qkvz_ba(qkvz, ba)
            mixed = jnp.concatenate([q.reshape(B, S, KDIM), k.reshape(B, S, KDIM), v.reshape(B, S, VDIM)], axis=-1)
            mixed = _causal_conv_silu(mixed, conv_w)
            q = mixed[..., :KDIM].reshape(B, S, H_K, DK)
            k = mixed[..., KDIM:2 * KDIM].reshape(B, S, H_K, DK)
            v = mixed[..., 2 * KDIM:].reshape(B, S, H_V, DV)
            beta = jax.nn.sigmoid(b)
            g = -jnp.exp(A_log) * jax.nn.softplus(a + dt_bias)
            rep = H_V // H_K
            q = jnp.repeat(q, rep, axis=2)
            k = jnp.repeat(k, rep, axis=2)
            o = _gated_delta_rule(q, k, v, g, beta)
            o = _gated_rmsnorm(o, z, norm_weight)
            return o.reshape(B, S, VDIM) @ W_out
        return _forward(hidden_states, W_qkvz, W_ba, conv_w, dt_bias, A_log, norm_weight, W_out)

    def _L0_ffn_ref(hidden_states, router_w, gate_up_proj, down_proj, shared_gate_w, shared_up_w, shared_down_w):
        import jax, jax.numpy as jnp
        import numpy as np
        E, H, I = (8, 256, 512)
        TOP_K = 1
        B, S = (1, 256)
        orig_shape = hidden_states.shape
        x = hidden_states.reshape(-1, H)
        T = x.shape[0]
        logits = x @ router_w.T
        top_vals, top_idx = jax.lax.top_k(logits, TOP_K)
        scores = jnp.full_like(logits, -jnp.inf)
        scores = scores.at[jnp.arange(T)[:, None], top_idx].set(top_vals)
        scores = jax.nn.sigmoid(scores.astype(jnp.float32)).astype(logits.dtype)
        xr = x[None, :, :] * scores.T[:, :, None]
        gate_up = jnp.einsum('eth,ehf->etf', xr, gate_up_proj)
        gate, up = jnp.split(gate_up, 2, axis=-1)
        routed = jnp.einsum('etf,efh->eth', up * jax.nn.silu(gate), down_proj)
        routed_sum = routed.sum(axis=0)
        shared = jax.nn.silu(x @ shared_gate_w) * (x @ shared_up_w) @ shared_down_w
        return (shared + routed_sum).reshape(orig_shape)

    def _L1_attn_ref(x, Wq, Wkv, Wo, bo):
        import jax, jax.numpy as jnp
        import numpy as np
        B, T, C = (2, 256, 256)
        H, KVH = (16, 4)
        HD = C // H
        REP = H // KVH

        def _alibi_slopes(n_head):
            start = 2.0 ** (-2.0 ** (-(np.log2(n_head) - 3.0)))
            return jnp.asarray([start ** (i + 1) for i in range(n_head)], jnp.float32)
        Bv, Tv, Cv = x.shape
        q = (x @ Wq).reshape(Bv, Tv, H, HD).transpose(0, 2, 1, 3)
        k, v = jnp.split(x @ Wkv, 2, axis=-1)
        k = k.reshape(Bv, Tv, KVH, HD).transpose(0, 2, 1, 3)
        v = v.reshape(Bv, Tv, KVH, HD).transpose(0, 2, 1, 3)
        qg = q.reshape(Bv, REP, KVH, Tv, HD)
        scores = jnp.einsum('brgtd,bgsd->brgts', qg, k) / jnp.sqrt(jnp.float32(HD))
        idx = jnp.arange(Tv)
        diff = (idx[None, :] - idx[:, None]).astype(jnp.float32)
        slopes = _alibi_slopes(H).reshape(REP, KVH)
        bias = jnp.tril(diff)[None, None] * slopes[:, :, None, None]
        causal = idx[None, :] <= idx[:, None]
        scores = jnp.where(causal[None, None, None], scores + bias[None], -jnp.inf)
        attn = jax.nn.softmax(scores, axis=-1)
        out = jnp.einsum('brgts,bgsd->brgtd', attn, v)
        out = out.reshape(Bv, H, Tv, HD).transpose(0, 2, 1, 3).reshape(Bv, Tv, Cv)
        return out @ Wo + bo

    def _L1_ffn_ref(hidden_states, ln1_w, ln2_w, Wq, Wk, Wv, Wo, A, B, W_in_base, W_up_base, W_down):
        import jax, jax.numpy as jnp
        import numpy as np
        B_, S, D = (2, 256, 256)
        F_ = 1024
        R = 16
        H = 16
        HD = D // H
        MOD_SCALE = 0.1
        EPS = 1e-06

        def _rmsnorm(x, w):
            v = jnp.mean(x * x, axis=-1, keepdims=True)
            return x * jax.lax.rsqrt(v + EPS) * w

        def _attention(x, Wq, Wk, Wv, Wo):
            b, s, d = x.shape
            q = (x @ Wq.T).reshape(b, s, H, HD)
            k = (x @ Wk.T).reshape(b, s, H, HD)
            v = (x @ Wv.T).reshape(b, s, H, HD)
            scores = jnp.einsum('bqhd,bkhd->bhqk', q, k) / np.sqrt(HD).astype(np.float32)
            causal = jnp.tril(jnp.ones((s, s), bool))
            scores = jnp.where(causal, scores, jnp.finfo(scores.dtype).min)
            probs = jax.nn.softmax(scores, axis=-1)
            out = jnp.einsum('bhqk,bkhd->bqhd', probs, v).reshape(b, s, d)
            return out @ Wo.T
        residual = hidden_states
        x = _rmsnorm(hidden_states, ln1_w)
        attn = _attention(x, Wq, Wk, Wv, Wo)
        mod = MOD_SCALE * jnp.tanh(attn @ A)
        h = _rmsnorm(residual, ln2_w)
        gate_pre = h @ W_in_base.T + mod * (h @ A) @ B
        gate = jax.nn.silu(gate_pre)
        up = h @ W_up_base.T
        mlp_out = gate * up @ W_down.T
        return residual + mlp_out
    x = L0_attn_hidden_states
    x = x + _L0_attn_ref(_layernorm(x, axis=-1), L0_attn_W_qkvz, L0_attn_W_ba, L0_attn_conv_w, L0_attn_dt_bias, L0_attn_A_log, L0_attn_norm_weight, L0_attn_W_out)
    x = x + _L0_ffn_ref(_layernorm(x, axis=-1), L0_ffn_router_w, L0_ffn_gate_up_proj, L0_ffn_down_proj, L0_ffn_shared_gate_w, L0_ffn_shared_up_w, L0_ffn_shared_down_w)
    x = x + _L1_attn_ref(_layernorm(x, axis=-1), L1_attn_Wq, L1_attn_Wkv, L1_attn_Wo, L1_attn_bo)
    x = x + _L1_ffn_ref(_layernorm(x, axis=-1), L1_ffn_ln1_w, L1_ffn_ln2_w, L1_ffn_Wq, L1_ffn_Wk, L1_ffn_Wv, L1_ffn_Wo, L1_ffn_A, L1_ffn_B, L1_ffn_W_in_base, L1_ffn_W_up_base, L1_ffn_W_down)
    return x

_drawn_inputs = setup_inputs


def setup_inputs(seed=0):
    import zlib

    import numpy as np

    out = dict(_drawn_inputs(seed))
    spreads = {'L0_attn_dt_bias': (1.0, 0.6),
     'L0_attn_norm_weight': (1.0, 0.6),
     'L1_attn_bo': (0.0, 1.498),
     'L1_ffn_ln1_w': (1.0, 0.6),
     'L1_ffn_ln2_w': (1.0, 0.6)}
    factors = {'L0_attn_W_qkvz': 2.817,
     'L0_attn_W_ba': 4.819,
     'L0_attn_conv_w': 2.775,
     'L0_attn_A_log': 8.0,
     'L0_attn_W_out': 2.828,
     'L0_ffn_router_w': 6.58,
     'L0_ffn_gate_up_proj': 6.143,
     'L0_ffn_down_proj': 6.125,
     'L1_attn_Wq': 64.0,
     'L1_ffn_Wq': 200.0,
     'L1_ffn_Wk': 200.0,
     'L1_ffn_Wv': 200.0,
     'L1_ffn_Wo': 200.0,
     'L1_ffn_A': 200.0,
     'L1_ffn_B': 200.0,
     'L1_ffn_W_in_base': 3.202,
     'L1_ffn_W_up_base': 3.155,
     'L1_ffn_W_down': 3.164,
     'L0_ffn_shared_gate_w': 8.0,
     'L0_ffn_shared_up_w': 8.0,
     'L0_ffn_shared_down_w': 8.0,
     'L1_attn_Wkv': 8.0,
     'L1_attn_Wo': 8.0}
    for name, (base, spread) in spreads.items():
        noise = np.random.default_rng([zlib.crc32(name.encode()), seed]).standard_normal(out[name].shape)
        drawn = base * np.exp(spread * noise) if base else spread * noise
        out[name] = jnp.asarray(drawn.astype(out[name].dtype))
    for name, factor in factors.items():
        out[name] = (out[name] * factor).astype(out[name].dtype)
    return out
```

```python
from contextlib import ExitStack

import numpy as np
import concourse.bass as bass
from concourse import mybir

F32 = mybir.dt.float32
BF16 = mybir.dt.bfloat16
I32 = mybir.dt.int32
ALU = mybir.AluOpType
ACT = mybir.ActivationFunctionType
AX = mybir.AxisListType

P = 128
NB, S, D = 4, 256, 256
TOK = NB * S
NT = TOK // P
KT = D // P
LN_EPS = 1e-5
RMS_EPS = 1e-6

HK, HV = 8, 16
VPK = HV // HK
HEADW = 2 * P + 2 * VPK * P
TAPS = 4
LEVELS = 7


def constant_arrays():
    r = np.arange(P)
    row, col = r[:, None], r[None, :]
    ident = (row == col).astype(np.float32)
    upto = (row <= col).astype(np.float32)
    after = (row > col).astype(np.float32)
    below = np.where(col < row, -30000.0, 0.0).astype(np.float32)
    f = np.concatenate([ident, upto, after, below], axis=1)
    masks = []
    for l in range(LEVELS):
        m = 1 << l
        lower = (row // (2 * m) == col // (2 * m)) & (row % (2 * m) >= m) & (col % (2 * m) < m)
        masks += [lower, lower.T]
    return f, np.concatenate(masks, axis=1).astype(np.int32)


class Norm:

    def __init__(self, nc, ctx, tag):
        sem = lambda n: ctx.enter_context(nc.semaphore(f"{tag}_{n}"))
        sb = lambda n, shape: ctx.enter_context(nc.sbuf_tensor(f"{tag}_{n}", shape, F32))
        self.stats_done, self.rstd_ready, self.normed = sem("stats_done"), sem("rstd_ready"), sem("normed")
        self.turned, self.stored = sem("turned"), sem("stored")
        self.stats = sb("stats", [P, NT, 6])
        self.moments = sb("moments", [P, NT, 2])
        self.rstd = sb("rstd", [P, NT])
        self.xn = sb("xn", [P, NT, D])
        self.xnT = sb("xnT", [P, KT, TOK])


def norm_vector(nc, dve, n, x):
    for t in range(NT):
        nc.vector.bn_stats(n.stats[:, t, :], x[:, t, :]).then_inc(n.stats_done, 1)
    dve.wait_ge(n.stats_done, NT)
    for t in range(NT):
        nc.vector.bn_aggr(n.moments[:, t, :], n.stats[:, t, :]).then_inc(n.stats_done, 1)
    dve.wait_ge(n.stats_done, 2 * NT)
    nc.vector.tensor_scalar(n.moments[:, :, 1], n.moments[:, :, 1], LN_EPS, None,
                            ALU.add).then_inc(n.stats_done, 1)
    dve.wait_ge(n.rstd_ready, 1)
    for t in range(NT):
        nc.vector.tensor_scalar(n.xn[:, t, :], x[:, t, :], n.moments[:, t, 0:1], n.rstd[:, t:t + 1],
                                ALU.subtract, ALU.mult).then_inc(n.normed, 1)


def norm_pool(nc, pool, n, minus_half):
    pool.wait_ge(n.stats_done, 2 * NT + 1)
    nc.gpsimd.tensor_tensor(n.rstd[:, :], n.moments[:, :, 1], minus_half, ALU.pow).then_inc(n.rstd_ready, 1)


def norm_tensor(nc, pe, n, bank, ident, src=None, ready=None):
    src = n.xn if src is None else src
    for j in range(NT // 2):
        pe.wait_ge(n.normed if ready is None else ready, 2 * j + 2)
        for t in range(2):
            for k in range(KT):
                last = nc.tensor.transpose(bank[j][:, (k * 2 + t) * P:(k * 2 + t + 1) * P],
                                           src[:, 2 * j + t, k * P:(k + 1) * P], ident)
        last.then_inc(n.turned, 1)


def norm_scalar(nc, act, n, bank):
    for j in range(NT // 2):
        act.wait_ge(n.turned, j + 1)
        nc.scalar.copy(n.xnT[:, :, 2 * j * P:(2 * j + 2) * P],
                       bank[j][:, :].rearrange("p (k t) -> p k t", k=KT)).then_inc(n.stored, 1)


def delta_steps():
    steps = []
    for ct in range(4):
        steps += [("proj", ct, half) for half in range(2)]
    steps += [("gate", j) for j in range(4)]
    steps += [("norms",), ("ktok",)] + [("vtok", j) for j in range(4)]
    for b in range(NB):
        steps += [("decay", b), ("gram", b), ("first", b)]
    for l in range(1, LEVELS):
        steps += [("mid", l, b) for b in range(NB)]
        for b in range(NB):
            steps += [("upper", l, b)] + ([("lower", l, b)] if l < LEVELS - 1 else [])
    steps += [("solve1", j) for j in range(2)] + [("state", j) for j in range(2)]
    steps += [("kstate", j) for j in range(2)] + [("qstate", j) for j in range(2)]
    steps += [("solve2", j) for j in range(2)]
    steps += [("out1", j) for j in range(2)] + [("out2", j) for j in range(2)]
    steps += [("turn", j) for j in range(4)] + [("final", j) for j in range(4)]
    return steps


BY_ACT = {"proj", "gate", "ktok", "decay", "mid", "solve1", "state", "qstate", "solve2", "out1", "turn"}


def delta_layer(nc, consts, x, W_qkvz, W_ba, conv_w, dt_bias, A_log, norm_weight, W_out, banks):
    ident, upto, after, below, masks, minus_half = consts
    STEPS = delta_steps()
    NS = len(STEPS)
    NBANK = len(banks)
    assert NS % NBANK == 0
    pos = {s: i for i, s in enumerate(STEPS)}
    act_steps = [s for s in STEPS if s[0] in BY_ACT]
    dve_steps = [s for s in STEPS if s[0] not in BY_ACT]
    act_pos = {s: i for i, s in enumerate(act_steps)}
    dve_pos = {s: i for i, s in enumerate(dve_steps)}
    NA, ND = len(act_steps), len(dve_steps)

    LINKS = (TAPS - 2) * 4 + 6
    with ExitStack() as ctx:
        sb = lambda n, shape, dt=F32: ctx.enter_context(nc.sbuf_tensor("dl_" + n, shape, dt))
        sem = lambda n: ctx.enter_context(nc.semaphore("dl_" + n))
        norm = Norm(nc, ctx, "dl")
        w_head = sb("w_head", [P, KT, HEADW])
        w_ba = sb("w_ba", [P, KT, 4 * HK])
        taps = sb("taps", [P, 4 * HK, TAPS])
        w_out = sb("w_out", [P, HV, D])
        gain = sb("gain", [P, 1])
        dtb = sb("dtb", [P, HV])
        rate = sb("rate", [P, HV])
        ones = sb("ones", [P, 1])
        tick = sb("tick", [1, 80])
        ident_b = sb("ident_b", [P, P], BF16)
        below_b = sb("below_b", [P, 4, P], BF16)
        beta = sb("beta", [P, NT, HV])
        gate_in = sb("gate_in", [P, NT, HV])
        sp = [sb(f"sp{i}", [P, NT, HV]) for i in range(4)]
        g = sb("g", [P, NT, HV])
        decay0 = sb("decay0", [P, NT, HV])
        xpad = sb("xpad", [P, 2, NB, S + TAPS - 1])
        conv = sb("conv", [P, 2, NB, S])
        kq = sb("kq", [P, NT, 2, P])
        vT = sb("vT", [P, VPK, TOK])
        ktok = sb("ktok", [P, NB, P])
        nv = sb("nv", [P, NT, VPK, P])
        sz = sb("sz", [P, NT, VPK, P])
        ssq = sb("ssq", [P, 2, NT])
        inv2 = sb("inv2", [P, 2, NT])
        power = sb("power", [P, NT])
        half = sb("half", [P, NT])
        ninvr = sb("ninvr", [P, NT])
        cneg = sb("cneg", [P, NT, VPK])
        mg = sb("mg", [P, 2, 4, P])
        dtm = sb("dtm", [P, 2, 4, P])
        dtc = sb("dtc", [P, NB, 4, P])
        nA = sb("nA", [P, NB, 4, P])
        nB = sb("nB", [P, NB, 4, P])
        T = sb("T", [P, NB, 4, P])
        U = sb("U", [P, NB, 4, P])
        X = sb("X", [P, NB, 4, P])
        sq = X[:, :, :, :].rearrange("p b u t -> p (b u) t").rearrange("p (i n) t -> p i n t", i=2)
        f = sb("f", [P, 2, NB, VPK, P])
        fd = sb("fd", [P, NB, VPK, P])
        state = sb("state", [P, NB, VPK, P])
        rhs2 = sb("rhs2", [P, NB, VPK, P])
        qs = sb("qs", [P, NB, VPK, P])
        o = nA[:, :, :, :].rearrange("p b (c v) d -> p b c v d", c=2)
        osq = X[:, :, :, :].rearrange("p b u t -> p (b u) t")
        oss = sb("oss", [P, NT, VPK])
        fac = sb("fac", [P, NT, VPK])
        fac2 = sb("fac2", [P, NT, VPK])
        minus_half2 = sb("minus_half2", [P, NT * VPK])
        og = T
        ogT = U

        loaded, w_loaded, prep, pooled = sem("loaded"), sem("w_loaded"), sem("prep"), sem("pooled")
        ba_done, sp_ready, g_ready, cum_done, start_ready = [sem(n) for n in (
            "ba_done", "sp_ready", "g_ready", "cum_done", "start_ready")]
        act_link = sem("act_link")
        filled, act_emptied, dve_emptied = sem("filled"), sem("act_emptied"), sem("dve_emptied")
        padded, conv_link, conv_done, silu_done, sq_done = [sem(n) for n in (
            "padded", "conv_link", "conv_done", "silu_done", "sq_done")]
        ssq_ready, root_ready, scale_ready = [sem(n) for n in ("ssq_ready", "root_ready", "scale_ready")]
        mg_ready, dtc_ready, tu_ready, fd_ready = [sem(n) for n in ("mg_ready", "dtc_ready", "tu_ready", "fd_ready")]
        rhs_link, osq_ready, oss_ready, fac_ready, og_ready = [sem(n) for n in (
            "rhs_link", "osq_ready", "oss_ready", "fac_ready", "og_ready")]
        dve_link = sem("dve_link")
        block = ctx.enter_context(nc.Block())

        def full(h, s):
            return NS * h + (pos[s] + 1)

        def act_done(h, s):
            return NA * h + (NA + act_pos[s] + 1)

        def dve_done(h, s):
            return ND * h + (ND + dve_pos[s] + 1)

        def bank(s):
            return banks[pos[s] % NBANK]

        def bank4(s):
            return bank(s)[:, :].rearrange("p (u t) -> p u t", u=4)

        def silu(act, h, ct):
            act.wait_ge(conv_done, h * 4 + (4 + ct + 1))
            c = conv[:, ct % 2, :, :].rearrange("p b t -> p (b t)")
            c2 = conv[:, ct % 2, :, :].rearrange("p b (c t) -> p (b c) t", c=2)
            if ct < 2:
                nc.scalar.activation(kq[:, :, 1 - ct, :], c2, ACT.Silu).then_inc(silu_done, 1)
            else:
                nc.scalar.activation(vT[:, ct - 2, :], c, ACT.Silu).then_inc(silu_done, 1)

        @block.sync
        def _(sync):
            sync.dma_start(w_ba[:, :, :], W_ba.rearrange("(k p) n -> p k n", p=P)).then_inc(loaded, 16)
            sync.dma_start(taps[:, :, :], conv_w.rearrange("(c p) j -> p c j", p=P)).then_inc(loaded, 16)
            sync.dma_start(w_out[:, :, :], W_out.rearrange("(h p) n -> p h n", p=P)).then_inc(loaded, 16)
            sync.dma_start(gain[:, :], norm_weight.rearrange("(p a) -> p a", a=1)).then_inc(loaded, 16)
            sync.dma_start(dtb[:, :], dt_bias.rearrange("(a h) -> a h", a=1).broadcast_to([P, HV])).then_inc(loaded, 16)
            sync.dma_start(rate[:, :], A_log.rearrange("(a h) -> a h", a=1).broadcast_to([P, HV])).then_inc(loaded, 16)
            w = W_qkvz.rearrange("(k p) n -> p k n", p=P)
            sync.dma_start(w_head[:, :, :], w[:, :, 0:HEADW]).then_inc(w_loaded, 16)
            with sync.Fori(0, HK - 1) as h:
                sync.wait_ge(filled, full(h, ("gate", 3)))
                sync.dma_start(w_head[:, :, :], w[:, :, bass.ds(h * HEADW + HEADW, HEADW)]).then_inc(w_loaded, 16)

        @block.tensor
        def _(pe):
            norm_tensor(nc, pe, norm, banks, ident)
            pe.wait_ge(loaded, 96)
            pe.wait_ge(norm.stored, NT // 2)
            for t in range(NT):
                for k in range(KT):
                    last = nc.tensor.matmul(banks[4][:, t * 4 * HK:(t + 1) * 4 * HK],
                                            norm.xnT[:, k, t * P:(t + 1) * P], w_ba[:, k, :],
                                            start=(k == 0), stop=(k == KT - 1))
            last.then_inc(ba_done, 1)
            pe.wait_ge(g_ready, 1)
            nc.tensor.matmul(banks[5][:, 0:NT * HV], upto, g[:, :, :].rearrange("p t h -> p (t h)"),
                             start=True, stop=True).then_inc(cum_done, 1)
            pe.wait_ge(start_ready, 1)

            with pe.Fori(0, HK) as h:
                def begin(s):
                    n = pos[s] - NBANK
                    before = STEPS[n]
                    if n >= 0:
                        if before in act_pos:
                            pe.wait_ge(act_emptied, act_done(h, before))
                        else:
                            pe.wait_ge(dve_emptied, dve_done(h, before))
                    elif before in act_pos:
                        pe.wait_ge(act_emptied, NA * h + (act_pos[before] + 1))
                    else:
                        pe.wait_ge(dve_emptied, ND * h + (dve_pos[before] + 1))

                for s in STEPS:
                    kind = s[0]
                    begin(s)
                    out, out4 = bank(s), bank4(s)
                    if kind == "proj":
                        _, ct, hf = s
                        pe.wait_ge(w_loaded, h * 16 + 16)
                        for k in range(KT):
                            last = nc.tensor.matmul(out[:, :], w_head[:, k, ct * P:(ct + 1) * P],
                                                    norm.xnT[:, k, hf * 512:(hf + 1) * 512],
                                                    start=(k == 0), stop=(k == KT - 1))
                    elif kind == "gate":
                        for t in range(2):
                            for k in range(KT):
                                tile = 2 * s[1] + t
                                last = nc.tensor.matmul(out[:, t * 256:(t + 1) * 256],
                                                        norm.xnT[:, k, tile * P:(tile + 1) * P],
                                                        w_head[:, k, 4 * P:6 * P],
                                                        start=(k == 0), stop=(k == KT - 1))
                    elif kind == "norms":
                        pe.wait_ge(sq_done, h * 2 + 2)
                        for i in range(2):
                            for t in range(NT):
                                last = nc.tensor.matmul(out[:, i * NT + t:i * NT + t + 1], sq[:, i, t, :],
                                                        ones[:, :], start=True, stop=True)
                    elif kind == "ktok":
                        for b in range(NB):
                            last = nc.tensor.transpose(out4[:, b, :], kq[:, 2 * b, 0, :], ident)
                    elif kind == "vtok":
                        pe.wait_ge(silu_done, h * 4 + 8)
                        for t in range(2):
                            for v in range(VPK):
                                tile = 2 * s[1] + t
                                last = nc.tensor.transpose(out4[:, 2 * t + v, :],
                                                           vT[:, v, tile * P:(tile + 1) * P], ident)
                    elif kind == "decay":
                        pe.wait_ge(mg_ready, h * NB + (s[1] + 1))
                        nc.tensor.matmul(out[:, :], ident_b[:, :], below_b[:, :, :].rearrange("p u t -> p (u t)"),
                                         start=True, stop=False)
                        last = nc.tensor.matmul(out[:, :], after, mg[:, s[1] % 2, :, :].rearrange("p u t -> p (u t)"),
                                                start=False, stop=True)
                    elif kind == "gram":
                        for c in range(2):
                            tile = 2 * s[1] + c
                            last = nc.tensor.matmul(out[:, c * 256:(c + 1) * 256], kq[:, tile, 0, :],
                                                    kq[:, tile, :, :].rearrange("p i t -> p (i t)"),
                                                    start=True, stop=True)
                    elif kind == "first":
                        pe.wait_ge(dve_emptied, dve_done(h, ("gram", s[1])))
                        for u in range(4):
                            last = nc.tensor.transpose(out4[:, u, :], nA[:, s[1], u, :], ident)
                    elif kind == "mid":
                        _, l, b = s
                        pe.wait_ge(dve_emptied, dve_done(h, ("first", b) if l == 1 else ("lower", l - 1, b)))
                        for u in range(4):
                            last = nc.tensor.matmul(out4[:, u, :], nA[:, b, u, :], T[:, b, u, :],
                                                    start=True, stop=True)
                    elif kind == "upper":
                        _, l, b = s
                        pe.wait_ge(act_emptied, act_done(h, ("mid", l, b)))
                        for u in range(4):
                            last = nc.tensor.matmul(out4[:, u, :], X[:, b, u, :], U[:, b, u, :],
                                                    start=True, stop=True)
                    elif kind == "lower":
                        _, l, b = s
                        for u in range(4):
                            last = nc.tensor.matmul(out4[:, u, :], U[:, b, u, :], X[:, b, u, :],
                                                    start=True, stop=True)
                    elif kind in ("solve1", "solve2"):
                        c = 0 if kind == "solve1" else 1
                        pe.wait_ge(dve_emptied, dve_done(h, ("upper", LEVELS - 1, 2 * s[1] + 1)))
                        if c:
                            pe.wait_ge(dve_emptied, dve_done(h, ("kstate", s[1])))
                        for i in range(2):
                            b = 2 * s[1] + i
                            for v in range(VPK):
                                rhs = rhs2[:, b, v, :] if c else nv[:, 2 * b, v, :]
                                last = nc.tensor.matmul(out4[:, 2 * i + v, :], U[:, b, 2 * c + v, :], rhs,
                                                        start=True, stop=True)
                    elif kind == "state":
                        pe.wait_ge(fd_ready, h * 2 + (s[1] + 1))
                        for i in range(2):
                            b = 2 * s[1] + i
                            last = nc.tensor.matmul(out[:, i * 256:(i + 1) * 256], ktok[:, b, :],
                                                    fd[:, b, :, :].rearrange("p v d -> p (v d)"),
                                                    start=True, stop=True)
                    elif kind in ("kstate", "qstate"):
                        pe.wait_ge(act_emptied, act_done(h, ("state", s[1])))
                        for i in range(2):
                            b = 2 * s[1] + i
                            last = nc.tensor.matmul(out[:, i * 256:(i + 1) * 256],
                                                    kq[:, 2 * b + 1, 0 if kind == "kstate" else 1, :],
                                                    state[:, b, :, :].rearrange("p v d -> p (v d)"),
                                                    start=True, stop=True)
                    elif kind in ("out1", "out2"):
                        c = 0 if kind == "out1" else 1
                        pe.wait_ge(act_emptied, act_done(h, ("solve1" if c == 0 else "solve2", s[1])))
                        for i in range(2):
                            b = 2 * s[1] + i
                            for v in range(VPK):
                                last = nc.tensor.matmul(out4[:, 2 * i + v, :], nB[:, b, 2 * c + v, :],
                                                        f[:, c, b, v, :], start=True, stop=True)
                    elif kind == "turn":
                        b = s[1]
                        pe.wait_ge(og_ready, h * NB + (b + 1))
                        for u in range(4):
                            last = nc.tensor.transpose(out4[:, u, :], og[:, b, u, :], ident)
                    elif kind == "final":
                        b = s[1]
                        pe.wait_ge(act_emptied, act_done(h, ("turn", b)))
                        for c in range(2):
                            for v in range(VPK):
                                last = nc.tensor.matmul(
                                    out[:, c * 256:(c + 1) * 256], ogT[:, b, 2 * c + v, :],
                                    w_out[:, bass.ds(h * VPK + v, 1), :].rearrange("p a n -> p (a n)"),
                                    start=(v == 0), stop=(v == VPK - 1))
                    last.then_inc(filled, 1)

        @block.scalar
        def _(act):
            act.nop().then_inc(act_emptied, NA)
            act.nop().then_inc(silu_done, 4)
            norm_scalar(nc, act, norm, banks)
            act.wait_ge(loaded, 96)
            act.wait_ge(ba_done, 1)
            ba = banks[4][:, 0:NT * 4 * HK].rearrange("p (t h i v) -> p t h i v", t=NT, h=HK, i=2)
            split = lambda m: m[:, :, :].rearrange("p t (h v) -> p t h v", v=VPK)
            for t in range(NT):
                nc.scalar.activation(split(beta)[:, t], ba[:, t, :, 0, :], ACT.Sigmoid).then_inc(sp_ready, 1)
            act.wait_ge(prep, 1)
            nc.scalar.activation(sp[0][:, :, :], gate_in[:, :, :], ACT.Abs).then_inc(act_link, 1)
            act.wait_ge(act_link, 1)
            nc.scalar.activation(sp[1][:, :, :], sp[0][:, :, :], ACT.Exp, scale=-1.0)
            nc.scalar.activation(rate[:, :], rate[:, :], ACT.Exp).then_inc(sp_ready, 1)
            act.wait_ge(padded, 9)
            act.wait_ge(cum_done, 1)
            nc.scalar.activation(decay0[:, :, :].rearrange("p t h -> p (t h)"), banks[5][:, 0:NT * HV],
                                 ACT.Exp).then_inc(start_ready, 1)
            with act.Fori(0, HK) as h:
                for s in act_steps:
                    kind = s[0]
                    act.wait_ge(filled, full(h, s))
                    src, src4 = bank(s), bank4(s)
                    if kind == "proj":
                        _, ct, hf = s
                        if hf == 0:
                            act.wait_ge(conv_done, h * 4 + (ct + 3))
                            act.wait_ge(silu_done, h * 4 + (ct + 3))
                        two = src[:, :].rearrange("p (b t) -> p b t", b=2)
                        tap = taps[:, bass.ds((h if ct == 0 else h + HK if ct == 1 else h * 2 + (2 * HK + ct - 2)), 1), :]
                        nc.scalar.copy(xpad[:, ct % 2, 2 * hf:2 * hf + 2, TAPS - 1:], two)
                        nc.scalar.mul(conv[:, ct % 2, 2 * hf:2 * hf + 2, :], two,
                                      tap[:, 0, TAPS - 1:TAPS]).then_inc(act_emptied, 1)
                        if hf == 1 and ct >= 1:
                            silu(act, h, ct - 1)
                        if hf == 1 and ct == 3:
                            silu(act, h, ct)
                    elif kind == "gate":
                        nc.scalar.activation(sz[:, 2 * s[1]:2 * s[1] + 2, :, :],
                                             src[:, :].rearrange("p (t v d) -> p t v d", t=2, v=VPK),
                                             ACT.Silu).then_inc(act_emptied, 1)
                    elif kind == "ktok":
                        nc.scalar.copy(ktok[:, :, :], src4).then_inc(act_emptied, 1)
                    elif kind == "decay":
                        act.wait_ge(dtc_ready, h * NB + (s[1] + 3))
                        nc.scalar.activation(dtm[:, s[1] % 2, :, :], src4, ACT.Exp).then_inc(act_emptied, 1)
                    elif kind == "mid":
                        nc.scalar.copy(X[:, s[2], :, :], src4).then_inc(act_emptied, 1)
                    elif kind in ("solve1", "solve2"):
                        nc.scalar.copy(f[:, 0 if kind == "solve1" else 1, 2 * s[1]:2 * s[1] + 2, :, :],
                                       src[:, :].rearrange("p (b v d) -> p b v d", b=2, v=VPK)).then_inc(act_emptied, 1)
                    elif kind == "state":
                        nc.scalar.copy(state[:, 2 * s[1]:2 * s[1] + 2, :, :],
                                       src[:, :].rearrange("p (b v d) -> p b v d", b=2, v=VPK)).then_inc(act_emptied, 1)
                    elif kind == "qstate":
                        for i in range(2):
                            b = 2 * s[1] + i
                            for v in range(VPK):
                                last = nc.scalar.mul(qs[:, b, v, :], src4[:, 2 * i + v, :],
                                                     decay0[:, 2 * b + 1, bass.ds(h * VPK + v, 1)])
                        last.then_inc(act_emptied, 1)
                    elif kind == "out1":
                        nc.scalar.copy(o[:, 2 * s[1]:2 * s[1] + 2, 0, :, :],
                                       src[:, :].rearrange("p (b v d) -> p b v d", b=2, v=VPK)).then_inc(act_emptied, 1)
                    elif kind == "turn":
                        nc.scalar.mul(ogT[:, s[1], :, :], src4, gain[:, 0:1]).then_inc(act_emptied, 1)

        @block.vector
        def _(dve):
            dve.nop().then_inc(dve_emptied, ND)
            dve.nop().then_inc(conv_done, 4)
            nc.vector.memset(ones[:, :], 1.0).then_inc(padded, 1)
            nc.vector.memset(xpad[:, :, :, :], 0.0).then_inc(padded, 1)
            nc.vector.memset(half[:, :], 0.5).then_inc(padded, 1)
            nc.vector.memset(minus_half2[:, :], -0.5).then_inc(padded, 1)
            nc.vector.tensor_copy(ident_b[:, :], ident).then_inc(padded, 1)
            for u in range(4):
                nc.vector.tensor_copy(below_b[:, u, :], below).then_inc(padded, 1)
            norm_vector(nc, dve, norm, x)
            links = [0]

            def link(ins):
                links[0] += 1
                ins.then_inc(dve_link, 1)
                dve.wait_ge(dve_link, links[0])

            dve.wait_ge(sp_ready, NT)
            dve.wait_ge(loaded, 96)
            ba = banks[4][:, 0:NT * 4 * HK].rearrange("p (t h i v) -> p t h i v", t=NT, h=HK, i=2)
            split = lambda m: m[:, :, :].rearrange("p t (h v) -> p t h v", v=VPK)
            for t in range(NT):
                last = nc.vector.tensor_tensor(split(gate_in)[:, t], ba[:, t, :, 1, :],
                                               dtb[:, :].rearrange("p (h v) -> p h v", v=VPK), ALU.add)
            last.then_inc(prep, 1)
            dve.wait_ge(sp_ready, NT + 1)
            e, z, z2, poly = sp[1], sp[0], sp[2], sp[3]
            link(nc.vector.tensor_scalar(z[:, :, :], e[:, :, :], 2.0, None, ALU.add))
            link(nc.vector.reciprocal(z[:, :, :], z[:, :, :]))
            link(nc.vector.tensor_tensor(z[:, :, :], z[:, :, :], e[:, :, :], ALU.mult))
            link(nc.vector.tensor_tensor(z2[:, :, :], z[:, :, :], z[:, :, :], ALU.mult))
            link(nc.vector.tensor_scalar(poly[:, :, :], z2[:, :, :], 2.0 / 17, 2.0 / 15, ALU.mult, ALU.add))
            for n in (13, 11, 9, 7, 5, 3, 1):
                link(nc.vector.tensor_tensor(poly[:, :, :], poly[:, :, :], z2[:, :, :], ALU.mult))
                link(nc.vector.tensor_scalar(poly[:, :, :], poly[:, :, :], 2.0 / n, None, ALU.add))
            link(nc.vector.tensor_tensor(poly[:, :, :], poly[:, :, :], z[:, :, :], ALU.mult))
            link(nc.vector.scalar_tensor_tensor(out=poly[:, :, :], in0=gate_in[:, :, :], scalar=0.0,
                                                in1=poly[:, :, :], op0=ALU.max, op1=ALU.add))
            for t in range(NT):
                last = nc.vector.scalar_tensor_tensor(out=g[:, t, :], in0=poly[:, t, :], scalar=-1.0,
                                                      in1=rate[:, :], op0=ALU.mult, op1=ALU.mult)
            link(last)
            nc.vector.tensor_scalar(g[:, :, :], g[:, :, :], -1000.0, None, ALU.max).then_inc(g_ready, 1)
            dve.wait_ge(start_ready, 1)
            with dve.Fori(0, HK) as h:
                hl = [0]

                def hlink(ins):
                    hl[0] += 1
                    ins.then_inc(conv_link, 1)
                    dve.wait_ge(conv_link, h * LINKS + hl[0])

                ticks = [0]

                def bear_wait():
                    nc.vector.memset(tick[:, ticks[0]:ticks[0] + 1], 0.0)
                    ticks[0] += 1

                def convolve(ct):
                    dve.wait_ge(act_emptied, act_done(h, ("proj", ct, 1)))
                    tap = taps[:, bass.ds((h if ct == 0 else h + HK if ct == 1 else h * 2 + (2 * HK + ct - 2)), 1), :]
                    acc = conv[:, ct % 2, :, :]
                    for j in range(TAPS - 1):
                        ins = nc.vector.scalar_tensor_tensor(out=acc, in0=xpad[:, ct % 2, :, j:j + S],
                                                             scalar=tap[:, 0, j:j + 1], in1=acc,
                                                             op0=ALU.mult, op1=ALU.add)
                        if j < TAPS - 2:
                            hlink(ins)
                    ins.then_inc(conv_done, 1)

                for ct in range(4):
                    convolve(ct)
                for s in dve_steps:
                    kind = s[0]
                    if kind == "gram":
                        dve.wait_ge(dtc_ready, h * NB + (4 + s[1] + 1))
                    if kind == "first":
                        dve.wait_ge(tu_ready, h * NB + (s[1] + 1))
                    dve.wait_ge(filled, full(h, s))
                    if kind in ("first", "upper", "lower"):
                        bear_wait()
                    src, src4 = bank(s), bank4(s)
                    if kind == "norms":
                        hlink(nc.vector.tensor_scalar(ssq[:, :, :], src[:, 0:2 * NT].rearrange("p (i t) -> p i t", i=2),
                                                      1e-6, None, ALU.add))
                        nc.vector.reciprocal(inv2[:, :, :], ssq[:, :, :]).then_inc(dve_emptied, 1)
                        dve.wait_ge(dve_emptied, dve_done(h, s))
                        for v in range(VPK):
                            last = nc.vector.scalar_tensor_tensor(
                                out=cneg[:, :, v], in0=inv2[:, 0, :], scalar=-1.0,
                                in1=beta[:, :, bass.ds(h * VPK + v, 1)].rearrange("p t a -> p (t a)"),
                                op0=ALU.mult, op1=ALU.mult)
                        last.then_inc(scale_ready, 1)
                        dve.wait_ge(root_ready, h + 1)
                        hlink(nc.vector.tensor_scalar(ninvr[:, :], power[:, :], -1.0, None, ALU.mult))
                    elif kind == "vtok":
                        for t in range(2):
                            tile = 2 * s[1] + t
                            last = nc.vector.tensor_scalar(nv[:, tile, :, :], src4[:, 2 * t:2 * t + 2, :],
                                                           ninvr[:, tile:tile + 1], None, ALU.mult)
                        last.then_inc(dve_emptied, 1)
                    elif kind == "gram":
                        b = s[1]
                        gram = src[:, :].rearrange("p (c i t) -> p c i t", c=2, i=2)
                        dc = dtc[:, b, :, :].rearrange("p (c v) t -> p c v t", c=2)
                        for i, dst in ((0, nA), (1, nB)):
                            last = nc.vector.tensor_tensor(
                                dst[:, b, :, :].rearrange("p (c v) t -> p c v t", c=2),
                                gram[:, :, i:i + 1, :].broadcast_to([P, 2, VPK, P]), dc, ALU.mult)
                        last.then_inc(dve_emptied, 1)
                    elif kind in ("first", "upper", "lower"):
                        l, b = (0, s[1]) if kind == "first" else (s[1], s[2])
                        m = lambda i: masks[:, 2 * l + i:2 * l + i + 1, :].broadcast_to([P, 4, P])
                        if kind == "first":
                            nc.vector.copy_predicated(U[:, b, :, :], m(1), nA[:, b, :, :])
                        if kind == "upper" and l < LEVELS - 1:
                            dve.wait_ge(filled, full(h, ("lower", l, b)))
                            bear_wait()
                        nc.vector.copy_predicated(U[:, b, :, :] if kind == "upper" else T[:, b, :, :],
                                                  m(1 if kind == "upper" else 0), src4).then_inc(dve_emptied, 1)
                    elif kind == "kstate":
                        for i in range(2):
                            b = 2 * s[1] + i
                            for v in range(VPK):
                                last = nc.vector.scalar_tensor_tensor(
                                    out=rhs2[:, b, v, :], in0=src4[:, 2 * i + v, :],
                                    scalar=decay0[:, 2 * b + 1, bass.ds(h * VPK + v, 1)],
                                    in1=nv[:, 2 * b + 1, v, :], op0=ALU.mult, op1=ALU.add)
                        last.then_inc(dve_emptied, 1)
                    elif kind == "out2":
                        dve.wait_ge(act_emptied, act_done(h, ("qstate", s[1])))
                        nc.vector.tensor_tensor(o[:, 2 * s[1]:2 * s[1] + 2, 1, :, :],
                                                src[:, :].rearrange("p (b v d) -> p b v d", b=2, v=VPK),
                                                qs[:, 2 * s[1]:2 * s[1] + 2, :, :], ALU.add).then_inc(dve_emptied, 1)
                        if s[1] == 1:
                            dve.wait_ge(osq_ready, h + 1)
                            hlink(nc.vector.tensor_reduce(oss[:, :, :].rearrange("p t v -> p (t v)"), osq, AX.X, ALU.add))
                            for v in range(VPK):
                                hlink(nc.vector.tensor_tensor(fac[:, :, v], oss[:, :, v], inv2[:, 1, :], ALU.mult))
                            hlink(nc.vector.tensor_scalar(fac[:, :, :], fac[:, :, :], 1.0 / (P * P), RMS_EPS,
                                                          ALU.mult, ALU.add))
                            for v in range(VPK):
                                last = nc.vector.scalar_tensor_tensor(
                                    out=fac2[:, :, v], in0=fac[:, :, v], scalar=float(P),
                                    in1=ssq[:, 1, :], op0=ALU.mult, op1=ALU.mult)
                            last.then_inc(oss_ready, 1)
                            dve.wait_ge(fac_ready, h + 1)
                            for b in range(NB):
                                for c in range(2):
                                    for v in range(VPK):
                                        last = nc.vector.scalar_tensor_tensor(
                                            out=og[:, b, 2 * c + v, :], in0=o[:, b, c, v, :],
                                            scalar=fac[:, 2 * b + c, v:v + 1], in1=sz[:, 2 * b + c, v, :],
                                            op0=ALU.mult, op1=ALU.mult)
                                last.then_inc(og_ready, 1)
                    elif kind == "final":
                        b = s[1]
                        xb = x[:, 2 * b:2 * b + 2, :]
                        nc.vector.tensor_tensor(xb, src[:, :].rearrange("p (t d) -> p t d", t=2), xb,
                                                ALU.add).then_inc(dve_emptied, 1)
                assert hl[0] == LINKS, hl

        @block.gpsimd
        def _(pool):
            pool.nop().then_inc(dtc_ready, 4)
            norm_pool(nc, pool, norm, minus_half)
            pool.wait_ge(padded, 9)
            pool.wait_ge(start_ready, 1)
            with pool.Fori(0, HK) as h:
                for i in range(2):
                    pool.wait_ge(silu_done, h * 4 + 6)
                    nc.gpsimd.tensor_tensor(sq[:, i, :, :], kq[:, :, i, :], kq[:, :, i, :],
                                            ALU.mult).then_inc(sq_done, 1)

                def masked_gates(b):
                    if b >= 2:
                        pool.wait_ge(filled, full(h, ("decay", b - 2)))
                        pool.wait_ge(padded, 9)
                    gates = g[:, 2 * b:2 * b + 2, bass.ds(h * VPK, VPK)].rearrange("p c (v a) -> p c v a", a=1)
                    last = nc.gpsimd.tensor_tensor(
                        mg[:, b % 2, :, :].rearrange("p (c v) t -> p c v t", c=2),
                        upto.rearrange("p (a b t) -> p a b t", a=1, b=1).broadcast_to([P, 2, VPK, P]),
                        gates.broadcast_to([P, 2, VPK, P]), ALU.mult)
                    last.then_inc(mg_ready, 1)

                masked_gates(0)
                masked_gates(1)
                pool.wait_ge(dve_emptied, dve_done(h, ("norms",)))
                nc.gpsimd.tensor_tensor(power[:, :], ssq[:, 0, :], half[:, :], ALU.pow).then_inc(root_ready, 1)
                pool.wait_ge(scale_ready, h + 1)
                for b in range(NB):
                    pool.wait_ge(act_emptied, act_done(h, ("decay", b)))
                    last = nc.gpsimd.tensor_tensor(
                        dtc[:, b, :, :].rearrange("p (c v) t -> p c v t", c=2),
                        dtm[:, b % 2, :, :].rearrange("p (c v) t -> p c v t", c=2),
                        cneg[:, 2 * b:2 * b + 2, :].rearrange("p c (v a) -> p c v a", a=1).broadcast_to([P, 2, VPK, P]),
                        ALU.mult)
                    last.then_inc(dtc_ready, 1)
                    for m in (T, U):
                        last = nc.gpsimd.tensor_copy(m[:, b, :, :], ident.rearrange("p (a t) -> p a t", a=1).broadcast_to([P, 4, P]))
                    last.then_inc(tu_ready, 1)
                    if b + 2 < NB:
                        masked_gates(b + 2)
                for j in range(2):
                    pool.wait_ge(act_emptied, act_done(h, ("solve1", j)))
                    for i in range(2):
                        b = 2 * j + i
                        last = nc.gpsimd.tensor_tensor(fd[:, b, :, :], f[:, 0, b, :, :],
                                                       dtc[:, b, 0:VPK, P - 1:P].broadcast_to([P, VPK, P]), ALU.mult)
                    last.then_inc(fd_ready, 1)
                pool.wait_ge(act_emptied, act_done(h, ("out1", 1)))
                pool.wait_ge(dve_emptied, dve_done(h, ("out2", 1)))
                oo = o[:, :, :, :, :].rearrange("p b c v d -> p (b c v) d")
                nc.gpsimd.tensor_tensor(osq, oo, oo, ALU.mult).then_inc(osq_ready, 1)
                pool.wait_ge(oss_ready, h + 1)
                nc.gpsimd.tensor_tensor(fac[:, :, :].rearrange("p t v -> p (t v)"),
                                        fac2[:, :, :].rearrange("p t v -> p (t v)"), minus_half2[:, :],
                                        ALU.pow).then_inc(fac_ready, 1)


NE, FF = 8, 512
SHARED = NE
FT = FF // P
SLOTS = NT + NE - 1
NS_COLS = 3 * NE + SLOTS + 1


def routing_constants():
    row = np.concatenate([NE - np.arange(NE), P * np.arange(NE), np.arange(SLOTS + 1), np.zeros(NE)])
    return np.broadcast_to(row.astype(np.float32), (P, NS_COLS)).copy()


def expert_layer(nc, consts, x, router_wT, gate_up, down, shared_gate, shared_up, shared_down, rconst,
                 slot_in, slot_out, banks):
    ident, upto, after, below, masks, minus_half = consts
    gate_bank, up_bank, dn_bank = banks[0:2], banks[2:4], banks[6:8]
    small_bank, ht_bank = banks[4], banks[5]
    with ExitStack() as ctx:
        sb = lambda n, shape, dt=F32: ctx.enter_context(nc.sbuf_tensor("ex_" + n, shape, dt))
        sem = lambda n: ctx.enter_context(nc.semaphore("ex_" + n))
        norm = Norm(nc, ctx, "ex")
        w_gu = sb("w_gu", [P, NE + 1, KT, 2 * FF])
        w_dn = sb("w_dn", [P, NE + 1, FT, D])
        w_r = sb("w_r", [P, KT, NE])
        rc = sb("rc", [P, NS_COLS])
        ones = sb("ones", [P, P])
        zero = sb("zero", [P, D])
        logits = sb("logits", [P, NT, NE])
        best = sb("best", [P, NT])
        score = sb("score", [P, NT])
        key = sb("key", [P, NT, NE])
        first = sb("first", [P, NT])
        onehot = sb("onehot", [P, NT + 1, NE])
        rank = sb("rank", [P, NT + 1, NE])
        over = sb("over", [P, NE, NE])
        tiles = sb("tiles", [P, NE])
        ends = sb("ends", [P, NE])
        starts = sb("starts", [P, NE])
        place = sb("place", [P, NT, NE])
        slot_f = sb("slot_f", [P, NT])
        slot = sb("slot", [P, NT], I32)
        past = sb("past", [P, SLOTS + 1, NE])
        owner_f = sb("owner_f", [P, SLOTS + 1])
        owner = sb("owner", [P, SLOTS + 1], I32)
        xr = sb("xr", [P, NT, D])
        xs = sb("xs", [P, 2, D])
        xsT = sb("xsT", [P, 2, KT, P])
        sg = sb("sg", [P, 2, FF])
        hid = sb("hid", [P, 2, FF])
        hT = sb("hT", [P, FT, P])
        ys = sb("ys", [P, 2, D])
        yg = sb("yg", [P, NT, D])

        small_loaded, shared_loaded, experts_loaded = sem("small_loaded"), sem("shared_loaded"), sem("experts_loaded")
        zero_ready, zeroed, link = sem("zero_ready"), sem("zeroed"), sem("link")
        logits_done, best_ready, onehot_ready, ranks_done = [sem(n) for n in (
            "logits_done", "best_ready", "onehot_ready", "ranks_done")]
        score_ready, scaled, slot_ready, scattered, owner_ready = [sem(n) for n in (
            "score_ready", "scaled", "slot_ready", "scattered", "owner_ready")]
        xt_filled, xt_stored = sem("xt_filled"), sem("xt_stored")
        xs_loaded = [sem(f"xs{i}_loaded") for i in range(2)]
        out_stored = [sem(f"out{i}_stored") for i in range(2)]
        gate_filled, up_filled, silu_ready, hid_ready = [sem(n) for n in (
            "gate_filled", "up_filled", "silu_ready", "hid_ready")]
        ht_filled, ht_stored, dn_filled, dn_stored, gathered = [sem(n) for n in (
            "ht_filled", "ht_stored", "dn_filled", "dn_stored", "gathered")]
        block = ctx.enter_context(nc.Block())

        @block.sync
        def _(sync):
            sync.dma_start(w_r[:, :, :], router_wT.rearrange("(k p) e -> p k e", p=P)).then_inc(small_loaded, 16)
            sync.dma_start(rc[:, :], rconst).then_inc(small_loaded, 16)
            sync.dma_start(w_gu[:, SHARED, :, 0:FF], shared_gate.rearrange("(k p) f -> p k f", p=P)).then_inc(shared_loaded, 16)
            sync.dma_start(w_gu[:, SHARED, :, FF:], shared_up.rearrange("(k p) f -> p k f", p=P)).then_inc(shared_loaded, 16)
            sync.dma_start(w_dn[:, SHARED, :, :], shared_down.rearrange("(k p) d -> p k d", p=P)).then_inc(shared_loaded, 16)
            sync.wait_ge(zero_ready, 1)
            sync.dma_start(slot_in.rearrange("(s p) d -> p s d", p=P),
                           zero[:, :].rearrange("p (a d) -> p a d", a=1).broadcast_to([P, SLOTS + 1, D])).then_inc(zeroed, 16)
            for e in range(NE):
                sync.dma_start(w_gu[:, e, :, :], gate_up[e].rearrange("(k p) f -> p k f", p=P)).then_inc(experts_loaded, 16)
                sync.dma_start(w_dn[:, e, :, :], down[e].rearrange("(k p) d -> p k d", p=P)).then_inc(experts_loaded, 16)
            sync.wait_ge(scattered, NT * 16)
            for r in range(2):
                sync.dma_start(xs[:, r, :], slot_in[r * P:(r + 1) * P, :]).then_inc(xs_loaded[r], 16)

            def store(r, par):
                sync.wait_ge(dn_stored, r + (NT + 1))
                sync.dma_start(slot_out[bass.ds(r * P, P), :] if not isinstance(r, int) else slot_out[r * P:(r + 1) * P, :],
                               ys[:, par, :]).then_inc(out_stored[par], 16)

            with sync.Fori(0, SLOTS // 2) as j:
                for par in range(2):
                    sync.wait_ge(xt_filled, j * 2 + (par + 1))
                    sync.dma_start(xs[:, par, :], slot_in[bass.ds(j * (2 * P) + (par + 2) * P, P), :]).then_inc(xs_loaded[par], 16)
                    store(j * 2 + par, par)
            store(SLOTS - 1, 0)
            for par in range(2):
                sync.wait_ge(out_stored[par], 16 * ((SLOTS + 1 - par) // 2))
                sync.wait_ge(xs_loaded[par], 16 * (SLOTS + 1) // 2)

        @block.tensor
        def _(pe):
            norm_tensor(nc, pe, norm, banks, ident)
            pe.wait_ge(norm.stored, NT // 2)
            pe.wait_ge(small_loaded, 32)
            for t in range(NT):
                for k in range(KT):
                    last = nc.tensor.matmul(small_bank[:, t * NE:(t + 1) * NE], norm.xnT[:, k, t * P:(t + 1) * P],
                                            w_r[:, k, :], start=(k == 0), stop=(k == KT - 1))
            last.then_inc(logits_done, 1)

            def gate_up_of(n, par, lhs, weights):
                for sem_, emptied, bank, at in ((gate_filled, silu_ready, gate_bank, 0), (up_filled, hid_ready, up_bank, FF)):
                    if not isinstance(n, int) or n >= 2:
                        pe.wait_ge(emptied, n - 1)
                    for k in range(KT):
                        last = nc.tensor.matmul(bank[par][:, :], lhs(k), weights(k, at), start=(k == 0), stop=(k == KT - 1))
                    last.then_inc(sem_, 1)

            def down_of(n, par, weights):
                pe.wait_ge(hid_ready, n + 1)
                if not isinstance(n, int) or n >= 1:
                    pe.wait_ge(ht_stored, n)
                for c in range(FT):
                    last = nc.tensor.transpose(ht_bank[:, c * P:(c + 1) * P], hid[:, par, c * P:(c + 1) * P], ident)
                last.then_inc(ht_filled, 1)
                pe.wait_ge(ht_stored, n + 1)
                if not isinstance(n, int) or n >= 2:
                    pe.wait_ge(dn_stored, n - 1)
                for c in range(FT):
                    last = nc.tensor.matmul(dn_bank[par][:, 0:D], hT[:, c, :], weights(c), start=(c == 0), stop=(c == FT - 1))
                last.then_inc(dn_filled, 1)

            def shared_gate_up(n):
                gate_up_of(n, n % 2, lambda k: norm.xnT[:, k, n * P:(n + 1) * P],
                           lambda k, at: w_gu[:, SHARED, k, at:at + FF])

            def shared_down_of(n):
                down_of(n, n % 2, lambda c: w_dn[:, SHARED, c, :])

            pe.wait_ge(shared_loaded, 48)
            shared_gate_up(0)
            for n in range(1, NT):
                shared_gate_up(n)
                shared_down_of(n - 1)
                if n == 3:
                    pe.wait_ge(onehot_ready, 1)
                    nc.tensor.matmul(small_bank[:, 0:(NT + 1) * NE], upto,
                                     onehot[:, :, :].rearrange("p t e -> p (t e)"), start=True, stop=False)
                    for t in range(NT):
                        last = nc.tensor.matmul(
                            small_bank[:, (t + 1) * NE:(NT + 1) * NE].rearrange("p (t e) -> p t e", e=NE), ones[:, :],
                            onehot[:, t:t + 1, :].broadcast_to([P, NT - t, NE]), start=False, stop=(t == NT - 1))
                    last.then_inc(ranks_done, 1)
            shared_down_of(NT - 1)

            pe.wait_ge(owner_ready, 1)
            pe.wait_ge(experts_loaded, 32 * NE)

            def turn_tokens(r, par, loads):
                pe.wait_ge(xs_loaded[par], loads * 16)
                if isinstance(r, int):
                    pe.wait_ge(slot_ready, 1)
                else:
                    pe.wait_ge(xt_stored, r)
                for k in range(KT):
                    last = nc.tensor.transpose(small_bank[:, k * P:(k + 1) * P], xs[:, par, k * P:(k + 1) * P], ident)
                last.then_inc(xt_filled, 1)
                pe.wait_ge(xt_stored, r + 1)

            def expert_of(r):
                at = slice(r, r + 1) if isinstance(r, int) else bass.ds(r, 1)
                return pe.value_load(owner[0:1, at], min_val=0, max_val=NE - 1)

            def routed_gate_up(r, par, loads):
                e = expert_of(r)
                turn_tokens(r, par, loads)
                gate_up_of(r + NT, par, lambda k: xsT[:, par, k, :],
                           lambda k, at: w_gu[:, bass.ds(e, 1), k, at:at + FF].rearrange("p a f -> p (a f)"))

            def routed_down(r, par):
                e = expert_of(r)
                down_of(r + NT, par, lambda c: w_dn[:, bass.ds(e, 1), c, :].rearrange("p a d -> p (a d)"))

            routed_gate_up(0, 0, 1)
            with pe.Fori(0, SLOTS // 2) as j:
                routed_gate_up(j * 2 + 1, 1, j + 1)
                routed_down(j * 2, 0)
                routed_gate_up(j * 2 + 2, 0, j + 2)
                routed_down(j * 2 + 1, 1)
            routed_down(SLOTS - 1, 0)

        @block.scalar
        def _(act):
            norm_scalar(nc, act, norm, banks)

            def silu_of(n, par):
                act.wait_ge(gate_filled, n + 1)
                if not isinstance(n, int) or n >= 2:
                    act.wait_ge(hid_ready, n - 1)
                nc.scalar.activation(sg[:, par, :], gate_bank[par][:, :], ACT.Silu).then_inc(silu_ready, 1)

            def store_ht(n):
                act.wait_ge(ht_filled, n + 1)
                if not isinstance(n, int) or n >= 1:
                    act.wait_ge(dn_filled, n)
                nc.scalar.copy(hT[:, :, :].rearrange("p c t -> p (c t)"), ht_bank[:, :]).then_inc(ht_stored, 1)

            silu_of(0, 0)
            for n in range(1, NT):
                silu_of(n, n % 2)
                store_ht(n - 1)
                if n == 2:
                    act.wait_ge(best_ready, 1)
                    nc.scalar.activation(score[:, :], best[:, :], ACT.Sigmoid).then_inc(score_ready, 1)
            store_ht(NT - 1)

            def store_xt(r, par):
                act.wait_ge(xt_filled, r + 1)
                act.wait_ge(up_filled, r + (NT - 1))
                nc.scalar.copy(xsT[:, par, :, :].rearrange("p k t -> p (k t)"), small_bank[:, 0:D]).then_inc(xt_stored, 1)

            store_xt(0, 0)
            silu_of(NT, 0)
            with act.Fori(0, SLOTS // 2) as j:
                store_xt(j * 2 + 1, 1)
                silu_of(j * 2 + (NT + 1), 1)
                store_ht(j * 2 + NT)
                store_xt(j * 2 + 2, 0)
                silu_of(j * 2 + (NT + 2), 0)
                store_ht(j * 2 + (NT + 1))
            store_ht(SLOTS - 1 + NT)

        @block.vector
        def _(dve):
            nc.vector.memset(zero[:, :], 0.0).then_inc(zero_ready, 1)
            nc.vector.memset(ones[:, :], 1.0)
            nc.vector.memset(onehot[:, NT, :], 0.0)
            norm_vector(nc, dve, norm, x)
            links = [0]

            def chain(ins):
                links[0] += 1
                ins.then_inc(link, 1)
                dve.wait_ge(link, links[0])

            def per_tile(m):
                return m[:, :].rearrange("p (t a) -> p t a", a=1).broadcast_to([P, NT, NE])

            def per_expert(m, n=NT):
                return m.rearrange("p (a e) -> p a e", a=1).broadcast_to([P, n, NE])

            dve.wait_ge(logits_done, 1)
            dve.wait_ge(small_loaded, 32)
            chain(nc.vector.tensor_copy(logits[:, :, :].rearrange("p t e -> p (t e)"), small_bank[:, 0:NT * NE]))
            nc.vector.tensor_reduce(best[:, :], logits[:, :, :], AX.X, ALU.max).then_inc(best_ready, 1)
            dve.wait_ge(best_ready, 1)
            chain(nc.vector.tensor_tensor(key[:, :, :], logits[:, :, :], per_tile(best), ALU.is_equal))
            chain(nc.vector.tensor_tensor(key[:, :, :], key[:, :, :], per_expert(rc[:, 0:NE]), ALU.mult))
            chain(nc.vector.tensor_reduce(first[:, :], key[:, :, :], AX.X, ALU.max))
            nc.vector.tensor_tensor(onehot[:, 0:NT, :], key[:, :, :], per_tile(first), ALU.is_equal).then_inc(onehot_ready, 1)

            def hidden_of(n, par):
                dve.wait_ge(up_filled, n + 1)
                dve.wait_ge(silu_ready, n + 1)
                if not isinstance(n, int) or n >= 2:
                    dve.wait_ge(ht_filled, n - 1)
                nc.vector.tensor_tensor(hid[:, par, :], up_bank[par][:, :], sg[:, par, :], ALU.mult).then_inc(hid_ready, 1)

            def add_shared(n):
                dve.wait_ge(dn_filled, n + 1)
                nc.vector.tensor_tensor(x[:, n, :], dn_bank[n % 2][:, 0:D], x[:, n, :], ALU.add).then_inc(dn_stored, 1)

            hidden_of(0, 0)
            for n in range(1, NT):
                hidden_of(n, n % 2)
                add_shared(n - 1)
                if n == 3:
                    dve.wait_ge(ranks_done, 1)
                    chain(nc.vector.tensor_copy(rank[:, :, :].rearrange("p t e -> p (t e)"), small_bank[:, 0:(NT + 1) * NE]))
                    chain(nc.vector.tensor_tensor(
                        over[:, :, :], rank[:, NT, :].rearrange("p (e a) -> p e a", a=1).broadcast_to([P, NE, NE]),
                        per_expert(rc[:, NE:2 * NE], NE), ALU.is_gt))
                    chain(nc.vector.tensor_reduce(tiles[:, :], over[:, :, :], AX.X, ALU.add))
                    chain(nc.vector.tensor_tensor_scan(ends[:, :], ones[:, 0:NE], tiles[:, :], 0.0, ALU.mult, ALU.add))
                    chain(nc.vector.tensor_tensor(starts[:, :], ends[:, :], tiles[:, :], ALU.subtract))
                    chain(nc.vector.tensor_scalar(starts[:, :], starts[:, :], float(P), -1.0, ALU.mult, ALU.add))
                    chain(nc.vector.tensor_tensor(place[:, :, :], rank[:, 0:NT, :], per_expert(starts[:, :]), ALU.add))
                    chain(nc.vector.tensor_tensor(place[:, :, :], place[:, :, :], onehot[:, 0:NT, :], ALU.mult))
                    chain(nc.vector.tensor_reduce(slot_f[:, :], place[:, :, :], AX.X, ALU.add))
                    nc.vector.tensor_copy(slot[:, :], slot_f[:, :]).then_inc(slot_ready, 1)
                    chain(nc.vector.tensor_tensor(
                        past[:, :, :], per_expert(ends[:, :], SLOTS + 1),
                        rc[:, 2 * NE:2 * NE + SLOTS + 1].rearrange("p (s a) -> p s a", a=1).broadcast_to([P, SLOTS + 1, NE]),
                        ALU.is_le))
                    chain(nc.vector.tensor_reduce(owner_f[:, :], past[:, :, :], AX.X, ALU.add))
                    chain(nc.vector.tensor_scalar(owner_f[:, :], owner_f[:, :], float(NE - 1), None, ALU.min))
                    nc.vector.tensor_copy(owner[:, :], owner_f[:, :]).then_inc(owner_ready, 1)
            add_shared(NT - 1)

            def store_down(n, par, stores):
                dve.wait_ge(dn_filled, n + 1)
                if not isinstance(stores, int) or stores:
                    dve.wait_ge(out_stored[par], stores * 16)
                nc.vector.tensor_copy(ys[:, par, :], dn_bank[par][:, 0:D]).then_inc(dn_stored, 1)

            hidden_of(NT, 0)
            hidden_of(NT + 1, 1)
            store_down(NT, 0, 0)
            hidden_of(NT + 2, 0)
            store_down(NT + 1, 1, 0)
            with dve.Fori(1, SLOTS // 2) as j:
                hidden_of(j * 2 + (NT + 1), 1)
                store_down(j * 2 + NT, 0, j)
                hidden_of(j * 2 + (NT + 2), 0)
                store_down(j * 2 + (NT + 1), 1, j)
            store_down(SLOTS - 1 + NT, 0, SLOTS // 2)
            dve.wait_ge(gathered, 16 * NT)
            for t in range(NT):
                nc.vector.tensor_tensor(x[:, t, :], x[:, t, :], yg[:, t, :], ALU.add)

        @block.gpsimd
        def _(pool):
            norm_pool(nc, pool, norm, minus_half)
            pool.wait_ge(score_ready, 1)
            pool.wait_ge(norm.normed, NT)
            nc.gpsimd.tensor_tensor(xr[:, :, :], norm.xn[:, :, :],
                                    score[:, :].rearrange("p (t a) -> p t a", a=1).broadcast_to([P, NT, D]),
                                    ALU.mult).then_inc(scaled, 1)
            pool.wait_ge(scaled, 1)
            pool.wait_ge(slot_ready, 1)
            pool.wait_ge(zeroed, 16)
            for t in range(NT):
                pool.indirect_dma_start(out=slot_in, out_offset=bass.IndirectOffsetOnAxis(slot[:, t:t + 1], 0),
                                        in_=xr[:, t, :], in_offset=None).then_inc(scattered, 16)
            for par in range(2):
                pool.wait_ge(out_stored[par], 16 * ((SLOTS + 1 - par) // 2))
            for t in range(NT):
                pool.indirect_dma_start(out=yg[:, t, :], out_offset=None, in_=slot_out,
                                        in_offset=bass.IndirectOffsetOnAxis(slot[:, t:t + 1], 0)).then_inc(gathered, 16)


HEADS, HD = 16, 16
GROUP = 4
ROUNDS = HEADS // GROUP
PAIR = S + P
LORA = 16
FFN1 = 1024
NEVER = -1e30


def score_bias(slopes):
    p, j = np.arange(P)[:, None], np.arange(S)[None, :]
    diff = np.concatenate([j - P - p, (j - p)[:, :P]], axis=1)
    rows = [np.where(diff <= 0, np.float32(4) * np.float32(m) * diff.astype(np.float32), NEVER) for m in slopes]
    return np.concatenate(rows, axis=1).astype(np.float32)


def alibi_slopes():
    start = 2.0 ** (-2.0 ** (-(np.log2(HEADS) - 3.0)))
    return [start ** (i + 1) for i in range(HEADS)]


def attention_steps(kv_tiles, last_steps):
    steps = [("q", 0), ("q", 1)] + [("k", i) for i in range((kv_tiles + 1) // 2)]
    steps += [("qk", 0, g) for g in range(GROUP)]
    for r in range(ROUNDS):
        if r + 1 < ROUNDS:
            steps += [("qk", r + 1, g) for g in range(GROUP)]
        steps += [("pt", r, i) for i in range(3)] + [("pv", r)]
    return steps + [("ot",)] + last_steps


def attention_bank(s):
    return {"q": lambda: s[1], "k": lambda: 2 + s[1], "qk": lambda: s[2], "pt": lambda: 4 + s[2], "pv": lambda: 7,
            "ot": lambda: 4, "wo": lambda: 5, "proj": lambda: 5, "tanh": lambda: 6, "ha": lambda: 7}[s[0]]()


def attention_layer(nc, consts, x, weights, bias_const, banks, modulated):
    ident, upto, after, below, masks, minus_half = consts
    KVT = ROUNDS if modulated else 1
    KVH = HEADS if modulated else GROUP
    tag = "mo" if modulated else "al"
    last_steps = [("proj", 0), ("tanh",), ("ha",)] if modulated else [("wo", 0)]
    STEPS = attention_steps(KVT, last_steps)
    BY_DVE = {"qk", "pv", "wo", "ha"}
    by_act = lambda s: s[0] not in BY_DVE and not (s[0] == "pt" and s[2] == 2)
    pos = {s: i for i, s in enumerate(STEPS)}
    act_steps = [s for s in STEPS if by_act(s)]
    dve_steps = [s for s in STEPS if not by_act(s)]
    act_pos = {s: i for i, s in enumerate(act_steps)}
    dve_pos = {s: i for i, s in enumerate(dve_steps)}
    NSTEP, NA, ND = len(STEPS), len(act_steps), len(dve_steps)
    NBIAS = 1 if modulated else HEADS

    with ExitStack() as ctx:
        sb = lambda n, shape, dt=F32: ctx.enter_context(nc.sbuf_tensor(f"{tag}_{n}", shape, dt))
        sem = lambda n: ctx.enter_context(nc.semaphore(f"{tag}_{n}"))
        norm = Norm(nc, ctx, tag)
        w_q = sb("w_q", [P, KT, HEADS, 32])
        w_k = sb("w_k", [P, KT, KVT * GROUP, 32])
        w_v = sb("w_v", [P, KT, KVH * HD])
        w_o = sb("w_o", [P, KT, D])
        bias = sb("bias", [P, NBIAS, PAIR])
        vp = sb("vp", [P, NT, KVH, HD + 1])
        qT = sb("qT", [P, ROUNDS, S])
        kT = sb("kT", [P, KVT, S])
        sc = sb("sc", [P, 2, GROUP, PAIR])
        top = sb("top", [P, 2, 2, GROUP])
        pT = sb("pT", [P, 3, GROUP, P])
        rec = sb("rec", [P, ROUNDS, 2, GROUP])
        att = sb("att", [P, 2, HEADS, HD])
        tick = sb("tick", [1, HEADS])
        attT = sb("attT", [P, KT, S])
        if modulated:
            gain1, gain2 = sb("gain1", [P, KT]), sb("gain2", [P, KT])
            sq = sb("sq", [P, NT, D])
            ms = sb("ms", [P, NT])
            rms = sb("rms", [P, NT])
            xr = sb("xr", [P, NT, D])
            hT = sb("hT", [P, KT, TOK])
            w_a = sb("w_a", [P, KT, LORA])
            w_b = sb("w_b", [LORA, FFN1])
            projT = sb("projT", [P, KT, S])
            tanhT = sb("tanhT", [LORA, S])
            modT = sb("modT", [LORA, TOK])
            w_in, w_up = sb("w_in", [P, KT, FFN1]), sb("w_up", [P, KT, FFN1])
            w_dn = sb("w_dn", [P, FFN1 // P, D])
            sg, hid = sb("sg", [P, 2, FF]), sb("hid", [P, 2, FF])
            hidT = sb("hidT", [P, FT, P])
            sq_ready, ms_ready, rms_ready, xr_ready = [sem(n) for n in ("sq_ready", "ms_ready", "rms_ready", "xr_ready")]
            gate_filled, up_filled, silu_ready, hid_ready = [sem(n) for n in (
                "gate_filled", "up_filled", "silu_ready", "hid_ready")]
            ht_filled, ht_stored, dn_filled, dn_stored = [sem(n) for n in (
                "ht_filled", "ht_stored", "dn_filled", "dn_stored")]
        else:
            bo = sb("bo", [1, D])
            ones_row = sb("ones_row", [1, P])
        loaded, mlp_loaded, padded = sem("loaded"), sem("mlp_loaded"), sem("padded")
        v_filled, v_stored = sem("v_filled"), sem("v_stored")
        filled, act_emptied, dve_emptied = sem("filled"), sem("act_emptied"), sem("dve_emptied")
        shifted, exp_ready, rec_ready = sem("shifted"), sem("exp_ready"), sem("rec_ready")
        NLOAD = 13 if modulated else 9
        block = ctx.enter_context(nc.Block())

        full = lambda b, s: NSTEP * b + (pos[s] + 1)
        act_done = lambda b, s: NA * b + (NA + act_pos[s] + 1)
        dve_done = lambda b, s: ND * b + (ND + dve_pos[s] + 1)
        bank = lambda s: banks[attention_bank(s)]

        def mlp_tensor(pe):
            def gate_and_up(n):
                t, c = n // 2, n % 2
                tok, cols = slice(t * P, (t + 1) * P), slice(c * FF, (c + 1) * FF)
                if n >= 2:
                    pe.wait_ge(silu_ready, n - 1)
                for k in range(KT):
                    nc.tensor.matmul(banks[c][:, :], hT[:, k, tok], w_in[:, k, cols], start=(k == 0), stop=False)
                nc.tensor.matmul(banks[c][:, :], modT[:, tok], w_b[:, cols], start=False, stop=True).then_inc(gate_filled, 1)
                if n >= 2:
                    pe.wait_ge(hid_ready, n - 1)
                for k in range(KT):
                    last = nc.tensor.matmul(banks[2 + c][:, :], hT[:, k, tok], w_up[:, k, cols],
                                            start=(k == 0), stop=(k == KT - 1))
                last.then_inc(up_filled, 1)

            def down(n):
                pe.wait_ge(hid_ready, n + 1)
                if n:
                    pe.wait_ge(ht_stored, n)
                for c in range(FT):
                    last = nc.tensor.transpose(banks[5][:, c * P:(c + 1) * P], hid[:, n % 2, c * P:(c + 1) * P], ident)
                last.then_inc(ht_filled, 1)
                pe.wait_ge(ht_stored, n + 1)
                if n >= 2:
                    pe.wait_ge(dn_stored, n - 1)
                for c in range(FT):
                    last = nc.tensor.matmul(banks[6 + n % 2][:, 0:D], hidT[:, c, :], w_dn[:, (n % 2) * FT + c, :],
                                            start=(c == 0), stop=(c == FT - 1))
                last.then_inc(dn_filled, 1)

            gate_and_up(0)
            for n in range(1, 2 * NT):
                gate_and_up(n)
                down(n - 1)
            down(2 * NT - 1)

        @block.sync
        def _(sync):
            sync.wait_ge(padded, 2)
            for name, w, tiles in (("Wq", w_q, HEADS), ("Wk", w_k, KVT * GROUP)):
                src = weights[name].rearrange("(k p) (h c) -> p k h c", p=P, c=HD)
                for k in range(KT):
                    sync.dma_start(w[:, k, :, 0:HD], src[:, k]).then_inc(loaded, 16)
            sync.dma_start(w_v[:, :, :], weights["Wv"].rearrange("(k p) n -> p k n", p=P)).then_inc(loaded, 16)
            sync.dma_start(w_o[:, :, :], weights["Wo"].rearrange("(k p) n -> p k n", p=P)).then_inc(loaded, 16)
            sync.dma_start(bias[:, :, :].rearrange("p h j -> p (h j)"), bias_const).then_inc(loaded, 16)
            if modulated:
                for k in range(KT):
                    sync.dma_start(gain1[:, k:k + 1], weights["ln1"][k * P:(k + 1) * P].rearrange("(p a) -> p a", a=1)).then_inc(loaded, 16)
                for k in range(KT):
                    sync.dma_start(gain2[:, k:k + 1], weights["ln2"][k * P:(k + 1) * P].rearrange("(p a) -> p a", a=1)).then_inc(loaded, 16)
                sync.dma_start(w_a[:, :, :], weights["A"].rearrange("(k p) r -> p k r", p=P)).then_inc(loaded, 16)
                sync.dma_start(w_b[:, :], weights["B"]).then_inc(loaded, 16)
                sync.dma_start(w_in[:, :, :], weights["W_in"].rearrange("(k p) n -> p k n", p=P)).then_inc(mlp_loaded, 16)
                sync.dma_start(w_up[:, :, :], weights["W_up"].rearrange("(k p) n -> p k n", p=P)).then_inc(mlp_loaded, 16)
                sync.dma_start(w_dn[:, :, :], weights["W_down"].rearrange("(k p) n -> p k n", p=P)).then_inc(mlp_loaded, 16)
            else:
                sync.dma_start(bo[:, :], weights["bo"].rearrange("(a d) -> a d", a=1)).then_inc(loaded, 16)
                sync.dma_start(ones_row[:, :], weights["ones"][0:1, 0:P]).then_inc(loaded, 16)

        @block.tensor
        def _(pe):
            if modulated:
                norm_tensor(nc, pe, norm, banks, ident, src=xr, ready=xr_ready)
            else:
                norm_tensor(nc, pe, norm, banks, ident)
            pe.wait_ge(norm.stored, NT // 2)
            pe.wait_ge(loaded, 16 * NLOAD)
            for j in range(NT // 2):
                for t in range(2):
                    for k in range(KT):
                        last = nc.tensor.matmul(banks[4 + j][:, t * KVH * HD:(t + 1) * KVH * HD],
                                                norm.xnT[:, k, (2 * j + t) * P:(2 * j + t + 1) * P], w_v[:, k, :],
                                                start=(k == 0), stop=(k == KT - 1))
                last.then_inc(v_filled, 1)
            pe.wait_ge(v_stored, NT // 2)

            with pe.Fori(0, NB) as b:
                for s in STEPS:
                    kind, out = s[0], bank(s)
                    before = [q for q in STEPS[:pos[s]] if attention_bank(q) == attention_bank(s)]
                    late = not before
                    q = (before or [q for q in STEPS if attention_bank(q) == attention_bank(s)])[-1]
                    if by_act(q):
                        pe.wait_ge(act_emptied, NA * b + (act_pos[q] + 1) if late else act_done(b, q))
                    else:
                        pe.wait_ge(dve_emptied, ND * b + (dve_pos[q] + 1) if late else dve_done(b, q))
                    tokens = bass.ds(b * S, S)
                    if kind in ("q", "k"):
                        w, tiles = (w_q, ROUNDS) if kind == "q" else (w_k, KVT)
                        for i in range(2 * s[1], min(2 * s[1] + 2, tiles)):
                            for k in range(KT):
                                last = nc.tensor.matmul(
                                    out[:, (i % 2) * S:(i % 2 + 1) * S],
                                    w[:, k, i * GROUP:(i + 1) * GROUP, :].rearrange("p h c -> p (h c)"),
                                    norm.xnT[:, k, tokens], start=(k == 0), stop=(k == KT - 1))
                    elif kind == "qk":
                        _, r, g = s
                        if (r, g) == (0, 0):
                            pe.wait_ge(act_emptied, act_done(b, ("k", (KVT + 1) // 2 - 1)))
                        rows = slice(32 * g, 32 * g + HD)
                        rk = r if modulated else 0
                        nc.tensor.matmul(out[:, 0:S], qT[rows, r, P:S], kT[rows, rk, 0:S], start=True, stop=True)
                        last = nc.tensor.matmul(out[:, S:PAIR], qT[rows, r, 0:P], kT[rows, rk, 0:P], start=True, stop=True)
                    elif kind == "pt":
                        _, r, i = s
                        pe.wait_ge(exp_ready, b * ROUNDS + (r + 1))
                        for g in range(GROUP):
                            last = nc.tensor.transpose(out[:, g * P:(g + 1) * P], sc[:, r % 2, g, i * P:(i + 1) * P], ident)
                    elif kind == "pv":
                        _, r = s
                        pe.wait_ge(act_emptied, act_done(b, ("pt", r, 1)))
                        pe.wait_ge(dve_emptied, dve_done(b, ("pt", r, 2)))
                        for tile, parts in ((0, [(2, 0)]), (1, [(0, 0), (1, 1)])):
                            for g in range(GROUP):
                                kv = r * GROUP + g if modulated else g
                                at = (tile * GROUP + g) * (HD + 1)
                                for i, (part, src) in enumerate(parts):
                                    last = nc.tensor.matmul(
                                        out[:, at:at + HD + 1], pT[:, part, g, :],
                                        vp[:, bass.ds(b * 2 + src, 1), kv, :].rearrange("p a c -> p (a c)"),
                                        start=(i == 0), stop=(i == len(parts) - 1))
                    elif kind == "ot":
                        pe.wait_ge(dve_emptied, dve_done(b, ("pv", ROUNDS - 1)))
                        flat = att[:, :, :, :].rearrange("p t h c -> p t (h c)")
                        for k in range(KT):
                            for t in range(2):
                                last = nc.tensor.transpose(out[:, (k * 2 + t) * P:(k * 2 + t + 1) * P],
                                                           flat[:, t, k * P:(k + 1) * P], ident)
                    elif kind == "wo":
                        pe.wait_ge(act_emptied, act_done(b, ("ot",)))
                        for t in range(2):
                            for k in range(KT):
                                nc.tensor.matmul(out[:, t * D:(t + 1) * D], attT[:, k, t * P:(t + 1) * P], w_o[:, k, :],
                                                 start=(k == 0), stop=False)
                            last = nc.tensor.matmul(out[:, t * D:(t + 1) * D], ones_row[:, :], bo[:, :],
                                                    start=False, stop=True)
                    elif kind == "proj":
                        pe.wait_ge(act_emptied, act_done(b, ("ot",)))
                        for m in range(KT):
                            for k in range(KT):
                                last = nc.tensor.matmul(out[:, m * S:(m + 1) * S], w_o[:, k, m * P:(m + 1) * P],
                                                        attT[:, k, :], start=(k == 0), stop=(k == KT - 1))
                    elif kind in ("tanh", "ha"):
                        if kind == "tanh":
                            pe.wait_ge(act_emptied, act_done(b, ("proj", 0)))
                        for k in range(KT):
                            last = nc.tensor.matmul(out[0:LORA, 0:S], w_a[:, k, :],
                                                    projT[:, k, :] if kind == "tanh" else hT[:, k, tokens],
                                                    start=(k == 0), stop=(k == KT - 1))
                    last.then_inc(filled, 1)
            if modulated:
                pe.wait_ge(dve_emptied, ND * (NB + 1))
                pe.wait_ge(act_emptied, NA * (NB + 1))
                pe.wait_ge(mlp_loaded, 48)
                mlp_tensor(pe)

        @block.scalar
        def _(act):
            act.nop().then_inc(act_emptied, NA)
            if modulated:
                act.wait_ge(loaded, 16 * NLOAD)
                for j in range(NT // 2):
                    act.wait_ge(norm.turned, j + 1)
                    for k in range(KT):
                        src = banks[j][:, k * 2 * P:(k + 1) * 2 * P]
                        nc.scalar.mul(norm.xnT[:, k, 2 * j * P:(2 * j + 2) * P], src, gain1[:, k:k + 1])
                        last = nc.scalar.mul(hT[:, k, 2 * j * P:(2 * j + 2) * P], src, gain2[:, k:k + 1])
                    last.then_inc(norm.stored, 1)
            else:
                norm_scalar(nc, act, norm, banks)
            act.wait_ge(padded, 3)
            for j in range(NT // 2):
                act.wait_ge(v_filled, j + 1)
                nc.scalar.copy(vp[:, 2 * j:2 * j + 2, :, 0:HD],
                               banks[4 + j][:, 0:2 * KVH * HD].rearrange("p (t h c) -> p t h c", t=2, c=HD)).then_inc(v_stored, 1)
            with act.Fori(0, NB) as b:
                def exponentials(r):
                    act.wait_ge(shifted, b * ROUNDS + (r + 1))
                    flat = sc[:, r % 2, :, :].rearrange("p g j -> p (g j)")
                    nc.scalar.activation(flat, flat, ACT.Exp).then_inc(exp_ready, 1)

                for s in act_steps:
                    kind, src = s[0], bank(s)
                    if kind == "pt" and s[2] == 0:
                        exponentials(s[1])
                    act.wait_ge(filled, full(b, s))
                    if kind in ("q", "k"):
                        dst, tiles = (qT, ROUNDS) if kind == "q" else (kT, KVT)
                        n = min(2, tiles - 2 * s[1])
                        nc.scalar.copy(dst[:, 2 * s[1]:2 * s[1] + n, :],
                                       src[:, 0:n * S].rearrange("p (r t) -> p r t", r=n)).then_inc(act_emptied, 1)
                    elif kind == "pt":
                        nc.scalar.copy(pT[:, s[2], :, :].rearrange("p g t -> p (g t)"), src[:, :]).then_inc(act_emptied, 1)
                    elif kind == "ot":
                        nc.scalar.copy(attT[:, :, :].rearrange("p k t -> p (k t)"), src[:, :]).then_inc(act_emptied, 1)
                    elif kind == "proj":
                        nc.scalar.copy(projT[:, :, :].rearrange("p k t -> p (k t)"), src[:, :]).then_inc(act_emptied, 1)
                    elif kind == "tanh":
                        nc.scalar.activation(tanhT[:, :], src[0:LORA, 0:S], ACT.Tanh).then_inc(act_emptied, 1)
            if modulated:
                for n in range(2 * NT + 1):
                    if n < 2 * NT:
                        act.wait_ge(gate_filled, n + 1)
                        if n >= 2:
                            act.wait_ge(hid_ready, n - 1)
                        nc.scalar.activation(sg[:, n % 2, :], banks[n % 2][:, :], ACT.Silu).then_inc(silu_ready, 1)
                    if n >= 1:
                        act.wait_ge(ht_filled, n)
                        if n >= 2:
                            act.wait_ge(dn_filled, n - 1)
                        nc.scalar.copy(hidT[:, :, :].rearrange("p c t -> p (c t)"), banks[5][:, :]).then_inc(ht_stored, 1)

        @block.vector
        def _(dve):
            dve.nop().then_inc(dve_emptied, ND)
            nc.vector.memset(w_q[:, :, :, HD:], 0.0).then_inc(padded, 1)
            nc.vector.memset(w_k[:, :, :, HD:], 0.0).then_inc(padded, 1)
            nc.vector.memset(vp[:, :, :, HD:], 1.0).then_inc(padded, 1)
            norm_vector(nc, dve, norm, x)
            if modulated:
                dve.wait_ge(sq_ready, 1)
                nc.vector.tensor_reduce(ms[:, :], sq[:, :, :], AX.X, ALU.add).then_inc(ms_ready, 1)
                dve.wait_ge(ms_ready, 1)
                nc.vector.tensor_scalar(ms[:, :], ms[:, :], 1.0 / D, RMS_EPS, ALU.mult, ALU.add).then_inc(ms_ready, 1)
                dve.wait_ge(rms_ready, 1)
                for t in range(NT):
                    nc.vector.tensor_scalar(xr[:, t, :], norm.xn[:, t, :], rms[:, t:t + 1], None, ALU.mult).then_inc(xr_ready, 1)
                for t in range(NT):
                    nc.vector.tensor_tensor(x[:, t, :], x[:, t, :], norm.xn[:, t, :], ALU.add)
            dve.wait_ge(loaded, 16 * NLOAD)
            with dve.Fori(0, NB) as b:
                for s in dve_steps:
                    kind, src = s[0], bank(s)
                    dve.wait_ge(filled, full(b, s))
                    if kind == "qk":
                        _, r, g = s
                        if g == 0 and r >= 2:
                            dve.wait_ge(filled, full(b, ("pt", r - 2, 2)))
                        h = 0 if modulated else r * GROUP + g
                        nc.vector.memset(tick[:, r * GROUP + g:r * GROUP + g + 1], 0.0)
                        for i, (lo, hi) in enumerate(((0, S), (S, PAIR))):
                            last = nc.vector.tensor_tensor_reduce(
                                out=sc[:, r % 2, g, lo:hi], in0=src[:, lo:hi], in1=bias[:, h, lo:hi], scale=0.25,
                                scalar=-3e38, op0=ALU.add, op1=ALU.max, accum_out=top[:, r % 2, i, g:g + 1])
                        last.then_inc(dve_emptied, 1)
                    elif kind == "pt":
                        nc.vector.tensor_copy(pT[:, 2, :, :].rearrange("p g t -> p (g t)"), src[:, :]).then_inc(dve_emptied, 1)
                    elif kind == "pv":
                        r = s[1]
                        both = src[:, 0:2 * GROUP * (HD + 1)].rearrange("p (t g c) -> p t g c", t=2, c=HD + 1)
                        nc.vector.reciprocal(rec[:, r, :, :], both[:, :, :, HD]).then_inc(rec_ready, 1)
                        dve.wait_ge(rec_ready, b * ROUNDS + (r + 1))
                        nc.vector.tensor_tensor(
                            att[:, :, r * GROUP:(r + 1) * GROUP, :], both[:, :, :, 0:HD],
                            rec[:, r, :, :].rearrange("p t (g a) -> p t g a", a=1).broadcast_to([P, 2, GROUP, HD]),
                            ALU.mult).then_inc(dve_emptied, 1)
                    elif kind == "wo":
                        xb = x[:, bass.ds(b * 2, 2), :]
                        nc.vector.tensor_tensor(xb, src[:, :].rearrange("p (t d) -> p t d", t=2), xb,
                                                ALU.add).then_inc(dve_emptied, 1)
                    elif kind == "ha":
                        dve.wait_ge(act_emptied, act_done(b, ("tanh",)))
                        nc.vector.scalar_tensor_tensor(out=modT[:, bass.ds(b * S, S)], in0=tanhT[:, :], scalar=0.1,
                                                       in1=src[0:LORA, 0:S], op0=ALU.mult, op1=ALU.mult).then_inc(dve_emptied, 1)
            if modulated:
                for n in range(2 * NT + 1):
                    if n < 2 * NT:
                        dve.wait_ge(up_filled, n + 1)
                        dve.wait_ge(silu_ready, n + 1)
                        if n >= 2:
                            dve.wait_ge(ht_filled, n - 1)
                        nc.vector.tensor_tensor(hid[:, n % 2, :], banks[2 + n % 2][:, :], sg[:, n % 2, :],
                                                ALU.mult).then_inc(hid_ready, 1)
                    if n >= 1:
                        t = (n - 1) // 2
                        dve.wait_ge(dn_filled, n)
                        if n >= 2:
                            dve.wait_ge(dn_stored, n - 1)
                        nc.vector.tensor_tensor(x[:, t, :], banks[6 + (n - 1) % 2][:, 0:D], x[:, t, :],
                                                ALU.add).then_inc(dn_stored, 1)

        @block.gpsimd
        def _(pool):
            norm_pool(nc, pool, norm, minus_half)
            if modulated:
                pool.wait_ge(norm.normed, NT)
                nc.gpsimd.tensor_tensor(sq[:, :, :], norm.xn[:, :, :], norm.xn[:, :, :], ALU.mult).then_inc(sq_ready, 1)
                pool.wait_ge(ms_ready, 2)
                nc.gpsimd.tensor_tensor(rms[:, :], ms[:, :], minus_half, ALU.pow).then_inc(rms_ready, 1)
            with pool.Fori(0, NB) as b:
                for r in range(ROUNDS):
                    pool.wait_ge(dve_emptied, dve_done(b, ("qk", r, GROUP - 1)))
                    for i, (lo, hi) in enumerate(((0, S), (S, PAIR))):
                        part = sc[:, r % 2, :, lo:hi]
                        last = nc.gpsimd.tensor_tensor(
                            part, part, top[:, r % 2, i, :].rearrange("p (g a) -> p g a", a=1).broadcast_to([P, GROUP, hi - lo]),
                            ALU.subtract)
                    last.then_inc(shifted, 1)


def alibi_layer(nc, consts, x, weights, bias_const, banks):
    attention_layer(nc, consts, x, weights, bias_const, banks, False)


def mod_layer(nc, consts, x, weights, bias_const, banks):
    attention_layer(nc, consts, x, weights, bias_const, banks, True)


_NAMES = ['L0_attn_hidden_states', 'L0_attn_W_qkvz', 'L0_attn_W_ba', 'L0_attn_conv_w', 'L0_attn_dt_bias', 'L0_attn_A_log', 'L0_attn_norm_weight', 'L0_attn_W_out', 'L0_ffn_router_w', 'L0_ffn_gate_up_proj', 'L0_ffn_down_proj', 'L0_ffn_shared_gate_w', 'L0_ffn_shared_up_w', 'L0_ffn_shared_down_w', 'L1_attn_Wq', 'L1_attn_Wkv', 'L1_attn_Wo', 'L1_attn_bo', 'L1_ffn_ln1_w', 'L1_ffn_ln2_w', 'L1_ffn_Wq', 'L1_ffn_Wk', 'L1_ffn_Wv', 'L1_ffn_Wo', 'L1_ffn_A', 'L1_ffn_B', 'L1_ffn_W_in_base', 'L1_ffn_W_up_base', 'L1_ffn_W_down']


def program(nc, a, const_f, const_m, out):
    with ExitStack() as ctx:
        cf = ctx.enter_context(nc.sbuf_tensor("const_f", [P, 4 * P], F32))
        masks = ctx.enter_context(nc.sbuf_tensor("masks", [P, 2 * LEVELS, P], I32))
        minus_half = ctx.enter_context(nc.sbuf_tensor("minus_half", [P, NT], F32))
        x = ctx.enter_context(nc.sbuf_tensor("x", [P, NT, D], F32))
        banks = [ctx.enter_context(nc.psum_tensor(f"bank{i}", [P, 512], F32)) for i in range(8)]
        loaded = ctx.enter_context(nc.semaphore("consts_loaded"))
        stored = ctx.enter_context(nc.semaphore("output_stored"))
        ident, upto, after, below = (cf[:, i * P:(i + 1) * P] for i in range(4))
        consts = (ident, upto, after, below, masks, minus_half[:, :])
        with nc.Block() as block:
            @block.sync
            def _(sync):
                sync.dma_start(x[:, :, :], a['L0_attn_hidden_states'].rearrange("b (t p) d -> p (b t) d", p=P)).then_inc(loaded, 16)
                sync.dma_start(cf[:, :], const_f).then_inc(loaded, 16)
                sync.dma_start(masks[:, :, :].rearrange("p l t -> p (l t)"), const_m).then_inc(loaded, 16)
                sync.wait_ge(loaded, 48)

            @block.vector
            def _(dve):
                nc.vector.memset(minus_half[:, :], -0.5)
        delta_layer(nc, consts, x, *[a['L0_attn_' + n] for n in ('W_qkvz', 'W_ba', 'conv_w', 'dt_bias', 'A_log', 'norm_weight', 'W_out')], banks)
        expert_layer(nc, consts, x, *[a['L0_ffn_' + n] for n in ('router_w', 'gate_up_proj', 'down_proj', 'shared_gate_w', 'shared_up_w', 'shared_down_w')], a["rconst"], a["slot_in"], a["slot_out"], banks)
        alibi_layer(nc, consts, x, {**{k: a['L1_attn_' + k] for k in ('Wq', 'Wo', 'bo')}, 'Wk': a['L1_attn_Wkv'][:, 0:GROUP * HD], 'Wv': a['L1_attn_Wkv'][:, GROUP * HD:], 'ones': a['ones']}, a['alibi'], banks)
        mod_layer(nc, consts, x, {k: a['L1_ffn_' + n] for k, n in (('Wq', 'Wq'), ('Wk', 'Wk'), ('Wv', 'Wv'), ('Wo', 'Wo'), ('ln1', 'ln1_w'), ('ln2', 'ln2_w'), ('A', 'A'), ('B', 'B'), ('W_in', 'W_in_base'), ('W_up', 'W_up_base'), ('W_down', 'W_down'))}, a['causal'], banks)
        with nc.Block() as block:
            @block.sync
            def _(sync):
                sync.dma_start(out.rearrange("b (t p) d -> p (b t) d", p=P), x[:, :, :]).then_inc(stored, 16)
                sync.wait_ge(stored, 16)


def kernel(**inputs):
    import numpy as _np
    import concourse.bacc as _bacc
    from concourse import mybir as _mybir
    from concourse.bass_utils import run_bass_kernel_spmd as _run

    nc = _bacc.Bacc("TRN2", target_bir_lowering=False, num_devices=1)
    arrays, handles = {}, {}
    turned = ('L0_ffn_router_w', 'L1_ffn_Wq', 'L1_ffn_Wk', 'L1_ffn_Wv', 'L1_ffn_Wo', 'L1_ffn_W_in_base', 'L1_ffn_W_up_base',
              'L1_ffn_W_down')
    for name in _NAMES:
        v = _np.asarray(inputs[name])
        v = _np.ascontiguousarray(v.T if name in turned else v)
        arrays[f"in_{name}"] = v
        handles[name] = nc.dram_tensor(f"in_{name}", v.shape, _mybir.dt.from_np(v.dtype), kind="ExternalInput").ap()
    consts = []
    for name, v in zip(("const_f32", "const_mask"), constant_arrays()):
        arrays[name] = v
        consts.append(nc.dram_tensor(name, v.shape, _mybir.dt.from_np(v.dtype), kind="ExternalInput").ap())
    for name, v in (("rconst", routing_constants()), ("alibi", score_bias(alibi_slopes())),
                    ("causal", score_bias([0.0])), ("ones", _np.ones((1, P), _np.float32))):
        arrays[name] = v
        handles[name] = nc.dram_tensor(name, v.shape, F32, kind="ExternalInput").ap()
    for name, tiles in (("slot_in", SLOTS + 1), ("slot_out", SLOTS)):
        handles[name] = nc.dram_tensor(name, (tiles * P, D), F32, kind="Internal").ap()
    out = nc.dram_tensor("out", (NB, S, D), F32, kind="ExternalOutput").ap()
    program(nc, handles, *consts, out)
    r = _run(nc, [arrays], core_ids=[0])
    return r.results[0]["out"]
```

```python
from contextlib import ExitStack

import numpy as np
import concourse.bass as bass
from concourse import mybir

F32 = mybir.dt.float32
BF16 = mybir.dt.bfloat16
I32 = mybir.dt.int32
ALU = mybir.AluOpType
ACT = mybir.ActivationFunctionType
AX = mybir.AxisListType

P = 128
NB, S, D = 4, 256, 256
TOK = NB * S
NT = TOK // P
KT = D // P
LN_EPS = 1e-5
RMS_EPS = 1e-6

HK, HV = 8, 16
VPK = HV // HK
HEADW = 2 * P + 2 * VPK * P
TAPS = 4
Q = 32
WARM_ROW = 22
UNITS = 2 * VPK


def constant_arrays():
    r = np.arange(P)
    row, col = r[:, None], r[None, :]
    ident = (row == col).astype(np.float32)
    upto = (row <= col).astype(np.float32)
    after = (row > col).astype(np.float32)
    below = np.where(col < row, -30000.0, 0.0).astype(np.float32)
    f = np.concatenate([ident, upto, after, below], axis=1)
    return f


class Norm:

    def __init__(self, nc, ctx, tag, xn=None):
        sem = lambda n: ctx.enter_context(nc.semaphore(f"{tag}_{n}"))
        sb = lambda n, shape: ctx.enter_context(nc.sbuf_tensor(f"{tag}_{n}", shape, F32))
        self.stats_done, self.rstd_ready, self.normed = sem("stats_done"), sem("rstd_ready"), sem("normed")
        self.turned, self.stored = sem("turned"), sem("stored")
        self.stats = sb("stats", [P, NT, 6])
        self.moments = sb("moments", [P, NT, 2])
        self.var_eps = sb("var_eps", [P, NT])
        self.rstd = sb("rstd", [P, NT])
        self.xn = sb("xn", [P, NT, D]) if xn is None else xn
        self.xnT = sb("xnT", [P, KT, TOK])


def norm_vector(nc, dve, n, x):
    for t in range(NT):
        nc.vector.bn_stats(n.stats[:, t, :], x[:, t, :]).then_inc(n.stats_done, 1)
    dve.wait_ge(n.stats_done, NT)
    for t in range(NT):
        nc.vector.bn_aggr(n.moments[:, t, :], n.stats[:, t, :]).then_inc(n.stats_done, 1)
    dve.wait_ge(n.stats_done, 2 * NT)
    nc.vector.tensor_scalar(n.var_eps[:, :], n.moments[:, :, 1], LN_EPS, None,
                            ALU.add).then_inc(n.stats_done, 1)
    dve.wait_ge(n.rstd_ready, 1)
    for t in range(NT):
        nc.vector.tensor_scalar(n.xn[:, t, :], x[:, t, :], n.moments[:, t, 0:1], n.rstd[:, t:t + 1],
                                ALU.subtract, ALU.mult).then_inc(n.normed, 1)


def norm_pool(nc, pool, n, minus_half):
    pool.wait_ge(n.stats_done, 2 * NT + 1)
    nc.gpsimd.tensor_tensor(n.rstd[:, :], n.var_eps[:, :], minus_half, ALU.pow).then_inc(n.rstd_ready, 1)


def norm_tensor(nc, pe, n, bank, ident, src=None, ready=None):
    src = n.xn if src is None else src
    for j in range(NT // 2):
        pe.wait_ge(n.normed if ready is None else ready, 2 * j + 2)
        for t in range(2):
            for k in range(KT):
                last = nc.tensor.transpose(bank[j][:, (k * 2 + t) * P:(k * 2 + t + 1) * P],
                                           src[:, 2 * j + t, k * P:(k + 1) * P], ident)
        last.then_inc(n.turned, 1)


def norm_scalar(nc, act, n, bank):
    for j in range(NT // 2):
        act.wait_ge(n.turned, j + 1)
        nc.scalar.copy(n.xnT[:, :, 2 * j * P:(2 * j + 2) * P],
                       bank[j][:, :].rearrange("p (k t) -> p k t", k=KT)).then_inc(n.stored, 1)


def delta_steps():
    proj = lambda p, cts: [("proj", p, ct, half) for ct in cts for half in range(2)]
    gate = lambda p: [("gate", p, j) for j in range(4)]

    def front(p):
        return [("norms", p), ("ktok", p)] + [("vtok", p, j) for j in range(4)] + [
            (kind, p, b) for b in range(NB) for kind in ("decay", "gram")]

    def inverse(p):
        return ([("mid5", p, j) for j in range(2)] + [(k, p, j) for j in range(2) for k in ("upper5", "lower5")]
                + [("mid6", p, j) for j in range(2)] + [("upper6", p, j) for j in range(2)])

    def back(p):
        two = lambda kind: [(kind, p, j) for j in range(2)]
        return (two("solve1") + two("state") + two("kstate") + two("qstate") + two("solve2") + two("out1")
                + two("out2"))

    tail = lambda p: [("turn", p, j) for j in range(4)] + [("final", p, j) for j in range(4)]

    first = proj(0, range(4))
    last = tail(0) + tail(1)
    steps = proj(1, range(2)) + front(0) + proj(1, range(2, 4)) + gate(0)[:2] + front(1)
    steps += gate(0)[2:] + gate(1)
    steps += inverse(0)
    def turns(a, b):
        return [s for i in range(max(len(a), len(b))) for s in a[i:i + 1] + b[i:i + 1]]

    steps += turns(back(0), inverse(1)) + back(1)
    return first, last, steps


BY_ACT = {"proj", "gate", "ktok", "decay", "mid5", "mid6", "solve1", "state", "qstate", "solve2", "out1", "turn"}


def delta_layer(nc, consts, x, W_qkvz, W_ba, conv_w, dt_bias, A_log, norm_weight, W_out, banks):
    ident, upto, after, below, minus_half = consts
    AHEAD, TAIL, MAIN = delta_steps()
    STEPS = AHEAD + TAIL + MAIN
    NS = len(STEPS)
    NBANK = len(banks)
    pos = {s: i for i, s in enumerate(STEPS)}
    act_steps = [s for s in STEPS if s[0] in BY_ACT]
    dve_steps = [s for s in STEPS if s[0] not in BY_ACT]
    act_pos = {s: i for i, s in enumerate(act_steps)}
    dve_pos = {s: i for i, s in enumerate(dve_steps)}
    NA, ND = len(act_steps), len(dve_steps)
    by_act = lambda steps: sum(s in act_pos for s in steps)
    PAIRS = HK // 2

    LINKS = 2 * ((TAPS - 2) * 4 + 2) + 1 + 2 * (Q - 1)
    with ExitStack() as ctx:
        sb = lambda n, shape, dt=F32: ctx.enter_context(nc.sbuf_tensor("dl_" + n, shape, dt))
        sem = lambda n: ctx.enter_context(nc.semaphore("dl_" + n))
        w_head = sb("w_head", [P, 2, KT, HEADW])
        w_ba = sb("w_ba", [P, KT, 4 * HK])
        taps = sb("taps", [P, 4 * HK, TAPS])
        w_out = sb("w_out", [P, 2 * VPK, D])
        gain = sb("gain", [P, 1])
        dtb = sb("dtb", [P, HV])
        rate = sb("rate", [P, HV])
        ones = sb("ones", [P, 1])
        tick = sb("tick", [P, 1])
        ident_b = sb("ident_b", [P, P], BF16)
        below_b = sb("below_b", [P, 4, P], BF16)
        beta = sb("beta", [P, NT, HV])
        gate_in = sb("gate_in", [P, NT, HV])
        sp = [sb(f"sp{i}", [P, NT, HV]) for i in range(4)]
        g = sb("g", [P, NT, HV])
        decay0 = sb("decay0", [P, NT, HV])
        xpad = sb("xpad", [P, 2, NB, S + TAPS - 1])
        conv = sb("conv", [P, 2, NB, S])
        kq = sb("kq", [P, 2, NT, 2, P])
        ktok = sb("ktok", [P, 2, NB, P])
        nv = sb("nv", [P, 2, NT, VPK, P])
        sz = sb("sz", [P, 2, NT, VPK, P])
        ssq = sb("ssq", [P, 2, 2, NT])
        inv2 = sb("inv2", [P, 2, 2, NT])
        power = sb("power", [P, NT])
        half = sb("half", [P, NT])
        ninvr = sb("ninvr", [P, NT])
        cneg = sb("cneg", [P, 2, NT, VPK])
        last_c = sb("last_c", [P, 2, NB, VPK])
        mg = sb("mg", [P, 2, 4, P])
        nA = sb("nA", [P, 2, NB, 4, P])
        nB = sb("nB", [P, 2, NB, 4, P])
        T = sb("T", [P, 2, NB, 4, P])
        U = sb("U", [P, 2, NB, 4, P])
        X = sb("X", [P, NB, 4, P])
        lanes = sb("lanes", [P, 2 * Q * Q + Q * Q // 4])
        blockA = lanes[:, 0:Q * Q].rearrange("p (t s) -> p t s", t=Q)
        blockT = lanes[:, Q * Q:2 * Q * Q].rearrange("p (t s) -> p t s", t=Q)
        norm = Norm(nc, ctx, "dl", xn=nA[:, 0, :, :, :].rearrange("p b u t -> p (b u t)").rearrange("p (t d) -> p t d", t=NT))
        rq = sb("rq", [P, 2, NB, VPK, P])
        vT = rq[:, :, :, :, :].rearrange("p v b i t -> p v (b i t)")
        sq = X[:, :, :, :].rearrange("p b u t -> p (b u) t").rearrange("p (i n) t -> p i n t", i=2)
        f = lanes[:, 0:2 * NB * VPK * P].rearrange("p (c b v d) -> p c b v d", c=2, b=NB, v=VPK)
        flat_conv = conv[:, :, :, :].rearrange("p i b t -> p (i b t)")
        fd = flat_conv[:, 0:NB * VPK * P].rearrange("p (b v d) -> p b v d", b=NB, v=VPK)
        state = flat_conv[:, NB * VPK * P:].rearrange("p (b v d) -> p b v d", b=NB, v=VPK)
        rhs2, qs = rq[:, 0], rq[:, 1]
        o = nA[:, :, :, :, :].rearrange("p i b (c v) d -> p i b c v d", c=2)
        osq = X[:, :, :, :].rearrange("p b u t -> p (b u) t")
        oss = sb("oss", [P, NT, VPK])
        fac = sb("fac", [P, 2, NT, VPK])
        fac2 = sb("fac2", [P, NT, VPK])
        minus_half2 = sb("minus_half2", [P, NT * VPK])
        og = T
        ogT = U

        loaded, w_loaded, prep, out_loaded = sem("loaded"), sem("w_loaded"), sem("prep"), sem("out_loaded")
        ba_done, sp_ready, g_ready, cum_done, start_ready = [sem(n) for n in (
            "ba_done", "sp_ready", "g_ready", "cum_done", "start_ready")]
        act_link = sem("act_link")
        filled, act_emptied, dve_emptied = sem("filled"), sem("act_emptied"), sem("dve_emptied")
        padded, conv_link, conv_done, silu_done, sq_done = [sem(n) for n in (
            "padded", "conv_link", "conv_done", "silu_done", "sq_done")]
        ssq_ready, root_ready, scale_ready = [sem(n) for n in ("ssq_ready", "root_ready", "scale_ready")]
        mg_ready, dtc_ready, tu_ready, fd_ready = [sem(n) for n in ("mg_ready", "dtc_ready", "tu_ready", "fd_ready")]
        factored, cleared, inverted = sem("factored"), sem("cleared"), sem("inverted")
        rows_done = sem("rows_done")
        rhs_link, osq_ready, oss_ready, fac_ready, og_ready = [sem(n) for n in (
            "rhs_link", "osq_ready", "oss_ready", "fac_ready", "og_ready")]
        dve_link, rms_link = sem("dve_link"), sem("rms_link")
        block = ctx.enter_context(nc.Block())

        def full(h, s):
            return NS * h + (pos[s] + 1)

        def act_done(h, s):
            return NA * h + (NA + act_pos[s] + 1)

        def dve_done(h, s):
            return ND * h + (ND + dve_pos[s] + 1)

        def bank(s):
            return banks[pos[s] % NBANK]

        def columns(kind, m, p, b, u):
            if kind == "mid6":
                return m[:, p, b, u, 0:2 * Q]
            if kind == "upper6":
                return m[:, p, b, u, 2 * Q:]
            blocks = m[:, p, b, u, :].rearrange("p (n t) -> p n t", n=2)
            return blocks[:, :, 0:Q] if kind == "mid5" else blocks[:, :, Q:]

        def bank4(s):
            return bank(s)[:, :].rearrange("p (u t) -> p u t", u=4)

        def channel_tile(h, p, ct):
            first = (0, HK, 2 * HK, 2 * HK + 1)[ct]
            return h * (2 if ct < 2 else 2 * VPK) + (first + (p if ct < 2 else p * VPK))

        def silu(act, h, p, ct):
            act.wait_ge(conv_done, h * 8 + (4 * p + ct + 3))
            c = conv[:, ct % 2, :, :].rearrange("p b t -> p (b t)")
            c2 = conv[:, ct % 2, :, :].rearrange("p b (c t) -> p (b c) t", c=2)
            if ct < 2:
                nc.scalar.activation(kq[:, p, :, 1 - ct, :], c2, ACT.Silu).then_inc(silu_done, 1)
            else:
                nc.scalar.activation(vT[:, ct - 2, :], c, ACT.Silu).then_inc(silu_done, 1)

        @block.sync
        def _(sync):
            sync.dma_start(w_ba[:, :, :], W_ba.rearrange("(k p) n -> p k n", p=P)).then_inc(loaded, 16)
            sync.dma_start(taps[:, :, :], conv_w.rearrange("(c p) j -> p c j", p=P)).then_inc(loaded, 16)
            sync.dma_start(gain[:, :], norm_weight.rearrange("(p a) -> p a", a=1)).then_inc(loaded, 16)
            sync.dma_start(dtb[:, :], dt_bias.rearrange("(a h) -> a h", a=1).broadcast_to([P, HV])).then_inc(loaded, 16)
            sync.dma_start(rate[:, :], A_log.rearrange("(a h) -> a h", a=1).broadcast_to([P, HV])).then_inc(loaded, 16)
            w = W_qkvz.rearrange("(k p) (h n) -> p k h n", p=P, h=HK)
            wo = W_out.rearrange("(h p) n -> p h n", p=P)

            def load(first):
                for k in range(KT):
                    sync.dma_start(w_head[:, :, k, :], w[:, k, first, :]).then_inc(w_loaded, 16)

            load(slice(0, 2))
            sync.dma_start(w_out[:, :, :], wo[:, 0:2 * VPK, :]).then_inc(out_loaded, 16)
            with sync.Fori(0, PAIRS - 1) as h:
                sync.wait_ge(filled, full(h, ("gate", 1, 3)))
                load(bass.ds(h * 2 + 2, 2))
                sync.wait_ge(filled, full(h + 1, ("final", 1, 3)))
                sync.dma_start(w_out[:, :, :], wo[:, bass.ds(h * (2 * VPK) + 2 * VPK, 2 * VPK), :]).then_inc(out_loaded, 16)

        @block.tensor
        def _(pe):
            norm_tensor(nc, pe, norm, banks, ident)
            pe.wait_ge(loaded, 80)
            pe.wait_ge(norm.stored, NT // 2)
            for t in range(NT):
                for k in range(KT):
                    last = nc.tensor.matmul(banks[4][:, t * 4 * HK:(t + 1) * 4 * HK],
                                            norm.xnT[:, k, t * P:(t + 1) * P], w_ba[:, k, :],
                                            start=(k == 0), stop=(k == KT - 1))
            last.then_inc(ba_done, 1)
            def steps_of(h, part):
                def sources(s):
                    kind, p, j = s[0], s[1], s[-1]
                    return {"mid6": [("lower5", p, j)], "upper5": [("mid5", p, j)], "upper6": [("mid6", p, j)],
                            "solve1": [("upper6", p, j)], "solve2": [("kstate", p, j)],
                            "kstate": [("state", p, j)], "qstate": [("state", p, j)], "out1": [("solve1", p, j)],
                            "out2": [("solve2", p, j)], "final": [("turn", p, j)]}.get(kind, [])

                def begin(s):
                    earlier = [q for q in STEPS[:pos[s]] if bank(q) is bank(s)]
                    before = (earlier or [q for q in STEPS if bank(q) is bank(s)])[-1]
                    mine = ([before] if earlier else []) + sources(s)
                    for emptied, order, count in ((act_emptied, act_pos, NA), (dve_emptied, dve_pos, ND)):
                        this = [order[q] for q in mine if q in order]
                        if this:
                            pe.wait_ge(emptied, count * h + (count + max(this) + 1))
                        elif not earlier and before in order:
                            pe.wait_ge(emptied, count * h + (order[before] + 1))

                for s in part:
                    kind, p, j = s[0], s[1], s[-1]
                    begin(s)
                    out, out4 = bank(s), bank4(s)
                    out8 = out[:, :].rearrange("p (b u t) -> p b u t", b=2, u=UNITS)
                    if kind == "proj":
                        _, _, ct, hf = s
                        if ct == 0:
                            pe.wait_ge(w_loaded, h * 32 + 32)
                        for k in range(KT):
                            last = nc.tensor.matmul(out[:, :], w_head[:, p, k, ct * P:(ct + 1) * P],
                                                    norm.xnT[:, k, hf * 512:(hf + 1) * 512],
                                                    start=(k == 0), stop=(k == KT - 1))
                    elif kind == "gate":
                        if s == ("gate", 1, 0):
                            pe.wait_ge(rows_done, h + 1)
                        for t in range(2):
                            for k in range(KT):
                                tile = 2 * j + t
                                last = nc.tensor.matmul(out[:, t * 256:(t + 1) * 256],
                                                        norm.xnT[:, k, tile * P:(tile + 1) * P],
                                                        w_head[:, p, k, 4 * P:6 * P],
                                                        start=(k == 0), stop=(k == KT - 1))
                    elif kind == "norms":
                        pe.wait_ge(sq_done, h * 4 + (2 * p + 2))
                        for i in range(2):
                            for t in range(NT):
                                last = nc.tensor.matmul(out[:, i * NT + t:i * NT + t + 1], sq[:, i, t, :],
                                                        ones[:, :], start=True, stop=True)
                    elif kind == "ktok":
                        for b in range(NB):
                            last = nc.tensor.transpose(out4[:, b, :], kq[:, p, 2 * b, 0, :], ident)
                    elif kind == "vtok":
                        pe.wait_ge(silu_done, h * 8 + (4 * p + 6))
                        for t in range(2):
                            for v in range(VPK):
                                tile = 2 * j + t
                                last = nc.tensor.transpose(out4[:, 2 * t + v, :],
                                                           vT[:, v, tile * P:(tile + 1) * P], ident)
                    elif kind == "decay":
                        pe.wait_ge(mg_ready, h * (2 * NB) + (p * NB + j + 1))
                        nc.tensor.matmul(out[:, :], ident_b[:, :], below_b[:, :, :].rearrange("p u t -> p (u t)"),
                                         start=True, stop=False)
                        last = nc.tensor.matmul(out[:, :], after, mg[:, j % 2, :, :].rearrange("p u t -> p (u t)"),
                                                start=False, stop=True)
                    elif kind == "gram":
                        for c in range(2):
                            tile = 2 * j + c
                            last = nc.tensor.matmul(out[:, c * 256:(c + 1) * 256], kq[:, p, tile, 0, :],
                                                    kq[:, p, tile, :, :].rearrange("p i t -> p (i t)"),
                                                    start=True, stop=True)
                    elif kind in ("mid5", "mid6"):
                        if kind == "mid5":
                            pe.wait_ge(inverted, h * 2 + 1)
                        for b in range(2):
                            for u in range(UNITS):
                                a_u, cols = nA[:, p, 2 * j + b, u, :], columns(kind, T, p, 2 * j + b, u)
                                if kind == "mid5":
                                    last = nc.tensor.matmul(out8[:, b, u, :], a_u, cols, start=True, stop=True)
                                else:
                                    last = nc.tensor.matmul(out8[2 * Q:, b, u, :], a_u[:, 2 * Q:], cols,
                                                            start=True, stop=True)
                    elif kind in ("upper5", "upper6"):
                        if kind == "upper5":
                            pe.wait_ge(inverted, h * 2 + 2)
                        for b in range(2):
                            for u in range(UNITS):
                                if kind == "upper5":
                                    last = nc.tensor.matmul(out8[:, b, u, :], X[:, 2 * j + b, u, :],
                                                            columns(kind, U, p, 2 * j + b, u), start=True, stop=True)
                                else:
                                    last = nc.tensor.matmul(out8[0:2 * Q, b, u, :], X[:, 2 * j + b, u, 0:2 * Q],
                                                            columns(kind, U, p, 2 * j + b, u), start=True, stop=True)
                    elif kind == "lower5":
                        for b in range(2):
                            for u in range(UNITS):
                                x_cols = X[:, 2 * j + b, u, :].rearrange("p (n t) -> p n t", n=2)[:, :, 0:Q]
                                last = nc.tensor.matmul(out8[:, b, u, :], U[:, p, 2 * j + b, u, :], x_cols,
                                                        start=True, stop=True)
                    elif kind in ("solve1", "solve2"):
                        c = 0 if kind == "solve1" else 1
                        for i in range(2):
                            b = 2 * j + i
                            for v in range(VPK):
                                rhs = rhs2[:, b, v, :] if c else nv[:, p, 2 * b, v, :]
                                last = nc.tensor.matmul(out4[:, 2 * i + v, :], U[:, p, b, 2 * c + v, :], rhs,
                                                        start=True, stop=True)
                    elif kind == "state":
                        pe.wait_ge(fd_ready, h * 4 + (2 * p + j + 1))
                        for i in range(2):
                            b = 2 * j + i
                            last = nc.tensor.matmul(out[:, i * 256:(i + 1) * 256], ktok[:, p, b, :],
                                                    fd[:, b, :, :].rearrange("p v d -> p (v d)"),
                                                    start=True, stop=True)
                    elif kind in ("kstate", "qstate"):
                        for i in range(2):
                            b = 2 * j + i
                            last = nc.tensor.matmul(out[:, i * 256:(i + 1) * 256],
                                                    kq[:, p, 2 * b + 1, 0 if kind == "kstate" else 1, :],
                                                    state[:, b, :, :].rearrange("p v d -> p (v d)"),
                                                    start=True, stop=True)
                    elif kind in ("out1", "out2"):
                        c = 0 if kind == "out1" else 1
                        for i in range(2):
                            b = 2 * j + i
                            for v in range(VPK):
                                last = nc.tensor.matmul(out4[:, 2 * i + v, :], nB[:, p, b, 2 * c + v, :],
                                                        f[:, c, b, v, :], start=True, stop=True)
                    elif kind == "turn":
                        pe.wait_ge(og_ready, h * (2 * NB) + (p * NB + j + 1 - 2 * NB))
                        for u in range(4):
                            last = nc.tensor.transpose(out4[:, u, :], og[:, p, j, u, :], ident)
                    elif kind == "final":
                        pe.wait_ge(out_loaded, h * 16)
                        for c in range(2):
                            for v in range(VPK):
                                last = nc.tensor.matmul(
                                    out[:, c * 256:(c + 1) * 256], ogT[:, p, j, 2 * c + v, :],
                                    w_out[:, p * VPK + v, :], start=(v == 0), stop=(v == VPK - 1))
                    last.then_inc(filled, 1)

            steps_of(0, AHEAD[:4])
            pe.wait_ge(g_ready, 1)
            nc.tensor.matmul(banks[5][:, 0:NT * HV], upto, g[:, :, :].rearrange("p t h -> p (t h)"),
                             start=True, stop=True).then_inc(cum_done, 1)
            pe.wait_ge(start_ready, 1)
            steps_of(0, AHEAD[4:])
            pe.wait_ge(filled, len(AHEAD))
            pe.nop().then_inc(filled, len(TAIL))
            pe.wait_ge(act_emptied, NA + by_act(AHEAD))
            steps_of(0, MAIN)
            with pe.Fori(1, PAIRS) as h:
                steps_of(h, STEPS)
            pe.wait_ge(filled, NS * PAIRS)
            pe.nop().then_inc(filled, len(AHEAD))
            pe.wait_ge(act_emptied, NA * (PAIRS + 1))
            pe.wait_ge(dve_emptied, ND * (PAIRS + 1))
            steps_of(PAIRS, TAIL)

        @block.scalar
        def _(act):
            act.nop().then_inc(act_emptied, NA)
            act.nop().then_inc(silu_done, 2)
            norm_scalar(nc, act, norm, banks)
            act.wait_ge(loaded, 80)
            act.wait_ge(ba_done, 1)
            ba = banks[4][:, 0:NT * 4 * HK].rearrange("p (t h i v) -> p t h i v", t=NT, h=HK, i=2)
            split = lambda m: m[:, :, :].rearrange("p t (h v) -> p t h v", v=VPK)
            for t in range(NT):
                nc.scalar.activation(split(beta)[:, t], ba[:, t, :, 0, :], ACT.Sigmoid).then_inc(sp_ready, 1)
            act.wait_ge(prep, 1)
            nc.scalar.activation(sp[0][:, :, :], gate_in[:, :, :], ACT.Abs).then_inc(act_link, 1)
            act.wait_ge(act_link, 1)
            nc.scalar.activation(sp[1][:, :, :], sp[0][:, :, :], ACT.Exp, scale=-1.0)
            nc.scalar.activation(rate[:, :], rate[:, :], ACT.Exp).then_inc(sp_ready, 1)
            act.wait_ge(padded, 10)
            act.wait_ge(cum_done, 1)
            nc.scalar.activation(decay0[:, :, :].rearrange("p t h -> p (t h)"), banks[5][:, 0:NT * HV],
                                 ACT.Exp).then_inc(start_ready, 1)
            def steps_of(h, part):
                silu_before = {("proj", 1, 0, 0): [(0, 2), (0, 3)], ("proj", 1, 2, 0): [(1, 0)], ("proj", 1, 3, 0): [(1, 1)]}
                silu_after = {("proj", 0, 1, 1): [(0, 0)], ("proj", 0, 2, 1): [(0, 1)],
                              ("gate", 0, 0): [(1, 2)], ("gate", 0, 1): [(1, 3)]}
                for s in [s for s in part if s in act_pos]:
                    kind, p, j = s[0], s[1], s[-1]
                    for tile in silu_before.get(s, []):
                        silu(act, h, *tile)
                    act.wait_ge(filled, full(h, s))
                    src, src4 = bank(s), bank4(s)
                    src_bvd = src[:, :].rearrange("p (b v d) -> p b v d", b=2, v=VPK)
                    if kind == "proj":
                        _, _, ct, hf = s
                        if hf == 0:
                            act.wait_ge(conv_done, h * 8 + (4 * p + ct + 1))
                            act.wait_ge(silu_done, h * 8 + (4 * p + ct + 1))
                        two = src[:, :].rearrange("p (b t) -> p b t", b=2)
                        tap = taps[:, bass.ds(channel_tile(h, p, ct), 1), :]
                        nc.scalar.copy(xpad[:, ct % 2, 2 * hf:2 * hf + 2, TAPS - 1:], two)
                        nc.scalar.mul(conv[:, ct % 2, 2 * hf:2 * hf + 2, :], two,
                                      tap[:, 0, TAPS - 1:TAPS]).then_inc(act_emptied, 1)
                    elif kind == "gate":
                        nc.scalar.activation(sz[:, p, 2 * j:2 * j + 2, :, :],
                                             src[:, :].rearrange("p (t v d) -> p t v d", t=2, v=VPK),
                                             ACT.Silu).then_inc(act_emptied, 1)
                    elif kind == "ktok":
                        nc.scalar.copy(ktok[:, p, :, :], src4).then_inc(act_emptied, 1)
                    elif kind == "decay":
                        nc.scalar.activation(nB[:, p, j, :, :], src4, ACT.Exp).then_inc(act_emptied, 1)
                    elif kind in ("mid5", "mid6"):
                        src8 = src[:, :].rearrange("p (n i t) -> p n i t", n=2 * UNITS, i=2 if kind == "mid5" else 1)
                        dst = X[:, 2 * j:2 * j + 2, :, :].rearrange("p b u t -> p (b u) t")
                        if kind == "mid5":
                            dst = dst.rearrange("p n (i t) -> p n i t", i=2)[:, :, :, 0:Q]
                        else:
                            dst = dst.rearrange("p n (i t) -> p n i t", i=1)[2 * Q:, :, :, 0:2 * Q]
                            src8 = src8[2 * Q:]
                        nc.scalar.copy(dst, src8).then_inc(act_emptied, 1)
                    elif kind in ("solve1", "solve2"):
                        nc.scalar.copy(f[:, 0 if kind == "solve1" else 1, 2 * j:2 * j + 2, :, :],
                                       src_bvd).then_inc(act_emptied, 1)
                    elif kind == "state":
                        nc.scalar.copy(state[:, 2 * j:2 * j + 2, :, :], src_bvd).then_inc(act_emptied, 1)
                    elif kind == "qstate":
                        for i in range(2):
                            b = 2 * j + i
                            for v in range(VPK):
                                last = nc.scalar.mul(qs[:, b, v, :], src4[:, 2 * i + v, :],
                                                     decay0[:, 2 * b + 1, bass.ds(h * (2 * VPK) + (p * VPK + v), 1)])
                        last.then_inc(act_emptied, 1)
                    elif kind == "out1":
                        nc.scalar.copy(o[:, p, 2 * j:2 * j + 2, 0, :, :], src_bvd).then_inc(act_emptied, 1)
                    elif kind == "turn":
                        nc.scalar.mul(ogT[:, p, j, :, :], src4, gain[:, 0:1]).then_inc(act_emptied, 1)
                    for tile in silu_after.get(s, []):
                        silu(act, h, *tile)

            steps_of(0, AHEAD)
            act.wait_ge(act_emptied, NA + by_act(AHEAD))
            act.nop().then_inc(act_emptied, by_act(TAIL))
            steps_of(0, MAIN)
            with act.Fori(1, PAIRS) as h:
                steps_of(h, STEPS)
            act.wait_ge(act_emptied, NA * (PAIRS + 1))
            act.nop().then_inc(act_emptied, by_act(AHEAD))
            steps_of(PAIRS, TAIL)

        @block.vector
        def _(dve):
            dve.nop().then_inc(dve_emptied, ND + len(TAIL) - by_act(TAIL))
            dve.nop().then_inc(conv_done, 2)
            nc.vector.memset(ones[:, :], 1.0).then_inc(padded, 1)
            norm_vector(nc, dve, norm, x)
            nc.vector.memset(xpad[:, :, :, :], 0.0).then_inc(padded, 1)
            nc.vector.memset(X[:, :, :, :], 0.0).then_inc(padded, 1)
            nc.vector.memset(half[:, :], 0.5).then_inc(padded, 1)
            nc.vector.memset(minus_half2[:, :], -0.5).then_inc(padded, 1)
            nc.vector.tensor_copy(ident_b[:, :], ident).then_inc(padded, 1)
            for u in range(4):
                nc.vector.tensor_copy(below_b[:, u, :], below).then_inc(padded, 1)
            links = [0]

            def link(ins):
                links[0] += 1
                ins.then_inc(dve_link, 1)
                dve.wait_ge(dve_link, links[0])

            dve.wait_ge(sp_ready, NT)
            dve.wait_ge(loaded, 80)
            ba = banks[4][:, 0:NT * 4 * HK].rearrange("p (t h i v) -> p t h i v", t=NT, h=HK, i=2)
            split = lambda m: m[:, :, :].rearrange("p t (h v) -> p t h v", v=VPK)
            for t in range(NT):
                last = nc.vector.tensor_tensor(split(gate_in)[:, t], ba[:, t, :, 1, :],
                                               dtb[:, :].rearrange("p (h v) -> p h v", v=VPK), ALU.add)
            last.then_inc(prep, 1)
            dve.wait_ge(sp_ready, NT + 1)
            e, z, z2, poly = sp[1], sp[0], sp[2], sp[3]
            link(nc.vector.tensor_scalar(z[:, :, :], e[:, :, :], 2.0, None, ALU.add))
            link(nc.vector.reciprocal(z[:, :, :], z[:, :, :]))
            link(nc.vector.tensor_tensor(z[:, :, :], z[:, :, :], e[:, :, :], ALU.mult))
            link(nc.vector.tensor_tensor(z2[:, :, :], z[:, :, :], z[:, :, :], ALU.mult))
            link(nc.vector.tensor_scalar(poly[:, :, :], z2[:, :, :], 2.0 / 17, 2.0 / 15, ALU.mult, ALU.add))
            for n in (13, 11, 9, 7, 5, 3, 1):
                link(nc.vector.tensor_tensor(poly[:, :, :], poly[:, :, :], z2[:, :, :], ALU.mult))
                link(nc.vector.tensor_scalar(poly[:, :, :], poly[:, :, :], 2.0 / n, None, ALU.add))
            link(nc.vector.tensor_tensor(poly[:, :, :], poly[:, :, :], z[:, :, :], ALU.mult))
            link(nc.vector.scalar_tensor_tensor(out=poly[:, :, :], in0=gate_in[:, :, :], scalar=0.0,
                                                in1=poly[:, :, :], op0=ALU.max, op1=ALU.add))
            for t in range(NT):
                last = nc.vector.scalar_tensor_tensor(out=g[:, t, :], in0=poly[:, t, :], scalar=-1.0,
                                                      in1=rate[:, :], op0=ALU.mult, op1=ALU.mult)
            link(last)
            nc.vector.tensor_scalar(g[:, :, :], g[:, :, :], -1000.0, None, ALU.max).then_inc(g_ready, 1)
            dve.wait_ge(start_ready, 1)
            def steps_of(h, part):
                hl = [0]

                def hlink(ins):
                    hl[0] += 1
                    ins.then_inc(conv_link, 1)
                    dve.wait_ge(conv_link, h * LINKS + hl[0])

                def convolve(p, ct):
                    dve.wait_ge(act_emptied, act_done(h, ("proj", p, ct, 1)))
                    tap = taps[:, bass.ds(channel_tile(h, p, ct), 1), :]
                    acc = conv[:, ct % 2, :, :]
                    for j in range(TAPS - 1):
                        ins = nc.vector.scalar_tensor_tensor(out=acc, in0=xpad[:, ct % 2, :, j:j + S],
                                                             scalar=tap[:, 0, j:j + 1], in1=acc,
                                                             op0=ALU.mult, op1=ALU.add)
                        if j < TAPS - 2:
                            hlink(ins)
                    ins.then_inc(conv_done, 1)

                def invert_blocks():
                    dve.wait_ge(tu_ready, h * 2 + 1)
                    units = lambda m, q: m[Q * q:Q * q + Q, :, :, :, Q * q:Q * q + Q].rearrange("s p b u t -> s (p b u) t")
                    for q in range(P // Q):
                        last = nc.vector.transpose(blockA[Q * q:Q * q + Q, :, :],
                                                   units(nA, q).rearrange("s n t -> s t n"))
                    hlink(last)
                    for i in range(Q - 1):
                        rows, cols = Q - 1 - i, i + 1
                        part = lanes[:, 2 * Q * Q:2 * Q * Q + rows * cols].rearrange("p (t j) -> p t j", t=rows)
                        hlink(nc.vector.tensor_tensor(part, blockA[:, i + 1:Q, i:i + 1].broadcast_to([P, rows, cols]),
                                                      blockT[:, i:i + 1, 0:cols].broadcast_to([P, rows, cols]), ALU.mult))
                        below_i = blockT[:, i + 1:Q, 0:cols]
                        hlink(nc.vector.tensor_tensor(below_i, below_i, part, ALU.add))
                        if i == WARM_ROW:
                            dve.nop().then_inc(rows_done, 1)
                    for q in range(P // Q):
                        last = nc.vector.transpose(units(T, q).rearrange("s n t -> s t n"),
                                                   blockT[Q * q:Q * q + Q, :, :].rearrange("n t j -> n j t"))
                    last.then_inc(inverted, 1)
                    dve.wait_ge(tu_ready, h * 2 + 2)
                    for q in range(P // Q):
                        last = nc.vector.transpose(units(U, q).rearrange("s n t -> s t n"), blockT[Q * q:Q * q + Q, :, :])
                    last.then_inc(inverted, 1)

                def normalise(n, p):
                    links = [0]

                    def rlink(ins):
                        links[0] += 1
                        ins.then_inc(rms_link, 1)
                        dve.wait_ge(rms_link, n * (VPK + 2) + links[0])

                    dve.wait_ge(osq_ready, n + 1)
                    rlink(nc.vector.tensor_reduce(oss[:, :, :].rearrange("p t v -> p (t v)"), osq, AX.X, ALU.add))
                    for v in range(VPK):
                        rlink(nc.vector.tensor_tensor(fac[:, p, :, v], oss[:, :, v], inv2[:, p, 1, :], ALU.mult))
                    rlink(nc.vector.tensor_scalar(fac[:, p, :, :], fac[:, p, :, :], 1.0 / (P * P), RMS_EPS,
                                                  ALU.mult, ALU.add))
                    for v in range(VPK):
                        last = nc.vector.scalar_tensor_tensor(
                            out=fac2[:, :, v], in0=fac[:, p, :, v], scalar=float(P),
                            in1=ssq[:, p, 1, :], op0=ALU.mult, op1=ALU.mult)
                    last.then_inc(oss_ready, 1)
                    dve.wait_ge(fac_ready, n + 1)
                    for b in range(NB):
                        for c in range(2):
                            for v in range(VPK):
                                last = nc.vector.scalar_tensor_tensor(
                                    out=og[:, p, b, 2 * c + v, :], in0=o[:, p, b, c, v, :],
                                    scalar=fac[:, p, 2 * b + c, v:v + 1], in1=sz[:, p, 2 * b + c, v, :],
                                    op0=ALU.mult, op1=ALU.mult)
                        last.then_inc(og_ready, 1)

                for ct in range(4):
                    if ct == 2 and part is not MAIN:
                        normalise(h * 2 - 1, 1)
                    if part is not TAIL:
                        convolve(0, ct)
                for s in [s for s in part if s in dve_pos]:
                    kind, p, j = s[0], s[1], s[-1]
                    if kind == "norms":
                        convolve(1, 2 * p)
                        convolve(1, 2 * p + 1)
                    if kind == "gram":
                        dve.wait_ge(dtc_ready, h * (2 * NB) + (p * NB + j + 1))
                    dve.wait_ge(filled, full(h, ("lower5", p, j) if kind == "upper5" else s))
                    src, src4 = bank(s), bank4(s)
                    src8 = src[:, :].rearrange("p (n i t) -> p n i t", n=2 * UNITS, i=2)
                    if kind == "norms":
                        hlink(nc.vector.tensor_scalar(ssq[:, p, :, :], src[:, 0:2 * NT].rearrange("p (i t) -> p i t", i=2),
                                                      1e-6, None, ALU.add))
                        nc.vector.reciprocal(inv2[:, p, :, :], ssq[:, p, :, :]).then_inc(dve_emptied, 1)
                        dve.wait_ge(dve_emptied, dve_done(h, s))
                        for v in range(VPK):
                            last = nc.vector.scalar_tensor_tensor(
                                out=cneg[:, p, :, v], in0=inv2[:, p, 0, :], scalar=-1.0,
                                in1=beta[:, :, bass.ds(h * (2 * VPK) + (p * VPK + v), 1)].rearrange("p t a -> p (t a)"),
                                op0=ALU.mult, op1=ALU.mult)
                        last.then_inc(scale_ready, 1)
                        dve.wait_ge(root_ready, h * 2 + (p + 1))
                        hlink(nc.vector.tensor_scalar(ninvr[:, :], power[:, :], -1.0, None, ALU.mult))
                    elif kind == "vtok":
                        for t in range(2):
                            tile = 2 * j + t
                            last = nc.vector.tensor_scalar(nv[:, p, tile, :, :], src4[:, 2 * t:2 * t + 2, :],
                                                           ninvr[:, tile:tile + 1], None, ALU.mult)
                        last.then_inc(dve_emptied, 1)
                    elif kind == "gram":
                        gram = src[:, :].rearrange("p (c i t) -> p c i t", c=2, i=2)
                        dc = nB[:, p, j, :, :].rearrange("p (c v) t -> p c v t", c=2)
                        for i, dst in ((0, nA), (1, nB)):
                            last = nc.vector.tensor_tensor(
                                dst[:, p, j, :, :].rearrange("p (c v) t -> p c v t", c=2),
                                gram[:, :, i:i + 1, :].broadcast_to([P, 2, VPK, P]), dc, ALU.mult)
                        last.then_inc(dve_emptied, 1)
                        if (p, j) == (1, NB - 1):
                            dve.wait_ge(dve_emptied, dve_done(h, s))
                            invert_blocks()
                    elif kind in ("upper5", "lower5"):
                        m, at, to = (U, 0, Q) if kind == "upper5" else (T, Q, 0)
                        for i in range(2):
                            rows = slice(2 * Q * i + at, 2 * Q * i + at + Q)
                            last = nc.vector.tensor_copy(
                                m[rows, p, 2 * j:2 * j + 2, :, 2 * Q * i + to:2 * Q * i + to + Q].rearrange("p b u t -> p (b u) t"),
                                src8[rows, :, i, :])
                        last.then_inc(dve_emptied, 1)
                    elif kind == "upper6":
                        nc.vector.tensor_copy(
                            U[0:2 * Q, p, 2 * j:2 * j + 2, :, 2 * Q:].rearrange("p b u t -> p (b u) t"),
                            src[0:2 * Q, :].rearrange("p (n t) -> p n t", n=2 * UNITS)).then_inc(dve_emptied, 1)
                    elif kind == "kstate":
                        for i in range(2):
                            b = 2 * j + i
                            for v in range(VPK):
                                last = nc.vector.scalar_tensor_tensor(
                                    out=rhs2[:, b, v, :], in0=src4[:, 2 * i + v, :],
                                    scalar=decay0[:, 2 * b + 1, bass.ds(h * (2 * VPK) + (p * VPK + v), 1)],
                                    in1=nv[:, p, 2 * b + 1, v, :], op0=ALU.mult, op1=ALU.add)
                        last.then_inc(dve_emptied, 1)
                        if (p, j) == (1, 1):
                            normalise(h * 2, 0)
                    elif kind == "out2":
                        dve.wait_ge(act_emptied, act_done(h, ("qstate", p, j)))
                        nc.vector.tensor_tensor(o[:, p, 2 * j:2 * j + 2, 1, :, :],
                                                src[:, :].rearrange("p (b v d) -> p b v d", b=2, v=VPK),
                                                qs[:, 2 * j:2 * j + 2, :, :], ALU.add).then_inc(dve_emptied, 1)
                    elif kind == "final":
                        xb = x[:, 2 * j:2 * j + 2, :]
                        nc.vector.tensor_tensor(xb, src[:, :].rearrange("p (t d) -> p t d", t=2), xb,
                                                ALU.add).then_inc(dve_emptied, 1)
                assert hl[0] == (0 if part is TAIL else LINKS), hl

            steps_of(0, MAIN)
            with dve.Fori(1, PAIRS) as h:
                steps_of(h, STEPS)
            steps_of(PAIRS, TAIL)

        @block.gpsimd
        def _(pool):
            norm_pool(nc, pool, norm, minus_half)
            pool.wait_ge(padded, 10)
            pool.wait_ge(start_ready, 1)
            with pool.Fori(0, PAIRS) as h:
                def masked_gates(p, b):
                    if b >= 2:
                        pool.wait_ge(filled, full(h, ("decay", p, b - 2)))
                    gates = g[:, 2 * b:2 * b + 2, bass.ds(h * (2 * VPK) + p * VPK, VPK)].rearrange("p c (v a) -> p c v a", a=1)
                    nc.gpsimd.tensor_tensor(
                        mg[:, b % 2, :, :].rearrange("p (c v) t -> p c v t", c=2),
                        upto.rearrange("p (a b t) -> p a b t", a=1, b=1).broadcast_to([P, 2, VPK, P]),
                        gates.broadcast_to([P, 2, VPK, P]), ALU.mult).then_inc(mg_ready, 1)

                for p in range(2):
                    if p:
                        pool.wait_ge(filled, full(h, ("decay", 0, NB - 1)))
                    pool.wait_ge(padded, 10)
                    masked_gates(p, 0)
                    masked_gates(p, 1)
                    for i in range(2):
                        pool.wait_ge(silu_done, h * 8 + (4 * p + 4))
                        nc.gpsimd.tensor_tensor(sq[:, i, :, :], kq[:, p, :, i, :], kq[:, p, :, i, :],
                                                ALU.mult).then_inc(sq_done, 1)
                    if p:
                        nc.gpsimd.memset(blockT, 0.0).then_inc(cleared, 1)
                        pool.wait_ge(cleared, h + 1)
                        nc.gpsimd.tensor_tensor(tick[:, 0:1], ones[:, :], ones[:, :], ALU.mult)
                        nc.gpsimd.memset(lanes[:, Q * Q:2 * Q * Q:Q + 1], 1.0)
                        nc.gpsimd.memset(T[:, :, :, :, :], 0.0).then_inc(tu_ready, 1)
                    pool.wait_ge(dve_emptied, dve_done(h, ("norms", p)))
                    nc.gpsimd.tensor_tensor(power[:, :], ssq[:, p, 0, :], half[:, :], ALU.pow).then_inc(root_ready, 1)
                    pool.wait_ge(scale_ready, h * 2 + (p + 1))
                    for b in range(NB):
                        pool.wait_ge(act_emptied, act_done(h, ("decay", p, b)))
                        dc = nB[:, p, b, :, :].rearrange("p (c v) t -> p c v t", c=2)
                        nc.gpsimd.tensor_tensor(
                            dc, dc, cneg[:, p, 2 * b:2 * b + 2, :].rearrange("p c (v a) -> p c v a", a=1)
                            .broadcast_to([P, 2, VPK, P]), ALU.mult).then_inc(factored, 1)
                        pool.wait_ge(factored, h * (2 * NB) + (p * NB + b + 1))
                        nc.gpsimd.tensor_tensor(last_c[:, p, b, :], dc[:, 0, :, P - 1],
                                                ones[:, :].broadcast_to([P, VPK]), ALU.mult).then_inc(dtc_ready, 1)
                        if b + 2 < NB:
                            masked_gates(p, b + 2)
                nc.gpsimd.memset(U[:, :, :, :, :], 0.0).then_inc(tu_ready, 1)

                def weighted(p, j):
                    pool.wait_ge(act_emptied, act_done(h, ("solve1", p, j)))
                    for i in range(2):
                        b = 2 * j + i
                        last = nc.gpsimd.tensor_tensor(
                            fd[:, b, :, :], f[:, 0, b, :, :],
                            last_c[:, p, b, :].rearrange("p (v a) -> p v a", a=1).broadcast_to([P, VPK, P]), ALU.mult)
                    last.then_inc(fd_ready, 1)

                def squares(p):
                    pool.wait_ge(act_emptied, act_done(h, ("out1", p, 1)))
                    pool.wait_ge(dve_emptied, dve_done(h, ("out2", p, 1)))
                    oo = o[:, p, :, :, :, :].rearrange("p b c v d -> p (b c v) d")
                    nc.gpsimd.tensor_tensor(osq, oo, oo, ALU.mult).then_inc(osq_ready, 1)

                def roots(p):
                    pool.wait_ge(oss_ready, h * 2 + (p + 1))
                    nc.gpsimd.tensor_tensor(fac[:, p, :, :].rearrange("p t v -> p (t v)"),
                                            fac2[:, :, :].rearrange("p t v -> p (t v)"), minus_half2[:, :],
                                            ALU.pow).then_inc(fac_ready, 1)

                weighted(0, 0)
                weighted(0, 1)
                weighted(1, 0)
                weighted(1, 1)
                squares(0)
                roots(0)
                squares(1)
                roots(1)


NE, FF = 8, 512
SHARED = NE
FT = FF // P
SLOTS = NT + NE - 1
NS_COLS = 3 * NE + SLOTS + 1


def routing_constants():
    row = np.concatenate([NE - np.arange(NE), P * np.arange(NE), np.arange(SLOTS + 1), np.zeros(NE)])
    return np.broadcast_to(row.astype(np.float32), (P, NS_COLS)).copy()


def expert_layer(nc, consts, x, router_wT, gate_up, down, shared_gate, shared_up, shared_down, rconst,
                 slot_in, slot_out, banks):
    ident, upto, after, below, minus_half = consts
    gate_bank, up_bank, dn_bank = banks[0:2], banks[2:4], banks[6:8]
    small_bank, ht_bank = banks[4], banks[5]
    with ExitStack() as ctx:
        sb = lambda n, shape, dt=F32: ctx.enter_context(nc.sbuf_tensor("ex_" + n, shape, dt))
        sem = lambda n: ctx.enter_context(nc.semaphore("ex_" + n))
        norm = Norm(nc, ctx, "ex")
        w_gu = sb("w_gu", [P, NE + 1, KT, 2 * FF])
        w_dn = sb("w_dn", [P, NE + 1, FT, D])
        w_r = sb("w_r", [P, KT, NE])
        rc = sb("rc", [P, NS_COLS])
        ones = sb("ones", [P, P])
        zero = sb("zero", [P, D])
        logits = sb("logits", [P, NT, NE])
        best = sb("best", [P, NT])
        score = sb("score", [P, NT])
        key = sb("key", [P, NT, NE])
        first = sb("first", [P, NT])
        onehot = sb("onehot", [P, NT + 1, NE])
        rank = sb("rank", [P, NT + 1, NE])
        over = sb("over", [P, NE, NE])
        tiles = sb("tiles", [P, NE])
        ends = sb("ends", [P, NE])
        starts = sb("starts", [P, NE])
        place = sb("place", [P, NT, NE])
        slot_f = sb("slot_f", [P, NT])
        slot = sb("slot", [P, NT], I32)
        past = sb("past", [P, SLOTS + 1, NE])
        owner_f = sb("owner_f", [P, SLOTS + 1])
        owner = sb("owner", [P, SLOTS + 1], I32)
        xr = sb("xr", [P, NT, D])
        xs = sb("xs", [P, 2, D])
        xsT = sb("xsT", [P, 2, KT, P])
        sg = sb("sg", [P, 2, FF])
        hid = sb("hid", [P, 2, FF])
        hT = sb("hT", [P, FT, P])
        ys = sb("ys", [P, 2, D])
        yg = sb("yg", [P, NT, D])

        small_loaded, shared_loaded, experts_loaded = sem("small_loaded"), sem("shared_loaded"), sem("experts_loaded")
        zero_ready, zeroed, link = sem("zero_ready"), sem("zeroed"), sem("link")
        logits_done, best_ready, onehot_ready, ranks_done = [sem(n) for n in (
            "logits_done", "best_ready", "onehot_ready", "ranks_done")]
        score_ready, scaled, slot_ready, scattered, owner_ready = [sem(n) for n in (
            "score_ready", "scaled", "slot_ready", "scattered", "owner_ready")]
        xt_filled, xt_stored = sem("xt_filled"), sem("xt_stored")
        xs_loaded = [sem(f"xs{i}_loaded") for i in range(2)]
        out_stored = [sem(f"out{i}_stored") for i in range(2)]
        gate_filled, up_filled, silu_ready, hid_ready = [sem(n) for n in (
            "gate_filled", "up_filled", "silu_ready", "hid_ready")]
        ht_filled, ht_stored, dn_filled, dn_stored, gathered = [sem(n) for n in (
            "ht_filled", "ht_stored", "dn_filled", "dn_stored", "gathered")]
        block = ctx.enter_context(nc.Block())

        @block.sync
        def _(sync):
            sync.dma_start(w_r[:, :, :], router_wT.rearrange("(k p) e -> p k e", p=P)).then_inc(small_loaded, 16)
            sync.dma_start(rc[:, :], rconst).then_inc(small_loaded, 16)
            sync.dma_start(w_gu[:, SHARED, :, 0:FF], shared_gate.rearrange("(k p) f -> p k f", p=P)).then_inc(shared_loaded, 16)
            sync.dma_start(w_gu[:, SHARED, :, FF:], shared_up.rearrange("(k p) f -> p k f", p=P)).then_inc(shared_loaded, 16)
            sync.dma_start(w_dn[:, SHARED, :, :], shared_down.rearrange("(k p) d -> p k d", p=P)).then_inc(shared_loaded, 16)
            sync.wait_ge(zero_ready, 1)
            sync.dma_start(slot_in.rearrange("(s p) d -> p s d", p=P),
                           zero[:, :].rearrange("p (a d) -> p a d", a=1).broadcast_to([P, SLOTS + 1, D])).then_inc(zeroed, 16)
            for e in range(NE):
                sync.dma_start(w_gu[:, e, :, :], gate_up[e].rearrange("(k p) f -> p k f", p=P)).then_inc(experts_loaded, 16)
                sync.dma_start(w_dn[:, e, :, :], down[e].rearrange("(k p) d -> p k d", p=P)).then_inc(experts_loaded, 16)
            sync.wait_ge(scattered, NT * 16)
            for r in range(2):
                sync.dma_start(xs[:, r, :], slot_in[r * P:(r + 1) * P, :]).then_inc(xs_loaded[r], 16)

            def store(r, par):
                sync.wait_ge(dn_stored, r + (NT + 1))
                sync.dma_start(slot_out[bass.ds(r * P, P), :] if not isinstance(r, int) else slot_out[r * P:(r + 1) * P, :],
                               ys[:, par, :]).then_inc(out_stored[par], 16)

            with sync.Fori(0, SLOTS // 2) as j:
                for par in range(2):
                    sync.wait_ge(xt_filled, j * 2 + (par + 1))
                    sync.dma_start(xs[:, par, :], slot_in[bass.ds(j * (2 * P) + (par + 2) * P, P), :]).then_inc(xs_loaded[par], 16)
                    store(j * 2 + par, par)
            store(SLOTS - 1, 0)
            for par in range(2):
                sync.wait_ge(out_stored[par], 16 * ((SLOTS + 1 - par) // 2))
                sync.wait_ge(xs_loaded[par], 16 * (SLOTS + 1) // 2)

        @block.tensor
        def _(pe):
            norm_tensor(nc, pe, norm, banks, ident)
            pe.wait_ge(norm.stored, NT // 2)
            pe.wait_ge(small_loaded, 32)
            for t in range(NT):
                for k in range(KT):
                    last = nc.tensor.matmul(small_bank[:, t * NE:(t + 1) * NE], norm.xnT[:, k, t * P:(t + 1) * P],
                                            w_r[:, k, :], start=(k == 0), stop=(k == KT - 1))
            last.then_inc(logits_done, 1)

            def gate_up_of(n, par, lhs, weights):
                for sem_, emptied, bank, at in ((gate_filled, silu_ready, gate_bank, 0), (up_filled, hid_ready, up_bank, FF)):
                    if not isinstance(n, int) or n >= 2:
                        pe.wait_ge(emptied, n - 1)
                    for k in range(KT):
                        last = nc.tensor.matmul(bank[par][:, :], lhs(k), weights(k, at), start=(k == 0), stop=(k == KT - 1))
                    last.then_inc(sem_, 1)

            def down_of(n, par, weights):
                pe.wait_ge(hid_ready, n + 1)
                if not isinstance(n, int) or n >= 1:
                    pe.wait_ge(ht_stored, n)
                for c in range(FT):
                    last = nc.tensor.transpose(ht_bank[:, c * P:(c + 1) * P], hid[:, par, c * P:(c + 1) * P], ident)
                last.then_inc(ht_filled, 1)
                pe.wait_ge(ht_stored, n + 1)
                if not isinstance(n, int) or n >= 2:
                    pe.wait_ge(dn_stored, n - 1)
                for c in range(FT):
                    last = nc.tensor.matmul(dn_bank[par][:, 0:D], hT[:, c, :], weights(c), start=(c == 0), stop=(c == FT - 1))
                last.then_inc(dn_filled, 1)

            def shared_gate_up(n):
                gate_up_of(n, n % 2, lambda k: norm.xnT[:, k, n * P:(n + 1) * P],
                           lambda k, at: w_gu[:, SHARED, k, at:at + FF])

            def shared_down_of(n):
                down_of(n, n % 2, lambda c: w_dn[:, SHARED, c, :])

            pe.wait_ge(shared_loaded, 48)
            shared_gate_up(0)
            for n in range(1, NT):
                shared_gate_up(n)
                shared_down_of(n - 1)
                if n == 3:
                    pe.wait_ge(onehot_ready, 1)
                    nc.tensor.matmul(small_bank[:, 0:(NT + 1) * NE], upto,
                                     onehot[:, :, :].rearrange("p t e -> p (t e)"), start=True, stop=False)
                    for t in range(NT):
                        last = nc.tensor.matmul(
                            small_bank[:, (t + 1) * NE:(NT + 1) * NE].rearrange("p (t e) -> p t e", e=NE), ones[:, :],
                            onehot[:, t:t + 1, :].broadcast_to([P, NT - t, NE]), start=False, stop=(t == NT - 1))
                    last.then_inc(ranks_done, 1)
            shared_down_of(NT - 1)

            pe.wait_ge(owner_ready, 1)
            pe.wait_ge(experts_loaded, 32 * NE)

            def turn_tokens(r, par, loads):
                pe.wait_ge(xs_loaded[par], loads * 16)
                if isinstance(r, int):
                    pe.wait_ge(slot_ready, 1)
                else:
                    pe.wait_ge(xt_stored, r)
                for k in range(KT):
                    last = nc.tensor.transpose(small_bank[:, k * P:(k + 1) * P], xs[:, par, k * P:(k + 1) * P], ident)
                last.then_inc(xt_filled, 1)
                pe.wait_ge(xt_stored, r + 1)

            def expert_of(r):
                at = slice(r, r + 1) if isinstance(r, int) else bass.ds(r, 1)
                return pe.value_load(owner[0:1, at], min_val=0, max_val=NE - 1)

            def routed_gate_up(r, par, loads):
                e = expert_of(r)
                turn_tokens(r, par, loads)
                gate_up_of(r + NT, par, lambda k: xsT[:, par, k, :],
                           lambda k, at: w_gu[:, bass.ds(e, 1), k, at:at + FF].rearrange("p a f -> p (a f)"))

            def routed_down(r, par):
                e = expert_of(r)
                down_of(r + NT, par, lambda c: w_dn[:, bass.ds(e, 1), c, :].rearrange("p a d -> p (a d)"))

            routed_gate_up(0, 0, 1)
            with pe.Fori(0, SLOTS // 2) as j:
                routed_gate_up(j * 2 + 1, 1, j + 1)
                routed_down(j * 2, 0)
                routed_gate_up(j * 2 + 2, 0, j + 2)
                routed_down(j * 2 + 1, 1)
            routed_down(SLOTS - 1, 0)

        @block.scalar
        def _(act):
            norm_scalar(nc, act, norm, banks)

            def silu_of(n, par):
                act.wait_ge(gate_filled, n + 1)
                if not isinstance(n, int) or n >= 2:
                    act.wait_ge(hid_ready, n - 1)
                nc.scalar.activation(sg[:, par, :], gate_bank[par][:, :], ACT.Silu).then_inc(silu_ready, 1)

            def store_ht(n):
                act.wait_ge(ht_filled, n + 1)
                if not isinstance(n, int) or n >= 1:
                    act.wait_ge(dn_filled, n)
                nc.scalar.copy(hT[:, :, :].rearrange("p c t -> p (c t)"), ht_bank[:, :]).then_inc(ht_stored, 1)

            silu_of(0, 0)
            for n in range(1, NT):
                silu_of(n, n % 2)
                store_ht(n - 1)
                if n == 2:
                    act.wait_ge(best_ready, 1)
                    nc.scalar.activation(score[:, :], best[:, :], ACT.Sigmoid).then_inc(score_ready, 1)
            store_ht(NT - 1)

            def store_xt(r, par):
                act.wait_ge(xt_filled, r + 1)
                act.wait_ge(up_filled, r + (NT - 1))
                nc.scalar.copy(xsT[:, par, :, :].rearrange("p k t -> p (k t)"), small_bank[:, 0:D]).then_inc(xt_stored, 1)

            store_xt(0, 0)
            silu_of(NT, 0)
            with act.Fori(0, SLOTS // 2) as j:
                store_xt(j * 2 + 1, 1)
                silu_of(j * 2 + (NT + 1), 1)
                store_ht(j * 2 + NT)
                store_xt(j * 2 + 2, 0)
                silu_of(j * 2 + (NT + 2), 0)
                store_ht(j * 2 + (NT + 1))
            store_ht(SLOTS - 1 + NT)

        @block.vector
        def _(dve):
            nc.vector.memset(zero[:, :], 0.0).then_inc(zero_ready, 1)
            nc.vector.memset(ones[:, :], 1.0)
            nc.vector.memset(onehot[:, NT, :], 0.0)
            norm_vector(nc, dve, norm, x)
            links = [0]

            def chain(ins):
                links[0] += 1
                ins.then_inc(link, 1)
                dve.wait_ge(link, links[0])

            def per_tile(m):
                return m[:, :].rearrange("p (t a) -> p t a", a=1).broadcast_to([P, NT, NE])

            def per_expert(m, n=NT):
                return m.rearrange("p (a e) -> p a e", a=1).broadcast_to([P, n, NE])

            dve.wait_ge(logits_done, 1)
            dve.wait_ge(small_loaded, 32)
            chain(nc.vector.tensor_copy(logits[:, :, :].rearrange("p t e -> p (t e)"), small_bank[:, 0:NT * NE]))
            nc.vector.tensor_reduce(best[:, :], logits[:, :, :], AX.X, ALU.max).then_inc(best_ready, 1)
            dve.wait_ge(best_ready, 1)
            chain(nc.vector.tensor_tensor(key[:, :, :], logits[:, :, :], per_tile(best), ALU.is_equal))
            chain(nc.vector.tensor_tensor(key[:, :, :], key[:, :, :], per_expert(rc[:, 0:NE]), ALU.mult))
            chain(nc.vector.tensor_reduce(first[:, :], key[:, :, :], AX.X, ALU.max))
            nc.vector.tensor_tensor(onehot[:, 0:NT, :], key[:, :, :], per_tile(first), ALU.is_equal).then_inc(onehot_ready, 1)

            def hidden_of(n, par):
                dve.wait_ge(up_filled, n + 1)
                dve.wait_ge(silu_ready, n + 1)
                if not isinstance(n, int) or n >= 2:
                    dve.wait_ge(ht_filled, n - 1)
                nc.vector.tensor_tensor(hid[:, par, :], up_bank[par][:, :], sg[:, par, :], ALU.mult).then_inc(hid_ready, 1)

            def add_shared(n):
                dve.wait_ge(dn_filled, n + 1)
                nc.vector.tensor_tensor(x[:, n, :], dn_bank[n % 2][:, 0:D], x[:, n, :], ALU.add).then_inc(dn_stored, 1)

            hidden_of(0, 0)
            for n in range(1, NT):
                hidden_of(n, n % 2)
                add_shared(n - 1)
                if n == 3:
                    dve.wait_ge(ranks_done, 1)
                    chain(nc.vector.tensor_copy(rank[:, :, :].rearrange("p t e -> p (t e)"), small_bank[:, 0:(NT + 1) * NE]))
                    chain(nc.vector.tensor_tensor(
                        over[:, :, :], rank[:, NT, :].rearrange("p (e a) -> p e a", a=1).broadcast_to([P, NE, NE]),
                        per_expert(rc[:, NE:2 * NE], NE), ALU.is_gt))
                    chain(nc.vector.tensor_reduce(tiles[:, :], over[:, :, :], AX.X, ALU.add))
                    chain(nc.vector.tensor_tensor_scan(ends[:, :], ones[:, 0:NE], tiles[:, :], 0.0, ALU.mult, ALU.add))
                    chain(nc.vector.tensor_tensor(starts[:, :], ends[:, :], tiles[:, :], ALU.subtract))
                    chain(nc.vector.tensor_scalar(starts[:, :], starts[:, :], float(P), -1.0, ALU.mult, ALU.add))
                    chain(nc.vector.tensor_tensor(place[:, :, :], rank[:, 0:NT, :], per_expert(starts[:, :]), ALU.add))
                    chain(nc.vector.tensor_tensor(place[:, :, :], place[:, :, :], onehot[:, 0:NT, :], ALU.mult))
                    chain(nc.vector.tensor_reduce(slot_f[:, :], place[:, :, :], AX.X, ALU.add))
                    nc.vector.tensor_copy(slot[:, :], slot_f[:, :]).then_inc(slot_ready, 1)
                    chain(nc.vector.tensor_tensor(
                        past[:, :, :], per_expert(ends[:, :], SLOTS + 1),
                        rc[:, 2 * NE:2 * NE + SLOTS + 1].rearrange("p (s a) -> p s a", a=1).broadcast_to([P, SLOTS + 1, NE]),
                        ALU.is_le))
                    chain(nc.vector.tensor_reduce(owner_f[:, :], past[:, :, :], AX.X, ALU.add))
                    chain(nc.vector.tensor_scalar(owner_f[:, :], owner_f[:, :], float(NE - 1), None, ALU.min))
                    nc.vector.tensor_copy(owner[:, :], owner_f[:, :]).then_inc(owner_ready, 1)
            add_shared(NT - 1)

            def store_down(n, par, stores):
                dve.wait_ge(dn_filled, n + 1)
                if not isinstance(stores, int) or stores:
                    dve.wait_ge(out_stored[par], stores * 16)
                nc.vector.tensor_copy(ys[:, par, :], dn_bank[par][:, 0:D]).then_inc(dn_stored, 1)

            hidden_of(NT, 0)
            hidden_of(NT + 1, 1)
            store_down(NT, 0, 0)
            hidden_of(NT + 2, 0)
            store_down(NT + 1, 1, 0)
            with dve.Fori(1, SLOTS // 2) as j:
                hidden_of(j * 2 + (NT + 1), 1)
                store_down(j * 2 + NT, 0, j)
                hidden_of(j * 2 + (NT + 2), 0)
                store_down(j * 2 + (NT + 1), 1, j)
            store_down(SLOTS - 1 + NT, 0, SLOTS // 2)
            dve.wait_ge(gathered, 16 * NT)
            for t in range(NT):
                nc.vector.tensor_tensor(x[:, t, :], x[:, t, :], yg[:, t, :], ALU.add)

        @block.gpsimd
        def _(pool):
            norm_pool(nc, pool, norm, minus_half)
            pool.wait_ge(score_ready, 1)
            pool.wait_ge(norm.normed, NT)
            nc.gpsimd.tensor_tensor(xr[:, :, :], norm.xn[:, :, :],
                                    score[:, :].rearrange("p (t a) -> p t a", a=1).broadcast_to([P, NT, D]),
                                    ALU.mult).then_inc(scaled, 1)
            pool.wait_ge(scaled, 1)
            pool.wait_ge(slot_ready, 1)
            pool.wait_ge(zeroed, 16)
            for t in range(NT):
                pool.indirect_dma_start(out=slot_in, out_offset=bass.IndirectOffsetOnAxis(slot[:, t:t + 1], 0),
                                        in_=xr[:, t, :], in_offset=None).then_inc(scattered, 16)
            for par in range(2):
                pool.wait_ge(out_stored[par], 16 * ((SLOTS + 1 - par) // 2))
            for t in range(NT):
                pool.indirect_dma_start(out=yg[:, t, :], out_offset=None, in_=slot_out,
                                        in_offset=bass.IndirectOffsetOnAxis(slot[:, t:t + 1], 0)).then_inc(gathered, 16)


HEADS, HD = 16, 16
GROUP = 4
ROUNDS = HEADS // GROUP
PAIR = S + P
LORA = 16
FFN1 = 1024
NEVER = -1e30


def score_bias(slopes):
    p, j = np.arange(P)[:, None], np.arange(S)[None, :]
    diff = np.concatenate([j - P - p, (j - p)[:, :P]], axis=1)
    rows = [np.where(diff <= 0, np.float32(4) * np.float32(m) * diff.astype(np.float32), NEVER) for m in slopes]
    return np.concatenate(rows, axis=1).astype(np.float32)


def alibi_slopes():
    start = 2.0 ** (-2.0 ** (-(np.log2(HEADS) - 3.0)))
    return [start ** (i + 1) for i in range(HEADS)]


def attention_steps(kv_tiles, last_steps):
    chains = []
    for c in range(2):
        chain = [[("q", c, 0), ("q", c, 1)] + [("k", c, i) for i in range((kv_tiles + 1) // 2)],
                 [("qk", c, 0, g) for g in range(GROUP)]]
        chain.append([("qk", c, 1, g) for g in range(GROUP)])
        for r in range(ROUNDS):
            later = [("qk", c, r + 2, g) for g in range(GROUP)] if r + 2 < ROUNDS else []
            chain += [[("pt", c, r, i) for i in range(3)], [("pv", c, r)] + later]
        chains.append(chain + [[("ot", c)]] + [[(kind, c)] for kind in last_steps])
    return [s for turn in zip(*chains) for part in turn for s in part]


def attention_layer(nc, consts, x, weights, bias_const, banks, modulated):
    ident, upto, after, below, minus_half = consts
    KVT = ROUNDS if modulated else 1
    KVH = HEADS if modulated else GROUP
    tag = "mo" if modulated else "al"
    last_steps = ["proj", "tanh", "ha"] if modulated else ["wo"]
    STEPS = attention_steps(KVT, last_steps)
    BY_DVE = {"qk", "pv", "wo", "ha"}
    by_act = lambda s: s[0] not in BY_DVE and not (s[0] == "pt" and s[3] == 2)
    pos = {s: i for i, s in enumerate(STEPS)}
    act_steps = [s for s in STEPS if by_act(s)]
    dve_steps = [s for s in STEPS if not by_act(s)]
    act_pos = {s: i for i, s in enumerate(act_steps)}
    dve_pos = {s: i for i, s in enumerate(dve_steps)}
    NSTEP, NA, ND = len(STEPS), len(act_steps), len(dve_steps)
    NBANK = len(banks)
    rounds = {s[1:3]: i for i, s in enumerate(s for s in STEPS if s[0] == "pt" and s[3] == 0)}
    NR = len(rounds)
    NBIAS = 1 if modulated else HEADS

    with ExitStack() as ctx:
        sb = lambda n, shape, dt=F32: ctx.enter_context(nc.sbuf_tensor(f"{tag}_{n}", shape, dt))
        sem = lambda n: ctx.enter_context(nc.semaphore(f"{tag}_{n}"))
        norm = Norm(nc, ctx, tag)
        w_q = sb("w_q", [P, KT, HEADS, 32])
        w_k = sb("w_k", [P, KT, KVT * GROUP, 32])
        raw_q = sb("raw_q", [P, KT, HEADS * HD])
        raw_k = sb("raw_k", [P, KT, KVT * GROUP * HD])
        w_v = sb("w_v", [P, KT, KVH * HD])
        w_o = sb("w_o", [P, KT, D])
        bias = sb("bias", [P, NBIAS, PAIR])
        vp = sb("vp", [P, NT, KVH, HD + 1])
        qT = sb("qT", [P, 2, ROUNDS, GROUP, S])
        kT = sb("kT", [P, 2, KVT, S])
        sc = sb("sc", [P, 2, 2, GROUP, PAIR])
        top = sb("top", [P, 2, 2, 2, GROUP])
        pT = sb("pT", [P, 2, 3, GROUP, P])
        rec = sb("rec", [P, 2, ROUNDS, 2, GROUP])
        att = sb("att", [P, 2, 2, HEADS, HD])
        tick = sb("tick", [1, 2 * HEADS])
        attT = sb("attT", [P, 2, KT, S])
        if modulated:
            gain1, gain2 = sb("gain1", [P, KT]), sb("gain2", [P, KT])
            ms = sb("ms", [P, NT])
            rms = sb("rms", [P, NT])
            xr = sb("xr", [P, NT, D])
            hT = sb("hT", [P, KT, TOK])
            w_a = sb("w_a", [P, KT, LORA])
            w_b = sb("w_b", [LORA, FFN1])
            projT = sb("projT", [P, 2, KT, S])
            tanhT = sb("tanhT", [LORA, 2, S])
            modT = sb("modT", [LORA, TOK])
            w_in, w_up = sb("w_in", [P, KT, FFN1]), sb("w_up", [P, KT, FFN1])
            w_dn = sb("w_dn", [P, FFN1 // P, D])
            sg, hid = sb("sg", [P, 2, FF]), sb("hid", [P, 2, FF])
            hidT = sb("hidT", [P, FT, P])
            ms_ready, rms_ready, xr_ready = [sem(n) for n in ("ms_ready", "rms_ready", "xr_ready")]
            gate_filled, up_filled, silu_ready, hid_ready = [sem(n) for n in (
                "gate_filled", "up_filled", "silu_ready", "hid_ready")]
            ht_filled, ht_stored, dn_filled, dn_stored = [sem(n) for n in (
                "ht_filled", "ht_stored", "dn_filled", "dn_stored")]
        else:
            bo = sb("bo", [1, D])
            ones_row = sb("ones_row", [1, P])
        loaded, mlp_loaded, padded, w_ready = sem("loaded"), sem("mlp_loaded"), sem("padded"), sem("w_ready")
        v_filled, v_stored = sem("v_filled"), sem("v_stored")
        filled, act_emptied, dve_emptied = sem("filled"), sem("act_emptied"), sem("dve_emptied")
        shifted, exp_ready, rec_ready = sem("shifted"), sem("exp_ready"), sem("rec_ready")
        NLOAD = 11 if modulated else 7
        block = ctx.enter_context(nc.Block())

        full = lambda b, s: NSTEP * b + (pos[s] + 1)
        act_done = lambda b, s: NA * b + (NA + act_pos[s] + 1)
        dve_done = lambda b, s: ND * b + (ND + dve_pos[s] + 1)
        bank = lambda s: banks[pos[s] % NBANK]

        def mlp_tensor(pe):
            def gate_and_up(n):
                t, c = n // 2, n % 2
                tok, cols = slice(t * P, (t + 1) * P), slice(c * FF, (c + 1) * FF)
                if n >= 2:
                    pe.wait_ge(silu_ready, n - 1)
                for k in range(KT):
                    nc.tensor.matmul(banks[c][:, :], hT[:, k, tok], w_in[:, k, cols], start=(k == 0), stop=False)
                nc.tensor.matmul(banks[c][:, :], modT[:, tok], w_b[:, cols], start=False, stop=True).then_inc(gate_filled, 1)
                if n >= 2:
                    pe.wait_ge(hid_ready, n - 1)
                for k in range(KT):
                    last = nc.tensor.matmul(banks[2 + c][:, :], hT[:, k, tok], w_up[:, k, cols],
                                            start=(k == 0), stop=(k == KT - 1))
                last.then_inc(up_filled, 1)

            def down(n):
                pe.wait_ge(hid_ready, n + 1)
                if n:
                    pe.wait_ge(ht_stored, n)
                for c in range(FT):
                    last = nc.tensor.transpose(banks[5][:, c * P:(c + 1) * P], hid[:, n % 2, c * P:(c + 1) * P], ident)
                last.then_inc(ht_filled, 1)
                pe.wait_ge(ht_stored, n + 1)
                if n >= 2:
                    pe.wait_ge(dn_stored, n - 1)
                for c in range(FT):
                    last = nc.tensor.matmul(banks[6 + n % 2][:, 0:D], hidT[:, c, :], w_dn[:, (n % 2) * FT + c, :],
                                            start=(c == 0), stop=(c == FT - 1))
                last.then_inc(dn_filled, 1)

            gate_and_up(0)
            for n in range(1, 2 * NT):
                gate_and_up(n)
                down(n - 1)
            down(2 * NT - 1)

        @block.sync
        def _(sync):
            sync.dma_start(raw_q[:, :, :], weights["Wq"].rearrange("(k p) n -> p k n", p=P)).then_inc(loaded, 16)
            sync.dma_start(raw_k[:, :, :], weights["Wk"].rearrange("(k p) n -> p k n", p=P)).then_inc(loaded, 16)
            sync.dma_start(w_v[:, :, :], weights["Wv"].rearrange("(k p) n -> p k n", p=P)).then_inc(loaded, 16)
            sync.dma_start(w_o[:, :, :], weights["Wo"].rearrange("(k p) n -> p k n", p=P)).then_inc(loaded, 16)
            sync.dma_start(bias[:, :, :].rearrange("p h j -> p (h j)"), bias_const).then_inc(loaded, 16)
            if modulated:
                for k in range(KT):
                    sync.dma_start(gain1[:, k:k + 1], weights["ln1"][k * P:(k + 1) * P].rearrange("(p a) -> p a", a=1)).then_inc(loaded, 16)
                for k in range(KT):
                    sync.dma_start(gain2[:, k:k + 1], weights["ln2"][k * P:(k + 1) * P].rearrange("(p a) -> p a", a=1)).then_inc(loaded, 16)
                sync.dma_start(w_a[:, :, :], weights["A"].rearrange("(k p) r -> p k r", p=P)).then_inc(loaded, 16)
                sync.dma_start(w_b[:, :], weights["B"]).then_inc(loaded, 16)
                sync.dma_start(w_in[:, :, :], weights["W_in"].rearrange("(k p) n -> p k n", p=P)).then_inc(mlp_loaded, 16)
                sync.dma_start(w_up[:, :, :], weights["W_up"].rearrange("(k p) n -> p k n", p=P)).then_inc(mlp_loaded, 16)
                sync.dma_start(w_dn[:, :, :], weights["W_down"].rearrange("(k p) n -> p k n", p=P)).then_inc(mlp_loaded, 16)
            else:
                sync.dma_start(bo[:, :], weights["bo"].rearrange("(a d) -> a d", a=1)).then_inc(loaded, 16)
                sync.dma_start(ones_row[:, :], weights["ones"][0:1, 0:P]).then_inc(loaded, 16)

        @block.tensor
        def _(pe):
            if modulated:
                norm_tensor(nc, pe, norm, banks, ident, src=xr, ready=xr_ready)
            else:
                norm_tensor(nc, pe, norm, banks, ident)
            pe.wait_ge(norm.stored, NT // 2)
            pe.wait_ge(loaded, 16 * NLOAD)
            for j in range(NT // 2):
                for t in range(2):
                    for k in range(KT):
                        last = nc.tensor.matmul(banks[4 + j][:, t * KVH * HD:(t + 1) * KVH * HD],
                                                norm.xnT[:, k, (2 * j + t) * P:(2 * j + t + 1) * P], w_v[:, k, :],
                                                start=(k == 0), stop=(k == KT - 1))
                last.then_inc(v_filled, 1)
            pe.wait_ge(v_stored, NT // 2)
            pe.wait_ge(padded, 5)
            pe.wait_ge(w_ready, 2)

            with pe.Fori(0, NB // 2) as b:
                def sources(s):
                    kind, c = s[0:2]
                    if kind == "qk":
                        return [("k", c, (KVT + 1) // 2 - 1)]
                    return {"pv": [("pt", c, s[2] , 1), ("pt", c, s[2], 2)] if kind == "pv" else [],
                            "ot": [("pv", c, ROUNDS - 1)], "wo": [("ot", c)], "proj": [("ot", c)],
                            "tanh": [("proj", c)]}.get(kind, [])

                def begin(s):
                    earlier = [q for q in STEPS[:pos[s]] if bank(q) is bank(s)]
                    before = (earlier or [q for q in STEPS if bank(q) is bank(s)])[-1]
                    mine = ([before] if earlier else []) + sources(s)
                    for emptied, order, count in ((act_emptied, act_pos, NA), (dve_emptied, dve_pos, ND)):
                        this = [order[q] for q in mine if q in order]
                        if this:
                            pe.wait_ge(emptied, count * b + (count + max(this) + 1))
                        elif not earlier and before in order:
                            pe.wait_ge(emptied, count * b + (order[before] + 1))

                for s in STEPS:
                    kind, c, out = s[0], s[1], bank(s)
                    begin(s)
                    tokens = bass.ds(b * (2 * S) + c * S, S)
                    if kind in ("q", "k"):
                        w, tiles = (w_q, ROUNDS) if kind == "q" else (w_k, KVT)
                        for i in range(2 * s[2], min(2 * s[2] + 2, tiles)):
                            for k in range(KT):
                                last = nc.tensor.matmul(
                                    out[:, (i % 2) * S:(i % 2 + 1) * S],
                                    w[:, k, i * GROUP:(i + 1) * GROUP, :].rearrange("p h c -> p (h c)"),
                                    norm.xnT[:, k, tokens], start=(k == 0), stop=(k == KT - 1))
                    elif kind == "qk":
                        _, _, r, g = s
                        rk = r if modulated else 0
                        nc.tensor.matmul(out[:, 0:S], qT[:, c, r, g, P:S], kT[:, c, rk, 0:S], start=True, stop=True)
                        last = nc.tensor.matmul(out[:, S:PAIR], qT[:, c, r, g, 0:P], kT[:, c, rk, 0:P], start=True, stop=True)
                    elif kind == "pt":
                        _, _, r, i = s
                        pe.wait_ge(exp_ready, b * NR + (rounds[c, r] + 1))
                        for g in range(GROUP):
                            last = nc.tensor.transpose(out[:, g * P:(g + 1) * P], sc[:, c, r % 2, g, i * P:(i + 1) * P], ident)
                    elif kind == "pv":
                        _, _, r = s
                        for tile, parts in ((0, [(2, 0)]), (1, [(0, 0), (1, 1)])):
                            for g in range(GROUP):
                                kv = r * GROUP + g if modulated else g
                                at = (tile * GROUP + g) * (HD + 1)
                                for i, (part, src) in enumerate(parts):
                                    last = nc.tensor.matmul(
                                        out[:, at:at + HD + 1], pT[:, c, part, g, :],
                                        vp[:, bass.ds(b * 4 + (2 * c + src), 1), kv, :].rearrange("p a c -> p (a c)"),
                                        start=(i == 0), stop=(i == len(parts) - 1))
                    elif kind == "ot":
                        flat = att[:, c, :, :, :].rearrange("p t h c -> p t (h c)")
                        for k in range(KT):
                            for t in range(2):
                                last = nc.tensor.transpose(out[:, (k * 2 + t) * P:(k * 2 + t + 1) * P],
                                                           flat[:, t, k * P:(k + 1) * P], ident)
                    elif kind == "wo":
                        for t in range(2):
                            for k in range(KT):
                                nc.tensor.matmul(out[:, t * D:(t + 1) * D], attT[:, c, k, t * P:(t + 1) * P], w_o[:, k, :],
                                                 start=(k == 0), stop=False)
                            last = nc.tensor.matmul(out[:, t * D:(t + 1) * D], ones_row[:, :], bo[:, :],
                                                    start=False, stop=True)
                    elif kind == "proj":
                        for m in range(KT):
                            for k in range(KT):
                                last = nc.tensor.matmul(out[:, m * S:(m + 1) * S], w_o[:, k, m * P:(m + 1) * P],
                                                        attT[:, c, k, :], start=(k == 0), stop=(k == KT - 1))
                    elif kind in ("tanh", "ha"):
                        for k in range(KT):
                            last = nc.tensor.matmul(out[0:LORA, 0:S], w_a[:, k, :],
                                                    projT[:, c, k, :] if kind == "tanh" else hT[:, k, tokens],
                                                    start=(k == 0), stop=(k == KT - 1))
                    last.then_inc(filled, 1)
            if modulated:
                pe.wait_ge(dve_emptied, ND * (NB // 2 + 1))
                pe.wait_ge(act_emptied, NA * (NB // 2 + 1))
                pe.wait_ge(mlp_loaded, 48)
                mlp_tensor(pe)

        @block.scalar
        def _(act):
            act.nop().then_inc(act_emptied, NA)
            if modulated:
                act.wait_ge(loaded, 16 * NLOAD)
                for j in range(NT // 2):
                    act.wait_ge(norm.turned, j + 1)
                    for k in range(KT):
                        src = banks[j][:, k * 2 * P:(k + 1) * 2 * P]
                        nc.scalar.mul(norm.xnT[:, k, 2 * j * P:(2 * j + 2) * P], src, gain1[:, k:k + 1])
                        last = nc.scalar.mul(hT[:, k, 2 * j * P:(2 * j + 2) * P], src, gain2[:, k:k + 1])
                    last.then_inc(norm.stored, 1)
            else:
                norm_scalar(nc, act, norm, banks)
            act.wait_ge(loaded, 16 * NLOAD)
            for raw, w in ((raw_q, w_q), (raw_k, w_k)):
                nc.scalar.copy(w[:, :, :, 0:HD], raw[:, :, :].rearrange("p k (h c) -> p k h c", c=HD)).then_inc(w_ready, 1)
            act.wait_ge(padded, 5)
            for j in range(NT // 2):
                act.wait_ge(v_filled, j + 1)
                nc.scalar.copy(vp[:, 2 * j:2 * j + 2, :, 0:HD],
                               banks[4 + j][:, 0:2 * KVH * HD].rearrange("p (t h c) -> p t h c", t=2, c=HD)).then_inc(v_stored, 1)
            with act.Fori(0, NB // 2) as b:
                def exponentials(c, r):
                    act.wait_ge(shifted, b * NR + (rounds[c, r] + 1))
                    flat = sc[:, c, r % 2, :, :].rearrange("p g j -> p (g j)")
                    nc.scalar.activation(flat, flat, ACT.Exp).then_inc(exp_ready, 1)

                for s in act_steps:
                    kind, c, src = s[0], s[1], bank(s)
                    if kind == "pt" and s[3] == 0:
                        exponentials(c, s[2])
                    act.wait_ge(filled, full(b, s))
                    if kind in ("q", "k"):
                        tiles = ROUNDS if kind == "q" else KVT
                        n, at = min(2, tiles - 2 * s[2]), 2 * s[2]
                        two = src[:, 0:n * S].rearrange("p (r t) -> p r t", r=n)
                        if kind == "q":
                            for g in range(GROUP):
                                rows = slice(32 * g, 32 * g + 32)
                                last = nc.scalar.copy(qT[rows, c, at:at + n, g, :], two[rows])
                        else:
                            last = nc.scalar.copy(kT[:, c, at:at + n, :], two)
                        last.then_inc(act_emptied, 1)
                    elif kind == "pt":
                        nc.scalar.copy(pT[:, c, s[3], :, :].rearrange("p g t -> p (g t)"), src[:, :]).then_inc(act_emptied, 1)
                    elif kind == "ot":
                        nc.scalar.copy(attT[:, c, :, :].rearrange("p k t -> p (k t)"), src[:, :]).then_inc(act_emptied, 1)
                    elif kind == "proj":
                        nc.scalar.copy(projT[:, c, :, :].rearrange("p k t -> p (k t)"), src[:, :]).then_inc(act_emptied, 1)
                    elif kind == "tanh":
                        nc.scalar.activation(tanhT[:, c, :], src[0:LORA, 0:S], ACT.Tanh).then_inc(act_emptied, 1)
            if modulated:
                for n in range(2 * NT + 1):
                    if n < 2 * NT:
                        act.wait_ge(gate_filled, n + 1)
                        if n >= 2:
                            act.wait_ge(hid_ready, n - 1)
                        nc.scalar.activation(sg[:, n % 2, :], banks[n % 2][:, :], ACT.Silu).then_inc(silu_ready, 1)
                    if n >= 1:
                        act.wait_ge(ht_filled, n)
                        if n >= 2:
                            act.wait_ge(dn_filled, n - 1)
                        nc.scalar.copy(hidT[:, :, :].rearrange("p c t -> p (c t)"), banks[5][:, :]).then_inc(ht_stored, 1)

        @block.vector
        def _(dve):
            dve.nop().then_inc(dve_emptied, ND)
            norm_vector(nc, dve, norm, x)
            if modulated:
                nc.vector.tensor_tensor(ms[:, :], norm.moments[:, :, 1], norm.rstd[:, :], ALU.mult).then_inc(ms_ready, 1)
                dve.wait_ge(ms_ready, 1)
                nc.vector.tensor_tensor(ms[:, :], ms[:, :], norm.rstd[:, :], ALU.mult).then_inc(ms_ready, 1)
                dve.wait_ge(ms_ready, 2)
                nc.vector.tensor_scalar(ms[:, :], ms[:, :], RMS_EPS, None, ALU.add).then_inc(ms_ready, 1)
                dve.wait_ge(rms_ready, 1)
                for t in range(NT):
                    nc.vector.tensor_scalar(xr[:, t, :], norm.xn[:, t, :], rms[:, t:t + 1], None, ALU.mult).then_inc(xr_ready, 1)
                for t in range(NT):
                    nc.vector.tensor_tensor(x[:, t, :], x[:, t, :], norm.xn[:, t, :], ALU.add)
            nc.vector.memset(qT[:, 0, :, :, :], 0.0).then_inc(padded, 1)
            dve.wait_ge(loaded, 16 * NLOAD)
            with dve.Fori(0, NB // 2) as b:
                for s in dve_steps:
                    kind, c, src = s[0], s[1], bank(s)
                    dve.wait_ge(filled, full(b, s))
                    if kind == "qk":
                        _, _, r, g = s
                        h = 0 if modulated else r * GROUP + g
                        at = c * HEADS + r * GROUP + g
                        nc.vector.memset(tick[:, at:at + 1], 0.0)
                        for i, (lo, hi) in enumerate(((0, S), (S, PAIR))):
                            last = nc.vector.tensor_tensor_reduce(
                                out=sc[:, c, r % 2, g, lo:hi], in0=src[:, lo:hi], in1=bias[:, h, lo:hi], scale=0.25,
                                scalar=-3e38, op0=ALU.add, op1=ALU.max, accum_out=top[:, c, r % 2, i, g:g + 1])
                        last.then_inc(dve_emptied, 1)
                    elif kind == "pt":
                        nc.vector.tensor_copy(pT[:, c, 2, :, :].rearrange("p g t -> p (g t)"), src[:, :]).then_inc(dve_emptied, 1)
                    elif kind == "pv":
                        r = s[2]
                        both = src[:, 0:2 * GROUP * (HD + 1)].rearrange("p (t g c) -> p t g c", t=2, c=HD + 1)
                        nc.vector.reciprocal(rec[:, c, r, :, :], both[:, :, :, HD]).then_inc(rec_ready, 1)
                        dve.wait_ge(rec_ready, b * NR + (rounds[c, r] + 1))
                        nc.vector.tensor_tensor(
                            att[:, c, :, r * GROUP:(r + 1) * GROUP, :], both[:, :, :, 0:HD],
                            rec[:, c, r, :, :].rearrange("p t (g a) -> p t g a", a=1).broadcast_to([P, 2, GROUP, HD]),
                            ALU.mult).then_inc(dve_emptied, 1)
                    elif kind == "wo":
                        xb = x[:, bass.ds(b * 4 + 2 * c, 2), :]
                        nc.vector.tensor_tensor(xb, src[:, :].rearrange("p (t d) -> p t d", t=2), xb,
                                                ALU.add).then_inc(dve_emptied, 1)
                    elif kind == "ha":
                        dve.wait_ge(act_emptied, act_done(b, ("tanh", c)))
                        nc.vector.scalar_tensor_tensor(out=modT[:, bass.ds(b * (2 * S) + c * S, S)], in0=tanhT[:, c, :], scalar=0.1,
                                                       in1=src[0:LORA, 0:S], op0=ALU.mult, op1=ALU.mult).then_inc(dve_emptied, 1)
            if modulated:
                for n in range(2 * NT + 1):
                    if n < 2 * NT:
                        dve.wait_ge(up_filled, n + 1)
                        dve.wait_ge(silu_ready, n + 1)
                        if n >= 2:
                            dve.wait_ge(ht_filled, n - 1)
                        nc.vector.tensor_tensor(hid[:, n % 2, :], banks[2 + n % 2][:, :], sg[:, n % 2, :],
                                                ALU.mult).then_inc(hid_ready, 1)
                    if n >= 1:
                        t = (n - 1) // 2
                        dve.wait_ge(dn_filled, n)
                        if n >= 2:
                            dve.wait_ge(dn_stored, n - 1)
                        nc.vector.tensor_tensor(x[:, t, :], banks[6 + (n - 1) % 2][:, 0:D], x[:, t, :],
                                                ALU.add).then_inc(dn_stored, 1)

        @block.gpsimd
        def _(pool):
            norm_pool(nc, pool, norm, minus_half)
            if modulated:
                pool.wait_ge(ms_ready, 3)
                nc.gpsimd.tensor_tensor(rms[:, :], ms[:, :], minus_half, ALU.pow).then_inc(rms_ready, 1)
            nc.gpsimd.memset(w_q[:, :, :, HD:], 0.0).then_inc(padded, 1)
            nc.gpsimd.memset(w_k[:, :, :, HD:], 0.0).then_inc(padded, 1)
            nc.gpsimd.memset(vp[:, :, :, HD:], 1.0).then_inc(padded, 1)
            nc.gpsimd.memset(qT[:, 1, :, :, :], 0.0).then_inc(padded, 1)
            with pool.Fori(0, NB // 2) as b:
                for c, r in rounds:
                    pool.wait_ge(dve_emptied, dve_done(b, ("qk", c, r, GROUP - 1)))
                    for i, (lo, hi) in enumerate(((0, S), (S, PAIR))):
                        part = sc[:, c, r % 2, :, lo:hi]
                        last = nc.gpsimd.tensor_tensor(
                            part, part, top[:, c, r % 2, i, :].rearrange("p (g a) -> p g a", a=1).broadcast_to([P, GROUP, hi - lo]),
                            ALU.subtract)
                    last.then_inc(shifted, 1)


def alibi_layer(nc, consts, x, weights, bias_const, banks):
    attention_layer(nc, consts, x, weights, bias_const, banks, False)


def mod_layer(nc, consts, x, weights, bias_const, banks):
    attention_layer(nc, consts, x, weights, bias_const, banks, True)


_NAMES = ['L0_attn_hidden_states', 'L0_attn_W_qkvz', 'L0_attn_W_ba', 'L0_attn_conv_w', 'L0_attn_dt_bias', 'L0_attn_A_log', 'L0_attn_norm_weight', 'L0_attn_W_out', 'L0_ffn_router_w', 'L0_ffn_gate_up_proj', 'L0_ffn_down_proj', 'L0_ffn_shared_gate_w', 'L0_ffn_shared_up_w', 'L0_ffn_shared_down_w', 'L1_attn_Wq', 'L1_attn_Wkv', 'L1_attn_Wo', 'L1_attn_bo', 'L1_ffn_ln1_w', 'L1_ffn_ln2_w', 'L1_ffn_Wq', 'L1_ffn_Wk', 'L1_ffn_Wv', 'L1_ffn_Wo', 'L1_ffn_A', 'L1_ffn_B', 'L1_ffn_W_in_base', 'L1_ffn_W_up_base', 'L1_ffn_W_down']


def program(nc, a, const_f, out):
    with ExitStack() as ctx:
        cf = ctx.enter_context(nc.sbuf_tensor("const_sb", [P, 4 * P], F32))
        minus_half = ctx.enter_context(nc.sbuf_tensor("minus_half", [P, NT], F32))
        x = ctx.enter_context(nc.sbuf_tensor("x", [P, NT, D], F32))
        banks = [ctx.enter_context(nc.psum_tensor(f"bank{i}", [P, 512], F32)) for i in range(8)]
        loaded = ctx.enter_context(nc.semaphore("consts_loaded"))
        stored = ctx.enter_context(nc.semaphore("output_stored"))
        ident, upto, after, below = (cf[:, i * P:(i + 1) * P] for i in range(4))
        consts = (ident, upto, after, below, minus_half[:, :])
        with nc.Block() as block:
            @block.sync
            def _(sync):
                sync.dma_start(x[:, :, :], a['L0_attn_hidden_states'].rearrange("b (t p) d -> p (b t) d", p=P)).then_inc(loaded, 16)
                sync.dma_start(cf[:, :], const_f).then_inc(loaded, 16)
                sync.wait_ge(loaded, 32)

            @block.vector
            def _(dve):
                nc.vector.memset(minus_half[:, :], -0.5)
        delta_layer(nc, consts, x, *[a['L0_attn_' + n] for n in ('W_qkvz', 'W_ba', 'conv_w', 'dt_bias', 'A_log', 'norm_weight', 'W_out')], banks)
        expert_layer(nc, consts, x, *[a['L0_ffn_' + n] for n in ('router_w', 'gate_up_proj', 'down_proj', 'shared_gate_w', 'shared_up_w', 'shared_down_w')], a["rconst"], a["slot_in"], a["slot_out"], banks)
        alibi_layer(nc, consts, x, {**{k: a['L1_attn_' + k] for k in ('Wq', 'Wo', 'bo')}, 'Wk': a['L1_attn_Wkv'][:, 0:GROUP * HD], 'Wv': a['L1_attn_Wkv'][:, GROUP * HD:], 'ones': a['ones']}, a['alibi'], banks)
        mod_layer(nc, consts, x, {k: a['L1_ffn_' + n] for k, n in (('Wq', 'Wq'), ('Wk', 'Wk'), ('Wv', 'Wv'), ('Wo', 'Wo'), ('ln1', 'ln1_w'), ('ln2', 'ln2_w'), ('A', 'A'), ('B', 'B'), ('W_in', 'W_in_base'), ('W_up', 'W_up_base'), ('W_down', 'W_down'))}, a['causal'], banks)
        with nc.Block() as block:
            @block.sync
            def _(sync):
                sync.dma_start(out.rearrange("b (t p) d -> p (b t) d", p=P), x[:, :, :]).then_inc(stored, 16)
                sync.wait_ge(stored, 16)


def kernel(**inputs):
    import numpy as _np
    import concourse.bacc as _bacc
    from concourse import mybir as _mybir
    from concourse.bass_utils import run_bass_kernel_spmd as _run

    nc = _bacc.Bacc("TRN2", target_bir_lowering=False, num_devices=1)
    arrays, handles = {}, {}
    turned = ('L0_ffn_router_w', 'L1_ffn_Wq', 'L1_ffn_Wk', 'L1_ffn_Wv', 'L1_ffn_Wo', 'L1_ffn_W_in_base', 'L1_ffn_W_up_base',
              'L1_ffn_W_down')
    for name in _NAMES:
        v = _np.asarray(inputs[name])
        v = _np.ascontiguousarray(v.T if name in turned else v)
        arrays[f"in_{name}"] = v
        handles[name] = nc.dram_tensor(f"in_{name}", v.shape, _mybir.dt.from_np(v.dtype), kind="ExternalInput").ap()
    for name, v in (("const_f", constant_arrays()), ("rconst", routing_constants()), ("alibi", score_bias(alibi_slopes())),
                    ("causal", score_bias([0.0])), ("ones", _np.ones((1, P), _np.float32))):
        arrays[name] = v
        handles[name] = nc.dram_tensor(name, v.shape, F32, kind="ExternalInput").ap()
    for name, tiles in (("slot_in", SLOTS + 1), ("slot_out", SLOTS)):
        handles[name] = nc.dram_tensor(name, (tiles * P, D), F32, kind="Internal").ap()
    out = nc.dram_tensor("out", (NB, S, D), F32, kind="ExternalOutput").ap()
    program(nc, handles, handles["const_f"], out)
    r = _run(nc, [arrays], core_ids=[0])
    return r.results[0]["out"]
```
